# Optimizing a Trainium2 kernel written in Bass

```python
import numpy as np
import jax
import jax.numpy as jnp

def _softmax(x, axis=-1):
    return jax.nn.softmax(x, axis=axis)

def _gelu(x):
    return jax.nn.gelu(x, approximate=True)

def _silu(x):
    return jax.nn.silu(x)

def _sigmoid(x):
    return jax.nn.sigmoid(x)

def _layernorm(x, axis=-1, eps=1e-05):
    m = jnp.mean(x, axis=axis, keepdims=True)
    v = jnp.var(x, axis=axis, keepdims=True)
    return (x - m) / jnp.sqrt(v + eps)

def _scatter_add(tgt, idx, src, axis=0):
    return tgt.at[idx].add(src)

def _segment_sum(src, seg, n):
    return jax.ops.segment_sum(src, seg, n)
kernel_name = 'mk_xattn_ffn_d2_seqx_r4_9f5bfe'

def setup_inputs(seed: int=0):
    np.random.seed(seed)
    _w = jnp.asarray

    def _rec_inputs():
        import jax
        import jax.numpy as jnp
        _rk = jax.random.key(seed)
        x = 7.22e-05 + 1 * jax.random.normal(jax.random.fold_in(_rk, 1), (8, 256, 512), jnp.float32)
        _lenS = 256 - jax.random.randint(jax.random.fold_in(_rk, 7), (8,), 0, max(1, 256 // 4) + 1, jnp.int32)
        _lenS2 = 256 - jax.random.randint(jax.random.fold_in(_rk, 8), (8,), 0, max(1, 256 // 4) + 1, jnp.int32)
        _ctx_2048P = jax.random.normal(jax.random.fold_in(_rk, 11), (8, 16, 512), jnp.float32)
        _ctx_2048c = jax.random.dirichlet(jax.random.fold_in(_rk, 511), 0.3 * jnp.ones((16,), jnp.float32), (8, 256))
        _ctx_2048t = jnp.einsum('bsk,bkd->bsd', _ctx_2048c, _ctx_2048P)
        _ctx_2048t = _ctx_2048t * jax.lax.rsqrt(jnp.mean(jnp.square(_ctx_2048t)) + 1e-12) * 0.953939
        ctx_2048 = 4.13588e-05 + 0.999923 * (_ctx_2048t + 0.3 * jax.random.normal(jax.random.fold_in(_rk, 611), (8, 256, 512), jnp.float32))
        _validS = jnp.arange(256)[None, :] < _lenS[:, None]
        _validS2 = jnp.arange(256)[None, :] < _lenS2[:, None]
        _causal = jnp.tril(jnp.ones((256, 256), dtype=bool))
        mask_SxS2_bc0 = jnp.logical_not(jnp.broadcast_to(_validS2[0:1, :], (256, 256)))
        mask_BxS2_bk0 = jnp.logical_not(jnp.broadcast_to(_validS2[:, :], (8, 256)))
        return (x, ctx_2048, mask_SxS2_bc0, mask_BxS2_bk0)
    x, ctx_2048, mask_SxS2_bc0, mask_BxS2_bk0 = _rec_inputs()

    def _L0_xattn_setup():
        import jax, jax.numpy as jnp
        import numpy as np
        B, LQ, LKV = (4, 256, 256)
        HID, H, G = (512, 32, 8)
        HD = HID // H
        HPG = H // G
        key = jax.random.key(seed)
        ks = jax.random.split(key, 10)
        s = 0.02
        inp = {'X': jax.random.normal(ks[0], (B, LQ, HID), jnp.float32), 'encoder_output': jax.random.normal(ks[1], (B, LKV, HID), jnp.float32), 'causal_mask': jnp.triu(jnp.ones((LQ, LKV), bool), 1), 'padding_mask': jnp.zeros((B, LKV), bool).at[B // 2:, LKV - LKV // 4:].set(True), 'Wq': jax.random.normal(ks[2], (HID, HID), jnp.float32) * s, 'bq': jnp.zeros((HID,), jnp.float32), 'Wk': jax.random.normal(ks[3], (G * HD, HID), jnp.float32) * s, 'bk': jnp.zeros((G * HD,), jnp.float32), 'Wv': jax.random.normal(ks[4], (G * HD, HID), jnp.float32) * s, 'bv': jnp.zeros((G * HD,), jnp.float32), 'Wo': jax.random.normal(ks[5], (HID, HID), jnp.float32) * s, 'bo': jnp.zeros((HID,), jnp.float32)}
        return inp
    _L0_xattn_all = _L0_xattn_setup()
    _L0_xattn_in = {k: v for k, v in _L0_xattn_all.items() if k in ('Wq', 'bq', 'Wk', 'bk', 'Wv', 'bv', 'Wo', 'bo')}
    del _L0_xattn_all

    def _L0_ffn_setup():
        import jax, jax.numpy as jnp
        import numpy as np
        D_MODEL = 512
        HIDDEN = int(2 * D_MODEL * 4 / 3)

        def ternary_quant(w):
            s = jnp.mean(jnp.abs(w))
            q = jnp.clip(jnp.round(w / s), -1.0, 1.0) * s
            return w + jax.lax.stop_gradient(q - w)
        key = jax.random.key(seed)
        k0, k1, k2, k3 = jax.random.split(key, 4)
        x = jax.random.normal(k0, (4, 1024, D_MODEL), dtype=jnp.float32)
        std_in = 1.0 / np.sqrt(D_MODEL)
        std_h = 1.0 / np.sqrt(HIDDEN)
        w1 = jax.random.uniform(k1, (HIDDEN, D_MODEL), jnp.float32, -std_in, std_in)
        w3 = jax.random.uniform(k2, (HIDDEN, D_MODEL), jnp.float32, -std_in, std_in)
        w2 = jax.random.uniform(k3, (D_MODEL, HIDDEN), jnp.float32, -std_h, std_h)
        return {'x': x, 'w1': w1, 'w3': w3, 'w2': w2}
    _L0_ffn_all = _L0_ffn_setup()
    _L0_ffn_in = {k: v for k, v in _L0_ffn_all.items() if k in ('w1', 'w3', 'w2')}
    del _L0_ffn_all

    def _L1_xattn_setup():
        import jax, jax.numpy as jnp
        import numpy as np
        BS, S, DK = (8, 128, 512)
        key = jax.random.key(seed)
        kq, kk, kv = jax.random.split(key, 3)
        q = jax.random.normal(kq, (BS, S, DK), dtype=jnp.float32)
        k = jax.random.normal(kk, (BS, S, DK), dtype=jnp.float32)
        v = jax.random.normal(kv, (BS, S, DK), dtype=jnp.float32)
        return {'q': q, 'k': k, 'v': v}
    _L1_xattn_all = _L1_xattn_setup()
    _L1_xattn_in = {k: v for k, v in _L1_xattn_all.items() if k in ()}
    del _L1_xattn_all

    def _L1_ffn_setup():
        import jax, jax.numpy as jnp
        import numpy as np
        TOP_K = 4
        key = jax.random.key(seed)
        ks = jax.random.split(key, 5)
        H, I, E = (512, 192, 32)
        s = 0.02
        return {'hidden_states': jax.random.normal(ks[0], (1, 256, H), jnp.float32), 'router_w': jax.random.normal(ks[1], (E, H), jnp.float32) * s, 'gate_w': jax.random.normal(ks[2], (E, I, H), jnp.float32) * s, 'up_w': jax.random.normal(ks[3], (E, I, H), jnp.float32) * s, 'down_w': jax.random.normal(ks[4], (E, H, I), jnp.float32) * s}
    _L1_ffn_all = _L1_ffn_setup()
    _L1_ffn_in = {k: v for k, v in _L1_ffn_all.items() if k in ('router_w', 'gate_w', 'up_w', 'down_w')}
    del _L1_ffn_all
    return {'x': x, 'ctx_2048': ctx_2048, 'mask_SxS2_bc0': mask_SxS2_bc0, 'mask_BxS2_bk0': mask_BxS2_bk0, 'L0_xattn_Wq': _L0_xattn_in['Wq'], 'L0_xattn_bq': _L0_xattn_in['bq'], 'L0_xattn_Wk': _L0_xattn_in['Wk'], 'L0_xattn_bk': _L0_xattn_in['bk'], 'L0_xattn_Wv': _L0_xattn_in['Wv'], 'L0_xattn_bv': _L0_xattn_in['bv'], 'L0_xattn_Wo': _L0_xattn_in['Wo'], 'L0_xattn_bo': _L0_xattn_in['bo'], 'L0_ffn_w1': _L0_ffn_in['w1'], 'L0_ffn_w3': _L0_ffn_in['w3'], 'L0_ffn_w2': _L0_ffn_in['w2'], 'L1_ffn_router_w': _L1_ffn_in['router_w'], 'L1_ffn_gate_w': _L1_ffn_in['gate_w'], 'L1_ffn_up_w': _L1_ffn_in['up_w'], 'L1_ffn_down_w': _L1_ffn_in['down_w']}

def reference(x, ctx_2048, mask_SxS2_bc0, mask_BxS2_bk0, L0_xattn_Wq, L0_xattn_bq, L0_xattn_Wk, L0_xattn_bk, L0_xattn_Wv, L0_xattn_bv, L0_xattn_Wo, L0_xattn_bo, L0_ffn_w1, L0_ffn_w3, L0_ffn_w2, L1_ffn_router_w, L1_ffn_gate_w, L1_ffn_up_w, L1_ffn_down_w):
    import jax
    import jax.numpy as jnp

    def _L0_xattn_ref(X, encoder_output, causal_mask, padding_mask, Wq, bq, Wk, bk, Wv, bv, Wo, bo):
        import jax, jax.numpy as jnp
        import numpy as np
        B, LQ, LKV = (4, 256, 256)
        HID, H, G = (512, 32, 8)
        HD = HID // H
        HPG = H // G
        b = X.shape[0]
        q = X @ Wq.T + bq
        k = encoder_output @ Wk.T + bk
        v = encoder_output @ Wv.T + bv
        q = q.reshape(b, LQ, G, HPG, HD).transpose(0, 2, 3, 1, 4)
        k = k.reshape(b, LKV, G, HD).transpose(0, 2, 1, 3)
        v = v.reshape(b, LKV, G, HD).transpose(0, 2, 1, 3)
        scores = jnp.einsum('bgrqd,bgkd->bgrqk', q, k) / jnp.sqrt(jnp.float32(HD))
        scores = jnp.where(causal_mask[None, None, None, :, :], -jnp.inf, scores)
        scores = jnp.where(padding_mask[:, None, None, None, :], -jnp.inf, scores)
        w = jax.nn.softmax(scores, axis=-1)
        out = jnp.einsum('bgrqk,bgkd->bgrqd', w, v)
        out = out.reshape(b, H, LQ, HD).transpose(0, 2, 1, 3).reshape(b, LQ, HID)
        return out @ Wo.T + bo

    def _L0_ffn_ref(x, w1, w3, w2):
        import jax, jax.numpy as jnp
        import numpy as np
        D_MODEL = 512
        HIDDEN = int(2 * D_MODEL * 4 / 3)

        def ternary_quant(w):
            s = jnp.mean(jnp.abs(w))
            q = jnp.clip(jnp.round(w / s), -1.0, 1.0) * s
            return w + jax.lax.stop_gradient(q - w)
        w1q = ternary_quant(w1)
        w3q = ternary_quant(w3)
        w2q = ternary_quant(w2)
        h1 = jnp.einsum('bsd,hd->bsh', x, w1q)
        h3 = jnp.einsum('bsd,hd->bsh', x, w3q)
        g = jax.nn.silu(h1) * h3
        return jnp.einsum('bsh,dh->bsd', g, w2q)

    def _L1_xattn_ref(q, k, v):
        import jax, jax.numpy as jnp
        import numpy as np
        BS, S, DK = (8, 128, 512)
        dk = q.shape[-1]
        scale = 1.0 / jnp.sqrt(jnp.asarray(dk, dtype=q.dtype))
        scaled = jnp.einsum('bsd,bse->bde', q, k) * scale
        attn = jax.nn.softmax(scaled, axis=1)
        out = jnp.einsum('bde,bse->bsd', attn, v)
        return out

    def _L1_ffn_ref(hidden_states, router_w, gate_w, up_w, down_w):
        import jax, jax.numpy as jnp
        import numpy as np
        TOP_K = 4
        B, S, H = hidden_states.shape
        E = router_w.shape[0]
        x = hidden_states.reshape(-1, H)
        logits = x @ router_w.T
        probs = jax.nn.softmax(logits.astype(jnp.float32), axis=-1)
        rw, sel = jax.lax.top_k(probs, TOP_K)
        rw = rw / jnp.sum(rw, axis=-1, keepdims=True)
        rw = rw.astype(x.dtype)

        def body(acc, expert):
            gw, uw, dw, e = expert
            w_tok = jnp.sum(jnp.where(sel == e, rw, 0.0), axis=-1)
            h = jax.nn.silu(x @ gw.T) * (x @ uw.T)
            y = h @ dw.T
            return (acc + w_tok[:, None] * y, None)
        acc0 = jnp.zeros_like(x)
        out, _ = jax.lax.scan(body, acc0, (gate_w, up_w, down_w, jnp.arange(E)))
        return out.reshape(B, S, H)
    x = x + _L0_xattn_ref(_layernorm(x, axis=-1), ctx_2048, mask_SxS2_bc0, mask_BxS2_bk0, L0_xattn_Wq, L0_xattn_bq, L0_xattn_Wk, L0_xattn_bk, L0_xattn_Wv, L0_xattn_bv, L0_xattn_Wo, L0_xattn_bo)
    x = x + _L0_ffn_ref(_layernorm(x, axis=-1), L0_ffn_w1, L0_ffn_w3, L0_ffn_w2)
    x = x + _L1_xattn_ref(_layernorm(x, axis=-1), ctx_2048, ctx_2048)
    x = x + _L1_ffn_ref(_layernorm(x, axis=-1), L1_ffn_router_w, L1_ffn_gate_w, L1_ffn_up_w, L1_ffn_down_w)
    return x

_drawn_inputs = setup_inputs


def setup_inputs(seed=0):
    import zlib

    import numpy as np

    out = dict(_drawn_inputs(seed))
    spreads = {'L0_xattn_bq': (0.0, 0.8),
     'L0_xattn_bk': (0.0, 0.8),
     'L0_xattn_bv': (0.0, 0.1),
     'L0_xattn_bo': (0.0, 0.1)}
    factors = {'L0_xattn_Wq': 8.0,
     'L0_xattn_Wk': 5.575,
     'L1_ffn_router_w': 4.967,
     'L1_ffn_gate_w': 4.709,
     'L1_ffn_up_w': 4.628,
     'L1_ffn_down_w': 4.629}
    for name, (base, spread) in spreads.items():
        noise = np.random.default_rng([zlib.crc32(name.encode()), seed]).standard_normal(out[name].shape)
        drawn = base * np.exp(spread * noise) if base else spread * noise
        out[name] = jnp.asarray(drawn.astype(out[name].dtype))
    for name, factor in factors.items():
        out[name] = (out[name] * factor).astype(out[name].dtype)
    return out
```

```python
from contextlib import ExitStack

import numpy as np

import concourse.bass as bass
from concourse import mybir

F32 = mybir.dt.float32
F16 = mybir.dt.float16
I32 = mybir.dt.int32
U32 = mybir.dt.uint32
U8 = mybir.dt.uint8
ALU = mybir.AluOpType
ACT = mybir.ActivationFunctionType
AX = mybir.AxisListType

P = 128
BATCH, SEQ, DM = 8, 256, 512
TOKENS = BATCH * SEQ
TT = SEQ // P
FT = DM // P
HEADS, GROUPS, HD = 32, 8, 16
HPG = HEADS // GROUPS
KVW = GROUPS * HD
HIDDEN = int(2 * DM * 4 / 3)
HT = -(-HIDDEN // P)
HPAD = HT * P
HPAIRS = -(-HT // 2)
EXPERTS, INTER, TOPK = 32, 192, 4
TILES = TOKENS // P
BS = 256
NBLK = TOKENS * TOPK // BS + EXPERTS - 1
SLOTS = NBLK * BS
EPS = 1e-5
MASKED = -30000.0
ROW_PAD = 4 * HD
ROW_MAX = ROW_PAD + 1
ROWS_A = ROW_MAX
ROWS_B = ROW_MAX + 3
G_SCALE = 1.0 / 64.0
P_SCALE = 256.0
HI, LO = 0, 1
PASSES = ((HI, HI), (HI, LO), (LO, HI))


def pair_width(hp):
    return min(2, HT - 2 * hp) * SEQ


def pick(view, n):
    if isinstance(n, int):
        return view[n]
    names = " ".join("bcde"[:len(view.shape) - 2])
    return view[bass.ds(n, 1)].rearrange(f"o a {names} -> (o a) {names}")


def early(n):
    return isinstance(n, int) and n < 2


def pipeline(eng, first, second, third):
    first(0, 0)
    first(1, 1)
    second(0, 0)
    first(2, 0)
    second(1, 1)
    third(0, 0)
    with eng.Fori(1, NBLK // 2) as i:
        for u in range(2):
            n = 2 * i + u
            first(n + 1, 1 - u)
            second(n, u)
            third(n - 1, 1 - u)
    second(NBLK - 1, 0)
    third(NBLK - 2, 1)
    third(NBLK - 1, 0)


def build(nc, x_d, ctx_d, ctxT_d, mq_d, mk_d, pad_d, wq_d, bq_d, wk_d, bk_d, wv_d, bv_d, wo_d, bo_d,
          w1_d, w3_d, w2_d, rw_d, gu_d, da_d, db_d, out_d):
    def dram(name, shape, dt):
        return nc.dram_tensor(name, shape, dt, kind="Internal").ap()

    q_dram = dram("q_dram", (2, DM, SEQ), F16)
    k_dram = dram("k_dram", (2, KVW, SEQ), F16)
    m_dram = dram("m_dram", (3, TT * HEADS, P), F16)
    padbias_dram = dram("padbias_dram", (BATCH, SEQ), F16)
    x3_dram = dram("x3_dram", (TOKENS, DM), F32)
    xn_dram = dram("xn_dram", (TOKENS, 2 * DM), F16)
    slots_dram = dram("slots_dram", (SLOTS, 2 * DM), F16)
    y_dram = dram("y_dram", (SLOTS, DM), F32)
    eid_dram = dram("eid_dram", (P,), I32)

    ctx = ExitStack()
    with ctx:
        def sb(name, shape, dt, scope=ctx):
            return scope.enter_context(nc.sbuf_tensor(name, shape, dt))

        def sem(name):
            return ctx.enter_context(nc.semaphore(name))

        bank = ctx.enter_context(nc.psum_tensor("bank", [P, 8, 512], F32))

        ident = sb("ident", [P, P], F32)
        ident16 = sb("ident16", [P, P], F16)
        ones16 = sb("ones16", [P, P], F16)
        route_w = sb("route_w", [P, TILES, TOPK], F32)
        route_e = sb("route_e", [P, TILES, TOPK], F32)

        with ExitStack() as dense:
            dense_layers(nc, dense, sb, sem, bank, ident, ident16, ones16, route_w, route_e,
                         x_d, ctx_d, ctxT_d, mq_d, mk_d, pad_d, wq_d, bq_d, wk_d, bk_d, wv_d, bv_d,
                         wo_d, bo_d, w1_d, w3_d, w2_d, rw_d, q_dram, k_dram, m_dram, padbias_dram,
                         x3_dram, xn_dram, slots_dram)
        with ExitStack() as sparse:
            expert_layer(nc, sparse, sb, sem, bank, ident16, ones16, route_w, route_e,
                         gu_d, da_d, db_d, x3_dram, xn_dram, slots_dram, y_dram, eid_dram, out_d)


def dense_layers(nc, dense, sb, sem, bank, ident, ident16, ones16, route_w, route_e,
                 x_d, ctx_d, ctxT_d, mq_d, mk_d, pad_d, wq_d, bq_d, wk_d, bk_d, wv_d, bv_d,
                 wo_d, bo_d, w1_d, w3_d, w2_d, rw_d, q_dram, k_dram, m_dram, padbias_dram,
                 x3_dram, xn_dram, slots_dram):

    def t(name, shape, dt, scope=dense):
        return sb(name, shape, dt, scope)

    wq16 = t("wq16", [P, 2, FT, DM], F16)
    wk16 = t("wk16", [P, 2, FT, KVW], F16)
    wv16 = t("wv16", [P, 2, FT, KVW], F16)
    wo16 = t("wo16", [P, 2, FT, DM], F16)
    rw16 = t("rw16", [P, 2, FT, EXPERTS], F16)
    w1t = t("w1t", [P, FT, HPAD], F16)
    w3t = t("w3t", [P, FT, HPAD], F16)
    w2t = t("w2t", [P, HT, DM], F16)
    half_s1 = t("half_s1", [P, 1], F32)
    ffn_scale = t("ffn_scale", [P, 1], F32)
    bq_col = t("bq_col", [P, FT], F32)
    bk_col = t("bk_col", [KVW, 1], F32)
    bv_row = t("bv_row", [P, KVW], F32)
    bo_row = t("bo_row", [P, DM], F32)
    mask_q = t("mask_q", [P, TT, SEQ], F16)
    mask_k = t("mask_k", [P, TT, SEQ], F16)
    neg_half = t("neg_half", [P, TT], F32)
    zeros = t("zeros", [P, 2016], F16)

    with ExitStack() as prologue:
        prepare(nc, prologue, sb, sem, bank, ident, ident16, ones16, wq16, wk16, wv16, wo16, rw16, w1t, w3t,
                w2t, half_s1, ffn_scale, bq_col, bk_col, bv_row, bo_row, mask_q, mask_k, neg_half, zeros,
                mq_d, mk_d, pad_d, wq_d, bq_d, wk_d, bk_d, wv_d, bv_d, wo_d, bo_d, w1_d, w3_d, w2_d,
                rw_d, padbias_dram)

    xin = t("xin", [P, TT, DM], F32)
    ctx_raw = t("ctx_raw", [P, TT, DM], F32)
    ctxT_raw = t("ctxT_raw", [P, FT, SEQ], F32)
    ctx16 = t("ctx16", [P, 2, TT, DM], F16)
    ctxT16 = t("ctxT16", [P, 2, FT, SEQ], F16)
    res = t("res", [P, TT, DM], F32)
    xn = t("xn", [P, TT, DM], F32)
    xT16 = t("xT16", [P, 2, FT, SEQ], F16)
    xs16 = t("xs16", [P, TT, 2, DM], F16)
    stats = t("stats", [P, TT, 6], F32)
    moments = t("moments", [P, TT, 2], F32)
    var_eps = t("var_eps", [P, TT], F32)
    rstd = t("rstd", [P, TT], F32)
    q32 = t("q32", [P, FT, SEQ], F32)
    q16 = t("q16", [P, 2, FT, SEQ], F16)
    k32 = t("k32", [KVW, SEQ], F32)
    k16 = t("k16", [KVW, 2, SEQ], F16)
    q_stack = t("q_stack", [ROWS_B, HEADS, SEQ], F16)
    k_stack = t("k_stack", [ROWS_B, GROUPS, SEQ], F16)
    v_ones = t("v_ones", [P, TT, GROUPS, 32], F32)
    neg_max = t("neg_max", [P, 2 * TT, HEADS], F32)
    nothing = t("nothing", [1, 1], F32)
    eps_col = t("eps_col", [P, TT], F32)
    m_rest = t("m_rest", [TT * HEADS, P], F32)
    m16 = t("m16", [TT * HEADS, 3, P], F16)
    probs = t("probs", [P, 16, 1024], F32)
    attn_raw = t("attn_raw", [P, 2, HPG, SEQ], F32)
    inv_sum = t("inv_sum", [P, 4, HPG, 4], F32)
    tanh_a = probs[:, 0, :].rearrange("p (a n) -> p a n", a=2)
    gate_b = probs[:, 1, :].rearrange("p (a n) -> p a n", a=2)
    g32 = probs[:, 2, :].rearrange("p (a n) -> p a n", a=2)
    g16 = probs[:, 3:6, :].rearrange("p a n -> p (a n)").bitcast(F16).rearrange(
        "p (s h n) -> p s h n", s=2, h=2 * HPAIRS)
    e32 = probs[:, 6:8, :].rearrange("p a n -> p (a n)").rearrange("p (e n) -> p e n", e=FT)
    p32 = probs[:, 8:10, :].rearrange("p a n -> p (a n)").rearrange("p (e n) -> p e n", e=FT)
    p16 = probs[:, 10:12, :].rearrange("p a n -> p (a n)").bitcast(F16).rearrange(
        "p (s e n) -> p s e n", s=2, e=FT)
    ch_neg = t("ch_neg", [P, FT], F32)
    ch_bias = t("ch_bias", [P, FT], F32)
    ch_sum = t("ch_sum", [P, FT], F32)
    ch_inv = t("ch_inv", [P, FT], F32)
    lg_neg = t("lg_neg", [P, TT], F32)
    lg_exp = t("lg_exp", [P, TT, EXPERTS], F32)
    lg_sum = t("lg_sum", [P, TT], F32)
    lg_inv = t("lg_inv", [P, TT], F32)
    lg_prob = t("lg_prob", [P, TT, EXPERTS], F32)
    top8 = t("top8", [P, TT, 8], F32)
    idx8 = t("idx8", [P, TT, 8], U32)
    top_sum = t("top_sum", [P, TT], F32)
    top_inv = t("top_inv", [P, TT], F32)

    names = ("x_loaded ctx_loaded k_stored k_stacked q_stored q_stacked m_stored m_stacked x3_stored "
             "xn_stored zeroed ctx_hi ctx_lo stats_ready rstd_ready xn_ready transposed hi_ready lo_ready "
             "k_ready v_ready q_ready q_scaled k_split v_placed q_split biased a_ready a_reduced "
             "m_turned m_split b_ready exp_done pv_ready raw_kept o_turned o_ready wo_ready x1_ready "
             "up_ready tanh_ready g_ready g_hi g_lo down_ready rows_hi rows_lo s_ready max_ready "
             "e_ready p_ready p_hi p_lo ch_ready x3_ready logits_ready lmax_ready lexp_ready "
             "dve_step pool_step ones_set").split()
    s = {n: sem(n) for n in names}
    S_SCALE = float(np.float32(1.0) / np.sqrt(np.float32(DM)))
    LN1, LN2, LN3, LN4 = range(4)
    T_ATTN_IN, T_ATTN_OUT, T_FFN, T_ROUTER = range(4)
    DVE_STEPS, POOL_STEPS = 34, 4

    class Chain:

        def __init__(self, eng, sem_, per, b):
            self.eng, self.sem, self.per, self.b, self.n = eng, sem_, per, b, 0

        def then(self, ins, alone=False):
            self.n += 1
            ins.then_inc(self.sem, 1)
            if alone:
                wait_apart(self.eng, self.sem, self.b * self.per + self.n)
            else:
                self.eng.wait_ge(self.sem, self.b * self.per + self.n)

        def end(self):
            assert self.n == self.per, self.n

    def wait_apart(dve, semaphore, value):
        dve.wait_ge(semaphore, value)
        dve.memset(nothing[:], 0.0)

    block = dense.enter_context(nc.Block())

    @block.sync
    def _(sp):
        def sp_wait(semaphore, value):
            value = sp.snap(value)
            sp.wait_ge(s["ones_set"], 1)
            sp.wait_ge(semaphore, value)

        def load_x(b):
            sp.dma_start(xin[:], pick(x_d, b).rearrange("(t p) d -> p t d", p=P)).then_inc(s["x_loaded"], 16)

        def load_ctx(b):
            sp.dma_start(ctxT_raw[:], pick(ctxT_d, b).rearrange("(t p) k -> p t k", p=P)).then_inc(s["ctx_loaded"], 16)
            sp.dma_start(ctx_raw[:], pick(ctx_d, b).rearrange("(t p) d -> p t d", p=P)).then_inc(s["ctx_loaded"], 16)

        def body(b, last):
            sp.wait_ge(s["k_split"], b + 1)
            for part in (HI, LO):
                sp.dma_start(k_dram[part], k16[:, part, :]).then_inc(s["k_stored"], 16)
            sp.wait_ge(s["k_stored"], b * 32 + 32)
            for i, part in enumerate((HI, LO, HI, LO)):
                sp.dma_start(k_stack[i * HD:(i + 1) * HD],
                             k_dram[part].rearrange("(g d) k -> d g k", d=HD)).then_inc(s["k_stacked"], 16)
            sp.dma_start(k_stack[ROW_PAD:ROW_PAD + 1],
                         pad_row(b)).then_inc(s["k_stacked"], 16)
            sp.wait_ge(s["q_split"], b + 1)
            for part in (HI, LO):
                sp.dma_start(q_dram[part].rearrange("(t p) q -> p t q", p=P),
                             q16[:, part]).then_inc(s["q_stored"], 16)
            sp.wait_ge(s["q_stored"], b * 32 + 32)
            for i, part in enumerate((HI, HI, LO, LO)):
                sp.dma_start(q_stack[i * HD:(i + 1) * HD],
                             q_dram[part].rearrange("(h d) q -> d h q", d=HD)).then_inc(s["q_stacked"], 16)
            sp.dma_start(slots_dram.rearrange("s c -> (s c)").rearrange("(p n c) -> p n c", p=P, c=2016)[
                :, bass.ds(b * 8, 8), :],
                zeros[:, :].unsqueeze(1).to_broadcast([P, 8, 2016])).then_inc(s["zeroed"], 16)
            if not last:
                sp_wait(s["ctx_lo"], b * 2 + 2)
                load_ctx(b + 1)
            sp.wait_ge(s["m_split"], b + 1)
            sp.dma_start(m_dram.rearrange("i h q -> h i q"), m16[:]).then_inc(s["m_stored"], 16)
            sp.wait_ge(s["m_stored"], b * 16 + 16)
            for tt in range(TT):
                sp.dma_start(q_stack[ROW_MAX:ROW_MAX + 3, :, tt * P:(tt + 1) * P],
                             m_dram[:, tt * HEADS:(tt + 1) * HEADS, :]).then_inc(s["m_stacked"], 16)
            if not last:
                sp_wait(s["x1_ready"], b * 2 + 2)
                load_x(b + 1)
            sp_wait(s["x3_ready"], b * 2 + 2)
            sp.dma_start(rows(x3_dram, b), res[:]).then_inc(s["x3_stored"], 16)
            sp.wait_ge(s["rows_hi"], b * 4 + 4)
            sp.wait_ge(s["rows_lo"], b * 4 + 4)
            sp.dma_start(rows(xn_dram, b), xs16[:].rearrange("p t s d -> p t (s d)")).then_inc(s["xn_stored"], 16)
            sp_wait(s["x3_stored"], b * 16 + 16)
            sp.wait_ge(s["xn_stored"], b * 16 + 16)

        def rows(dram, b):
            return pick(dram.rearrange("(b t p) c -> b p t c", b=BATCH, p=P), b)

        def pad_row(b):
            return padbias_dram[bass.ds(b, 1)].unsqueeze(1).to_broadcast([1, GROUPS, SEQ])

        sp.dma_start(ctxT_raw[:], ctxT_d[0].rearrange("(t p) k -> p t k", p=P)).then_inc(s["ctx_loaded"], 16)
        sp.dma_start(ctx_raw[:], ctx_d[0].rearrange("(t p) d -> p t d", p=P)).then_inc(s["ctx_loaded"], 16)
        sp.dma_start(xin[:], x_d[0].rearrange("(t p) d -> p t d", p=P)).then_inc(s["x_loaded"], 16)
        sp.wait_ge(s["ones_set"], 5)
        with sp.Fori(0, BATCH - 1) as b:
            body(b, False)
        body(BATCH - 1, True)
        sp.wait_ge(s["zeroed"], BATCH * 16)

    @block.gpsimd
    def _(pool):
        def body(b):
            steps = Chain(pool, s["pool_step"], POOL_STEPS, b)

            def inverse_deviation(ln):
                pool.wait_ge(s["stats_ready"], b * 4 + ln + 1)
                steps.then(pool.tensor_tensor(var_eps[:], moments[:, :, 1], eps_col[:], ALU.add))
                pool.tensor_tensor(rstd[:], var_eps[:], neg_half[:], ALU.pow).then_inc(s["rstd_ready"], 1)

            pool.wait_ge(s["ctx_hi"], b * 2 + 1)
            pool.tensor_tensor(ctxT16[:, LO], ctxT_raw[:], ctxT16[:, HI], ALU.subtract).then_inc(s["ctx_lo"], 1)
            inverse_deviation(LN1)
            pool.wait_ge(s["ctx_hi"], b * 2 + 2)
            pool.tensor_tensor(ctx16[:, LO], ctx_raw[:], ctx16[:, HI], ALU.subtract).then_inc(s["ctx_lo"], 1)
            pool.wait_ge(s["xn_ready"], b * 8 + 2)
            pool.tensor_tensor(xin[:], xin[:], bo_row[:].unsqueeze(1).to_broadcast([P, TT, DM]),
                               ALU.add).then_inc(s["biased"], 1)
            inverse_deviation(LN2)
            for hp in range(HPAIRS):
                w = pair_width(hp)
                pool.wait_ge(s["g_hi"], b * HPAIRS + hp + 1)
                pool.tensor_tensor(g16[:, LO, 2 * hp:2 * hp + w // SEQ, :].rearrange("p h n -> p (h n)"),
                                   g32[:, hp % 2, 0:w],
                                   g16[:, HI, 2 * hp:2 * hp + w // SEQ, :].rearrange("p h n -> p (h n)"),
                                   ALU.subtract).then_inc(s["g_lo"], 1)
            for ln in (LN3, LN4):
                inverse_deviation(ln)
                for tt in range(TT):
                    n = TT * (ln - LN3) + tt + 1
                    pool.wait_ge(s["rows_hi"], b * 4 + n)
                    pool.tensor_tensor(xs16[:, tt, LO], xn[:, tt], xs16[:, tt, HI],
                                       ALU.subtract).then_inc(s["rows_lo"], 1)
                if ln == LN3:
                    for et in range(FT):
                        pool.wait_ge(s["p_hi"], b * FT + et + 1)
                        pool.tensor_tensor(p16[:, LO, et], p32[:, et], p16[:, HI, et],
                                           ALU.subtract).then_inc(s["p_lo"], 1)
            steps.end()

        pool.wait_ge(s["ones_set"], 5)
        with pool.Fori(0, BATCH) as b:
            body(b)

    @block.scalar
    def _(act):
        def body(b):
            def high_part(which, first_bank):
                for i in range(2):
                    act.wait_ge(s["transposed"], b * 8 + 2 * which + i + 1)
                    act.copy(xT16[:, HI, 2 * i:2 * i + 2, :].rearrange("p t n -> p (t n)"),
                             bank[:, first_bank + i, :]).then_inc(s["hi_ready"], 1)

            act.wait_ge(s["ctx_loaded"], b * 32 + 32)
            act.copy(ctxT16[:, HI], ctxT_raw[:]).then_inc(s["ctx_hi"], 1)
            act.copy(ctx16[:, HI], ctx_raw[:]).then_inc(s["ctx_hi"], 1)
            high_part(T_ATTN_IN, 0)
            for ht in range(FT):
                if ht % 2 == 0:
                    act.wait_ge(s["q_ready"], b * 2 + ht // 2 + 1)
                act.activation(q32[:, ht], bank[:, 4 + ht // 2, (ht % 2) * SEQ:(ht % 2 + 1) * SEQ],
                               ACT.Identity, bias=bq_col[:, ht:ht + 1],
                               scale=1.0 / 4.0).then_inc(s["q_scaled"], 1)
            for u in range(16):
                act.wait_ge(s["b_ready"], b * 16 + u + 1)
                act.activation(probs[:, u], bank[:, 2 * (u % 3):2 * (u % 3) + 2, :].rearrange("p a n -> p (a n)"),
                               ACT.Exp).then_inc(s["exp_done"], 1)
                if u in (10, 15):
                    gg = 0 if u == 10 else 1
                    act.wait_ge(s["pv_ready"], b * 2 + gg + 1)
                    act.copy(attn_raw[:, gg].rearrange("p r n -> p (r n)"),
                             bank[:, 6:8, :].rearrange("p a n -> p (a n)")).then_inc(s["raw_kept"], 1)
            high_part(T_ATTN_OUT, 4)
            high_part(T_FFN, 0)
            for hp in range(HPAIRS + 1):
                if hp < HPAIRS:
                    w = pair_width(hp)
                    act.wait_ge(s["up_ready"], b * HPAIRS + hp + 1)
                    if hp >= 2:
                        act.wait_ge(s["g_ready"], b * HPAIRS + hp - 1)
                    act.activation(tanh_a[:, hp % 2, 0:w], bank[:, 2 * (hp % 3), 0:w], ACT.Tanh,
                                   scale=half_s1[:, 0:1]).then_inc(s["tanh_ready"], 1)
                if hp >= 1:
                    j = hp - 1
                    w = pair_width(j)
                    act.wait_ge(s["g_ready"], b * HPAIRS + j + 1)
                    act.copy(g16[:, HI, 2 * j:2 * j + w // SEQ, :].rearrange("p h n -> p (h n)"),
                             g32[:, j % 2, 0:w]).then_inc(s["g_hi"], 1)

            def rows_high(ln):
                for tt in range(TT):
                    act.wait_ge(s["xn_ready"], b * 8 + 2 * ln + tt + 1)
                    act.copy(xs16[:, tt, HI], xn[:, tt]).then_inc(s["rows_hi"], 1)

            rows_high(LN3)
            for et in range(FT):
                act.wait_ge(s["max_ready"], b * FT + et + 1)
                act.activation(e32[:, et], bank[:, et, :], ACT.Exp, bias=ch_bias[:, et:et + 1], scale=S_SCALE,
                               accum_out=ch_sum[:, et:et + 1]).then_inc(s["e_ready"], 1)
            for et in range(FT):
                act.wait_ge(s["p_ready"], b * FT + et + 1)
                act.copy(p16[:, HI, et], p32[:, et]).then_inc(s["p_hi"], 1)
            rows_high(LN4)
            high_part(T_ROUTER, 6)
            act.wait_ge(s["lmax_ready"], b + 1)
            for tt in range(TT):
                act.activation(lg_exp[:, tt], bank[:, 0, tt * EXPERTS:(tt + 1) * EXPERTS], ACT.Exp,
                               bias=lg_neg[:, tt:tt + 1],
                               accum_out=lg_sum[:, tt:tt + 1]).then_inc(s["lexp_ready"], 1)

        with act.Fori(0, BATCH) as b:
            body(b)

    @block.tensor
    def _(pe):
        def body(b):
            def three(out, left, right, n, stop_last=True):
                for i in range(n):
                    for j, (lp, rp) in enumerate(PASSES):
                        last = pe.matmul(out, left(lp, i), right(rp, i), start=(i == 0 and j == 0),
                                         stop=(i == n - 1 and j == 2))
                return last

            def turn(which, first_bank):
                for ft in range(FT):
                    for tt in range(TT):
                        last = pe.transpose(
                            bank[:, first_bank + ft // 2, (ft % 2) * SEQ + tt * P:(ft % 2) * SEQ + (tt + 1) * P],
                            xn[:, tt, ft * P:(ft + 1) * P], ident[:])
                    if ft % 2 == 1:
                        last.then_inc(s["transposed"], 1)

            pe.wait_ge(s["ctx_hi"], b * 2 + 1)
            pe.wait_ge(s["ctx_lo"], b * 2 + 1)
            three(bank[0:KVW, 2, 0:SEQ], lambda p, i: wk16[:, p, i, :], lambda p, i: ctxT16[:, p, i, :],
                  FT).then_inc(s["k_ready"], 1)
            for kt in range(TT):
                last = three(bank[:, 3, kt * KVW:(kt + 1) * KVW],
                             lambda p, i: ctxT16[:, p, i, kt * P:(kt + 1) * P],
                             lambda p, i: wv16[:, p, i, :], FT)
            last.then_inc(s["v_ready"], 1)
            pe.wait_ge(s["xn_ready"], b * 8 + 2)
            turn(T_ATTN_IN, 0)
            pe.wait_ge(s["lo_ready"], b * 8 + 2)
            for ht in range(FT):
                last = three(bank[:, 4 + ht // 2, (ht % 2) * SEQ:(ht % 2 + 1) * SEQ],
                             lambda p, i: wq16[:, p, i, ht * P:(ht + 1) * P],
                             lambda p, i: xT16[:, p, i, :], FT)
                if ht % 2 == 1:
                    last.then_inc(s["q_ready"], 1)
            pe.wait_ge(s["k_stacked"], b * 80 + 80)
            pe.wait_ge(s["q_stacked"], b * 64 + 64)
            for u in range(16):
                g, qt = u // 2, u % 2
                if u >= 4:
                    pe.wait_ge(s["a_reduced"], b * 16 + u - 3)
                for half in range(2):
                    out = bank[:, 2 * (u % 4) + half, :]
                    pe.matmul(out.rearrange("p (a n) -> p a n", a=2), ident16[:],
                              mask_q[:, qt, :].unsqueeze(1).to_broadcast([P, 2, SEQ]), start=True, stop=True)
                    for r in range(2):
                        h = HPG * g + 2 * half + r
                        last = pe.matmul(out[:, r * SEQ:(r + 1) * SEQ],
                                         q_stack[0:ROWS_A, h, qt * P:(qt + 1) * P],
                                         k_stack[0:ROWS_A, g, :], start=False, stop=True,
                                         skip_group_check=True)
                last.then_inc(s["a_ready"], 1)
            pe.wait_ge(s["a_reduced"], b * 16 + 16)
            pe.transpose(bank[:, 6, 0:P], neg_max[:].rearrange("p t h -> p (t h)"),
                         ident[:]).then_inc(s["m_turned"], 1)

            def pv(gg):
                pe.wait_ge(s["exp_done"], b * 16 + 8 * gg + 8)
                if gg == 1:
                    pe.wait_ge(s["raw_kept"], b * 2 + 1)
                for kt in range(TT):
                    for half in range(2):
                        for j in range(4):
                            last = pe.matmul(bank[32 * j:32 * j + 32, 6 + half, :], v_ones[:, kt, 4 * gg + j, :],
                                             probs[:, 8 * gg + 2 * j + kt, half * 512:(half + 1) * 512],
                                             start=(kt == 0), stop=(kt == TT - 1), tile_position=(0, 32 * j))
                last.then_inc(s["pv_ready"], 1)

            pe.wait_ge(s["m_stacked"], b * 32 + 32)
            for u in range(16):
                gg, j, kt = u // 8, u % 8 // 2, u % 2
                g = 4 * gg + j
                if u >= 3:
                    pe.wait_ge(s["exp_done"], b * 16 + u - 2)
                for half in range(2):
                    out = bank[:, 2 * (u % 3) + half, :]
                    pe.matmul(out.rearrange("p (a n) -> p a n", a=2), ident16[:],
                              mask_k[:, kt, :].unsqueeze(1).to_broadcast([P, 2, SEQ]), start=True, stop=True)
                    h = HPG * g + 2 * half
                    last = pe.matmul(out, k_stack[0:ROWS_B, g, kt * P:(kt + 1) * P],
                                     q_stack[0:ROWS_B, h:h + 2, :].rearrange("k h q -> k (h q)"),
                                     start=False, stop=True, skip_group_check=True)
                last.then_inc(s["b_ready"], 1)
                if u == 9:
                    pe.wait_ge(s["v_placed"], b + 1)
                    pv(0)
            pv(1)
            pe.wait_ge(s["raw_kept"], b * 2 + 2)
            for qt in range(TT):
                for gg in range(2):
                    for r in range(HPG):
                        last = pe.transpose(bank[:, 2 * qt + gg, r * P:(r + 1) * P],
                                            attn_raw[:, gg, r, qt * P:(qt + 1) * P], ident[:])
                    last.then_inc(s["o_turned"], 1)
            pe.wait_ge(s["o_ready"], b * 4 + 4)
            turn(T_ATTN_OUT, 4)
            pe.wait_ge(s["lo_ready"], b * 8 + 4)
            for tt in range(TT):
                three(bank[:, 6 + tt, :], lambda p, i: xT16[:, p, i, tt * P:(tt + 1) * P],
                      lambda p, i: wo16[:, p, i, :], FT).then_inc(s["wo_ready"], 1)
            pe.wait_ge(s["xn_ready"], b * 8 + 4)
            turn(T_FFN, 0)
            pe.wait_ge(s["lo_ready"], b * 8 + 6)
            for hp in range(HPAIRS):
                if hp >= 3:
                    pe.wait_ge(s["g_ready"], b * HPAIRS + hp - 2)
                for which, w in enumerate((w1t, w3t)):
                    for a in range(pair_width(hp) // SEQ):
                        h0 = (2 * hp + a) * P
                        for ft in range(FT):
                            for part in (HI, LO):
                                last = pe.matmul(bank[:, 2 * (hp % 3) + which, a * SEQ:(a + 1) * SEQ],
                                                 w[:, ft, h0:h0 + P], xT16[:, part, ft, :],
                                                 start=(ft == 0 and part == HI), stop=(ft == FT - 1 and part == LO))
                last.then_inc(s["up_ready"], 1)
            pe.wait_ge(s["g_lo"], b * HPAIRS + HPAIRS)
            for tt in range(TT):
                for ht in range(HT):
                    for part in (HI, LO):
                        last = pe.matmul(bank[:, 6 + tt, :], g16[:, part, ht, tt * P:(tt + 1) * P], w2t[:, ht, :],
                                         start=(ht == 0 and part == HI), stop=(ht == HT - 1 and part == LO))
                last.then_inc(s["down_ready"], 1)
            pe.wait_ge(s["rows_lo"], b * 4 + 2)
            pe.wait_ge(s["ctx_lo"], b * 2 + 2)
            for et in range(FT):
                three(bank[:, et, :], lambda p, i: ctx16[:, p, i, et * P:(et + 1) * P],
                      lambda p, i: xs16[:, i, p, :], TT).then_inc(s["s_ready"], 1)
            for et in range(FT):
                pe.wait_ge(s["p_lo"], b * FT + et + 1)
                for tt in range(TT):
                    for j, (lp, rp) in enumerate(PASSES):
                        last = pe.matmul(bank[:, 4 + tt, :], ctxT16[:, lp, et, tt * P:(tt + 1) * P],
                                         p16[:, rp, et, :], start=(et == 0 and j == 0),
                                         stop=(et == FT - 1 and j == 2))
                    if et == FT - 1:
                        last.then_inc(s["ch_ready"], 1)
            pe.wait_ge(s["xn_ready"], b * 8 + 8)
            turn(T_ROUTER, 6)
            pe.wait_ge(s["lo_ready"], b * 8 + 8)
            for tt in range(TT):
                last = three(bank[:, 0, tt * EXPERTS:(tt + 1) * EXPERTS],
                             lambda p, i: xT16[:, p, i, tt * P:(tt + 1) * P], lambda p, i: rw16[:, p, i, :], FT)
            last.then_inc(s["logits_ready"], 1)

        with pe.Fori(0, BATCH) as b:
            body(b)

    @block.vector
    def _(dve):
        def body(b):
            steps = Chain(dve, s["dve_step"], DVE_STEPS, b)

            def layer_norm(ln, src):
                for tt in range(TT):
                    ins = dve.bn_stats(stats[:, tt], src[:, tt])
                steps.then(ins, alone=True)
                for tt in range(TT):
                    ins = dve.bn_aggr(moments[:, tt], stats[:, tt])
                ins.then_inc(s["stats_ready"], 1)
                dve.wait_ge(s["rstd_ready"], b * 4 + ln + 1)
                for tt in range(TT):
                    dve.tensor_scalar(xn[:, tt], src[:, tt], moments[:, tt, 0:1], rstd[:, tt:tt + 1],
                                      ALU.subtract, ALU.mult).then_inc(s["xn_ready"], 1)

            def low_part(which, first_bank):
                for i in range(2):
                    dve.wait_ge(s["hi_ready"], b * 8 + 2 * which + i + 1)
                    dve.tensor_tensor(xT16[:, LO, 2 * i:2 * i + 2, :].rearrange("p t n -> p (t n)"),
                                      bank[:, first_bank + i, :],
                                      xT16[:, HI, 2 * i:2 * i + 2, :].rearrange("p t n -> p (t n)"),
                                      ALU.subtract).then_inc(s["lo_ready"], 1)

            dve.wait_ge(s["x_loaded"], b * 16 + 16)
            layer_norm(LN1, xin)
            dve.wait_ge(s["k_ready"], b + 1)
            steps.then(dve.tensor_scalar(k32[:], bank[0:KVW, 2, 0:SEQ], bk_col[:, 0:1], None, ALU.add))
            steps.then(dve.tensor_copy(k16[:, HI], k32[:]))
            dve.tensor_tensor(k16[:, LO], k32[:], k16[:, HI], ALU.subtract).then_inc(s["k_split"], 1)
            dve.wait_ge(s["v_ready"], b + 1)
            for kt in range(TT):
                ins = dve.tensor_tensor(v_ones[:, kt, :, 0:HD],
                                        bank[:, 3, kt * KVW:(kt + 1) * KVW].rearrange("p (g d) -> p g d", d=HD),
                                        bv_row[:].rearrange("p (g d) -> p g d", d=HD), ALU.add)
            ins.then_inc(s["v_placed"], 1)
            low_part(T_ATTN_IN, 0)
            dve.wait_ge(s["q_scaled"], b * FT + FT)
            steps.then(dve.tensor_copy(q16[:, HI], q32[:]))
            dve.tensor_tensor(q16[:, LO], q32[:], q16[:, HI], ALU.subtract).then_inc(s["q_split"], 1)
            for u in range(16):
                g, qt = u // 2, u % 2
                dve.wait_ge(s["a_ready"], b * 16 + u + 1)
                dve.tensor_reduce(neg_max[:, qt, HPG * g:HPG * (g + 1)],
                                  bank[:, 2 * (u % 4):2 * (u % 4) + 2, :].rearrange("p a (r n) -> p (a r) n", r=2),
                                  AX.X, ALU.max, negate=True).then_inc(s["a_reduced"], 1)
            dve.wait_ge(s["m_turned"], b + 1)
            turned = bank[0:TT * HEADS, 6, 0:P]
            steps.then(dve.tensor_copy(m16[:, 0], turned))
            steps.then(dve.tensor_tensor(m_rest[:], turned, m16[:, 0], ALU.subtract))
            steps.then(dve.tensor_copy(m16[:, 1], m_rest[:]))
            dve.tensor_tensor(m16[:, 2], m_rest[:], m16[:, 1], ALU.subtract).then_inc(s["m_split"], 1)
            for i in range(4):
                qt, gg = i // 2, i % 2
                dve.wait_ge(s["o_turned"], b * 4 + i + 1)
                ps = bank[:, i, :].rearrange("p (r j e) -> p r j e", r=HPG, j=4)
                steps.then(dve.reciprocal(inv_sum[:, i], ps[:, :, :, HD]))
                dve.tensor_tensor(xn[:, qt, gg * SEQ:(gg + 1) * SEQ].rearrange("p (j r d) -> p r j d", j=4, r=HPG),
                                  ps[:, :, :, 0:HD],
                                  inv_sum[:, i].unsqueeze(3).to_broadcast([P, HPG, 4, HD]),
                                  ALU.mult).then_inc(s["o_ready"], 1)
            low_part(T_ATTN_OUT, 4)
            dve.wait_ge(s["biased"], b + 1)
            for tt in range(TT):
                dve.wait_ge(s["wo_ready"], b * 2 + tt + 1)
                dve.tensor_tensor(res[:, tt], bank[:, 6 + tt, :], xin[:, tt], ALU.add).then_inc(s["x1_ready"], 1)
            dve.wait_ge(s["x1_ready"], b * 2 + 2)
            layer_norm(LN2, res)
            low_part(T_FFN, 0)
            for hp in range(HPAIRS):
                w = pair_width(hp)
                dve.wait_ge(s["tanh_ready"], b * HPAIRS + hp + 1)
                steps.then(dve.scalar_tensor_tensor(out=gate_b[:, hp % 2, 0:w], in0=tanh_a[:, hp % 2, 0:w], scalar=1.0,
                                                    in1=bank[:, 2 * (hp % 3) + 1, 0:w], op0=ALU.add, op1=ALU.mult))
                if hp >= 2:
                    dve.wait_ge(s["g_lo"], b * HPAIRS + hp - 1)
                dve.scalar_tensor_tensor(out=g32[:, hp % 2, 0:w], in0=gate_b[:, hp % 2, 0:w], scalar=G_SCALE,
                                         in1=bank[:, 2 * (hp % 3), 0:w], op0=ALU.mult,
                                         op1=ALU.mult).then_inc(s["g_ready"], 1)
            for tt in range(TT):
                dve.wait_ge(s["down_ready"], b * 2 + tt + 1)
                ins = dve.scalar_tensor_tensor(out=res[:, tt], in0=bank[:, 6 + tt, :], scalar=ffn_scale[:, 0:1],
                                               in1=res[:, tt], op0=ALU.mult, op1=ALU.add)
            steps.then(ins)
            layer_norm(LN3, res)
            for et in range(FT):
                dve.wait_ge(s["s_ready"], b * FT + et + 1)
                steps.then(dve.tensor_reduce(ch_neg[:, et:et + 1], bank[:, et, :], AX.X, ALU.max, negate=True))
                dve.tensor_scalar(ch_bias[:, et:et + 1], ch_neg[:, et:et + 1], S_SCALE, None,
                                  ALU.mult).then_inc(s["max_ready"], 1)
            for et in range(FT):
                dve.wait_ge(s["e_ready"], b * FT + et + 1)
                steps.then(dve.reciprocal(ch_inv[:, et:et + 1], ch_sum[:, et:et + 1]))
                dve.tensor_scalar(p32[:, et], e32[:, et], ch_inv[:, et:et + 1], P_SCALE, ALU.mult,
                                  ALU.mult).then_inc(s["p_ready"], 1)
            for tt in range(TT):
                dve.wait_ge(s["ch_ready"], b * 2 + tt + 1)
                dve.scalar_tensor_tensor(out=res[:, tt], in0=bank[:, 4 + tt, :], scalar=1.0 / P_SCALE,
                                         in1=res[:, tt], op0=ALU.mult, op1=ALU.add).then_inc(s["x3_ready"], 1)
            dve.wait_ge(s["x3_ready"], b * 2 + 2)
            layer_norm(LN4, res)
            low_part(T_ROUTER, 6)
            dve.wait_ge(s["logits_ready"], b + 1)
            dve.tensor_reduce(lg_neg[:], bank[:, 0, 0:TT * EXPERTS].rearrange("p (t e) -> p t e", t=TT), AX.X,
                              ALU.max, negate=True).then_inc(s["lmax_ready"], 1)
            dve.wait_ge(s["lexp_ready"], b * 2 + 2)
            steps.then(dve.reciprocal(lg_inv[:], lg_sum[:]))
            for tt in range(TT):
                ins = dve.tensor_scalar(lg_prob[:, tt], lg_exp[:, tt], lg_inv[:, tt:tt + 1], None, ALU.mult)
            steps.then(ins, alone=True)
            for tt in range(TT):
                ins = dve.max(top8[:, tt], lg_prob[:, tt])
            steps.then(ins, alone=True)
            for tt in range(TT):
                dve.max_index(idx8[:, tt], top8[:, tt], lg_prob[:, tt])
            steps.then(dve.tensor_reduce(top_sum[:], top8[:, :, 0:TOPK], AX.X, ALU.add))
            steps.then(dve.reciprocal(top_inv[:], top_sum[:]))
            dve.tensor_copy(route_e[:, bass.ds(b * TT, TT), :], idx8[:, :, 0:TOPK])
            dve.tensor_tensor(route_w[:, bass.ds(b * TT, TT), :], top8[:, :, 0:TOPK],
                              top_inv[:].unsqueeze(2).to_broadcast([P, TT, TOPK]), ALU.mult)
            steps.end()

        dve.memset(q_stack[ROW_PAD:ROWS_B], 1.0).then_inc(s["ones_set"], 1)
        dve.memset(k_stack[ROW_PAD:ROWS_B], 1.0).then_inc(s["ones_set"], 1)
        dve.memset(eps_col[:], EPS).then_inc(s["ones_set"], 1)
        dve.memset(neg_max[:], 0.0).then_inc(s["ones_set"], 1)
        dve.memset(v_ones[:], 1.0).then_inc(s["ones_set"], 1)
        dve.wait_ge(s["ones_set"], 5)
        with dve.Fori(0, BATCH) as b:
            body(b)



def prepare(nc, scope, sb, sem, bank, ident, ident16, ones16, wq16, wk16, wv16, wo16, rw16, w1t, w3t, w2t,
            half_s1, ffn_scale, bq_col, bk_col, bv_row, bo_row, mask_q, mask_k, neg_half, zeros,
            mq_d, mk_d, pad_d, wq_d, bq_d, wk_d, bk_d, wv_d, bv_d, wo_d, bo_d, w1_d, w3_d, w2_d, rw_d,
            padbias_dram):

    def t(name, shape, dt):
        return sb(name, shape, dt, scope)

    split = [(wk_d, wk16, KVW), (wv_d, wv16, KVW), (wq_d, wq16, DM), (wo_d, wo16, DM), (rw_d, rw16, EXPERTS)]
    raw = [t(f"raw{i}", [P, FT, n], F32) for i, (_, _, n) in enumerate(split)]
    w1_raw = t("w1_raw", [P, FT, HIDDEN], F32)
    w3_raw = t("w3_raw", [P, FT, HIDDEN], F32)
    w2_raw = t("w2_raw", [P, HT, DM], F32)
    below = t("below", [P, HT * DM], F16)
    mq_raw = t("mq_raw", [P, TT, SEQ // 4], I32)
    mk_raw = t("mk_raw", [P, TT, SEQ // 4], I32)
    pad_raw = t("pad_raw", [BATCH, SEQ // 4], I32)
    pad16 = t("pad16", [BATCH, SEQ], F16)
    bq_raw = t("bq_raw", [P, FT], F32)
    ones32 = t("ones32", [P, P], F32)
    part_sums = t("part_sums", [P, 3, 140], F32)
    sums = t("sums", [P, 3], F32)
    scales = t("scales", [P, 3], F32)
    thresholds = t("thresholds", [P, 3, 2], F32)
    s12 = t("s12", [P, 1], F32)
    ws_loaded, small_loaded = sem("ws_loaded"), sem("small_loaded")
    ternary_loaded = [sem(f"ternary_loaded{i}") for i in range(3)]
    w_hi, pool_made, w2_zeroed = sem("w_hi"), sem("pool_made"), sem("w2_zeroed")
    sums_made, totals_made, pre_step, pad_stored = sem("sums_made"), sem("totals_made"), sem("pre_step"), sem("pad_stored")
    pad_made = sem("pad_made")
    TAIL = HIDDEN - (HT - 1) * P
    with nc.Block() as block:
        @block.sync
        def _(sp):
            sp.wait_ge(w2_zeroed, 1)
            sp.dma_start(w2_raw[:, 0:HT - 1, :],
                         w2_d[0:(HT - 1) * P].rearrange("(t p) d -> p t d", p=P)).then_inc(ternary_loaded[2], 16)
            sp.dma_start(w2_raw[0:TAIL, HT - 1, :], w2_d[(HT - 1) * P:HIDDEN]).then_inc(ternary_loaded[2], 16)
            sp.dma_start(w3_raw[:], w3_d).then_inc(ternary_loaded[1], 16)
            sp.wait_ge(pad_made, 1)
            sp.dma_start(padbias_dram, pad16[:]).then_inc(pad_stored, 16)
            sp.wait_ge(pad_stored, 16)

        @block.scalar
        def _(act):
            act.dma_start(w1_raw[:], w1_d).then_inc(ternary_loaded[0], 16)
            for i, (src, _, _) in enumerate(split):
                act.dma_start(raw[i][:], src).then_inc(ws_loaded, 16)
            act.wait_ge(ws_loaded, 16 * len(split))
            for i, (_, dst, _) in enumerate(split):
                act.copy(dst[:, HI], raw[i][:]).then_inc(w_hi, 1)

        @block.gpsimd
        def _(pool):
            pool.memset(ident[:], 0.0)
            pool.memset(ident16[:], 0.0)
            pool.memset(zeros[:], 0.0)
            pool.memset(neg_half[:], -0.5).then_inc(pool_made, 1)
            pool.dma_start(mq_raw[:], mq_d).then_inc(small_loaded, 16)
            pool.dma_start(mk_raw[:], mk_d).then_inc(small_loaded, 16)
            pool.dma_start(pad_raw[:], pad_d).then_inc(small_loaded, 16)
            pool.dma_start(bq_raw[:], bq_d).then_inc(small_loaded, 16)
            pool.dma_start(bk_col[:], bk_d).then_inc(small_loaded, 16)
            pool.dma_start(bv_row[:], bv_d.to_broadcast([P, KVW])).then_inc(small_loaded, 16)
            pool.dma_start(bo_row[:], bo_d.to_broadcast([P, DM])).then_inc(small_loaded, 16)
            pool.wait_ge(pool_made, 1)
            for m in (ident, ident16):
                pool.affine_select(out=m[:], in_=m[:], compare_op=ALU.not_equal, fill=1.0, base=0,
                                   pattern=[[-1, P]], channel_multiplier=1).then_inc(pool_made, 1)
            for i, (_, dst, _) in enumerate(split):
                pool.wait_ge(w_hi, i + 1)
                pool.tensor_tensor(dst[:, LO], raw[i][:], dst[:, HI], ALU.subtract)

        @block.tensor
        def _(pe):
            pe.wait_ge(sums_made, 4)
            pe.matmul(bank[:, 0, 0:3], ones32[:], sums[:], start=True, stop=True).then_inc(totals_made, 1)

        @block.vector
        def _(dve):
            count = [0]

            def step(ins):
                count[0] += 1
                ins.then_inc(pre_step, 1)
                dve.wait_ge(pre_step, count[0])

            step(dve.memset(w2_raw[64:P, HT - 1, :], 0.0))
            dve.memset(w2_raw[0:64, HT - 1, :], 0.0).then_inc(w2_zeroed, 1)
            dve.memset(w1t[:, :, HIDDEN:HPAD], 0.0)
            dve.memset(w3t[:, :, HIDDEN:HPAD], 0.0)
            dve.memset(ones16[:], 1.0)
            dve.memset(ones32[:], 1.0).then_inc(sums_made, 1)
            dve.wait_ge(small_loaded, 7 * 16)
            dve.tensor_scalar(mask_q[:], mq_raw[:].bitcast(U8), MASKED, None, ALU.mult)
            dve.tensor_scalar(mask_k[:], mk_raw[:].bitcast(U8), MASKED, None, ALU.mult)
            dve.tensor_scalar(pad16[:], pad_raw[:].bitcast(U8), MASKED, None, ALU.mult).then_inc(pad_made, 1)
            dve.tensor_scalar(bq_col[:], bq_raw[:], 1.0 / 4.0, None, ALU.mult)
            flat = [w1_raw[:].rearrange("p t n -> p (t n)"), w3_raw[:].rearrange("p t n -> p (t n)"),
                    w2_raw[:].rearrange("p t n -> p (t n)")]
            chunks = [FT * HIDDEN // 140, FT * HIDDEN // 140, 44]
            for i in range(3):
                dve.wait_ge(ternary_loaded[i], 32 if i == 2 else 16)
                n = flat[i].shape[1] // chunks[i]
                step(dve.tensor_reduce(part_sums[:, i, 0:n], flat[i].rearrange("p (n c) -> p n c", c=chunks[i]),
                                       AX.X, ALU.add, apply_absolute_value=True))
                dve.tensor_reduce(sums[:, i:i + 1], part_sums[:, i, 0:n], AX.X, ALU.add).then_inc(sums_made, 1)
            dve.wait_ge(totals_made, 1)
            step(dve.tensor_scalar(scales[:], bank[:, 0, 0:3], 1.0 / (HIDDEN * DM), None, ALU.mult))
            dve.tensor_scalar(thresholds[:, :, 0], scales[:], 0.5, None, ALU.mult)
            dve.tensor_scalar(thresholds[:, :, 1], scales[:], -0.5, None, ALU.mult)
            dve.tensor_scalar(half_s1[:], scales[:, 0:1], 0.5, None, ALU.mult)
            step(dve.tensor_tensor(s12[:], scales[:, 0:1], scales[:, 1:2], ALU.mult))
            step(dve.scalar_tensor_tensor(out=ffn_scale[:], in0=s12[:], scalar=0.5 / G_SCALE, in1=scales[:, 2:3],
                                          op0=ALU.mult, op1=ALU.mult))
            for i, (w, dst) in enumerate(((flat[0], w1t[:, :, 0:HIDDEN]), (flat[1], w3t[:, :, 0:HIDDEN]),
                                          (flat[2], w2t[:]))):
                n = w.shape[1]
                step(dve.tensor_scalar(below[:, 0:n], w, thresholds[:, i, 1:2], None, ALU.is_lt))
                shaped = [a.rearrange("p (t n) -> p t n", n=dst.shape[2]) for a in (w, below[:, 0:n])]
                step(dve.scalar_tensor_tensor(out=dst, in0=shaped[0], scalar=thresholds[:, i, 0:1], in1=shaped[1],
                                              op0=ALU.is_gt, op1=ALU.subtract))


def expert_layer(nc, scope, sb, sem, bank, ident16, ones16, route_w, route_e, gu_d, da_d, db_d, x3_dram,
                 xn_dram, slots_dram, y_dram, eid_dram, out_d):

    def t(name, shape, dt):
        return sb(name, shape, dt, scope)

    GU = 2 * INTER
    expert_i = t("expert_i", [P, EXPERTS], I32)
    expert_f = t("expert_f", [P, EXPERTS], F32)
    block_i = t("block_i", [P, 1], I32)
    block_f = t("block_f", [P, 1], F32)
    before = t("before", [P, P], F16)
    starts_ends = t("starts_ends", [EXPERTS, 2 * EXPERTS], F16)
    chosen = t("chosen", [P, TILES * TOPK, EXPERTS], F32)
    member = t("member", [P, TILES, EXPERTS], F16)
    slot_of = t("slot_of", [P, TILES, EXPERTS], F32)
    picked = t("picked", [P, TILES * TOPK, EXPERTS], F32)
    slot_f = t("slot_f", [P, TILES * TOPK], F32)
    slot_u = t("slot_u", [P, TILES * TOPK], U32)
    count_i = t("count_i", [EXPERTS, 1], I32)
    blocks_i = t("blocks_i", [EXPERTS, 1], I32)
    blocks_f = t("blocks_f", [EXPERTS, 1], F32)
    blocks_row = t("blocks_row", [EXPERTS, P], F16)
    base = t("base", [P, 2 * EXPERTS], F32)
    ended = t("ended", [P, EXPERTS], F32)
    eid_f = t("eid_f", [P, 1], F32)
    eid_i = t("eid_i", [P, 1], I32)
    eids = t("eids", [1, P], I32)
    rows16 = t("rows16", [P, TILES, 2 * DM], F16)
    xg = t("xg", [P, 2, TT, 2 * DM], F16)
    xgT = t("xgT", [P, 2, 2, FT, BS], F16)
    gu_raw = t("gu_raw", [P, 2, FT, GU], F32)
    dn_raw = t("dn_raw", [P, 2, 2, DM], F32)
    gu16 = t("gu16", [P, 2, 2, FT, GU], F16)
    dn16 = t("dn16", [P, 2, 2, 2, DM], F16)
    silu_g = t("silu_g", [P, 2, 2 * BS], F32)
    h32 = t("h32", [P, 2, 2 * BS], F32)
    h16 = t("h16", [P, 2, 2, 2 * BS], F16)
    y32 = t("y32", [P, 2, TT, DM], F32)
    NY = 8
    yg = t("yg", [P, NY, DM], F32)
    acc = t("acc", [P, 2, DM], F32)

    names = ("rows_loaded iotas member_ready counted blocks_ready based slots_ready eid_ready eid_out eid_in "
             "scattered route_step gu_hi dn_hi gu_lo dn_lo x_turned xT_hi xT_lo gate_ready "
             "silu_done h_ready h_hi h_lo y_ready y_act y_dve added out_stored "
             "padded tri_ready ").split()
    s = {n: sem("e_" + n) for n in names}
    gu_loaded, dn_loaded, xg_loaded, y_stored, x3_loaded = (
        [sem(f"e_{n}{u}") for u in range(2)] for n in ("gu_loaded", "dn_loaded", "xg_loaded", "y_stored", "x3_loaded"))
    y_gathered = [sem(f"e_y_gathered{i}") for i in range(NY)]
    block = scope.enter_context(nc.Block())

    @block.sync
    def _(sp):
        sp.dma_start(rows16[:], xn_dram.rearrange("(t p) c -> p t c", p=P)).then_inc(s["rows_loaded"], 16)
        sp.wait_ge(s["eid_ready"], 1)
        sp.dma_start(eid_dram.rearrange("(p o) -> p o", o=1), eid_i[:]).then_inc(s["eid_out"], 16)
        sp.wait_ge(s["eid_out"], 16)
        sp.dma_start(eids[:], eid_dram.rearrange("(o p) -> o p", o=1)).then_inc(s["eid_in"], 16)
        sp.wait_ge(s["eid_in"], 16)
        sp.wait_ge(s["padded"], 1)

        def gate_up_weights(n, u):
            e = sp.value_load(eids[0:1, bass.ds(n, 1)], min_val=0, max_val=EXPERTS - 1)
            if not early(n):
                sp.wait_ge(s["gu_lo"], n - 1)
            sp.dma_start(gu_raw[:, u], gu_d[bass.ds(e, 1)].rearrange("o p t n -> (o p) t n")).then_inc(gu_loaded[u], 16)

        def down_weights(n, u):
            e = sp.value_load(eids[0:1, bass.ds(n, 1)], min_val=0, max_val=EXPERTS - 1)
            if not early(n):
                sp.wait_ge(s["dn_lo"], n - 1)
            sp.dma_start(dn_raw[:, u, 0], da_d[bass.ds(e, 1)].rearrange("o p n -> (o p) n")).then_inc(dn_loaded[u], 16)
            sp.dma_start(dn_raw[64:P, u, 1], db_d[bass.ds(e, 1)].rearrange("o p n -> (o p) n")).then_inc(dn_loaded[u], 16)

        def tokens(n, u):
            if not early(n):
                sp.wait_ge(s["x_turned"], 2 * n - 2)
            src = pick(slots_dram.rearrange("(n t p) c -> n p t c", n=NBLK, p=P), n)
            sp.dma_start(xg[:, u], src).then_inc(xg_loaded[u], 16)

        for u in range(2):
            gate_up_weights(u, u)
            down_weights(u, u)
        sp.wait_ge(s["scattered"], 16 * TILES * TOPK)
        tokens(0, 0)
        tokens(1, 1)
        with sp.Fori(1, NBLK // 2) as i:
            for u in range(2):
                gate_up_weights(2 * i + u, u)
                tokens(2 * i + u, u)
                down_weights(2 * i + u, u)
        gate_up_weights(NBLK - 1, 0)
        tokens(NBLK - 1, 0)
        down_weights(NBLK - 1, 0)
        for tile in range(2):
            sp.dma_start(acc[:, tile], x3_dram[tile * P:(tile + 1) * P]).then_inc(x3_loaded[tile % 2], 16)
        for tile in range(TILES):
            sp.wait_ge(s["added"], TOPK * (tile + 1))
            sp.dma_start(out_d[tile * P:(tile + 1) * P], acc[:, tile % 2]).then_inc(s["out_stored"], 16)
            if tile + 2 < TILES:
                sp.wait_ge(s["out_stored"], 16 * (tile + 1))
                sp.dma_start(acc[:, tile % 2], x3_dram[(tile + 2) * P:(tile + 3) * P]).then_inc(x3_loaded[tile % 2], 16)
        sp.wait_ge(s["out_stored"], 16 * TILES)

    @block.gpsimd
    def _(pool):
        pool.memset(before[:], 1.0)
        pool.memset(starts_ends[:], 1.0).then_inc(s["iotas"], 1)
        pool.iota(expert_i[:], pattern=[[1, EXPERTS]], base=0, channel_multiplier=0).then_inc(s["iotas"], 1)
        pool.iota(block_i[:], pattern=[[0, 1]], base=0, channel_multiplier=1).then_inc(s["iotas"], 1)
        pool.wait_ge(s["iotas"], 1)
        pool.affine_select(out=before[:], in_=before[:], compare_op=ALU.is_gt, fill=0.0, base=0,
                           pattern=[[1, P]], channel_multiplier=-1).then_inc(s["tri_ready"], 1)
        pool.affine_select(out=starts_ends[:, 0:EXPERTS], in_=starts_ends[:, 0:EXPERTS], compare_op=ALU.is_gt,
                           fill=0.0, base=0, pattern=[[1, EXPERTS]], channel_multiplier=-1).then_inc(s["tri_ready"], 1)
        pool.affine_select(out=starts_ends[:, EXPERTS:], in_=starts_ends[:, EXPERTS:], compare_op=ALU.is_ge,
                           fill=0.0, base=0, pattern=[[1, EXPERTS]], channel_multiplier=-1).then_inc(s["tri_ready"], 1)
        pool.wait_ge(s["rows_loaded"], 16)
        pool.wait_ge(s["slots_ready"], 1)
        for tile in range(TILES):
            for k in range(TOPK):
                c = tile * TOPK + k
                pool.indirect_dma_start(out=slots_dram,
                                        out_offset=bass.IndirectOffsetOnAxis(ap=slot_u[:, c:c + 1], axis=0),
                                        in_=rows16[:, tile, :], in_offset=None).then_inc(s["scattered"], 16)

        def split_down(n, u):
            if not (isinstance(n, int) and n >= NBLK - 2):
                pool.wait_ge(s["dn_hi"], n + 3)
                pool.tensor_tensor(dn16[:, u, LO], dn_raw[:, u], dn16[:, u, HI], ALU.subtract).then_inc(s["dn_lo"], 1)

        def split_h(n, u):
            pool.wait_ge(s["h_hi"], n + 1)
            pool.tensor_tensor(h16[:, u, LO], h32[:, u], h16[:, u, HI], ALU.subtract).then_inc(s["h_lo"], 1)

        split_down(-2, 0)
        split_down(-1, 1)
        pipeline(pool, lambda n, u: None, split_h, split_down)
        pool.wait_ge(y_stored[0], 16 * (NBLK // 2 + 2))
        pool.wait_ge(y_stored[1], 16 * (NBLK // 2 + 1))
        for c in range(TILES * TOPK):
            if c >= NY:
                pool.wait_ge(s["added"], c - NY + 1)
            pool.indirect_dma_start(out=yg[:, c % NY], out_offset=None, in_=y_dram,
                                    in_offset=bass.IndirectOffsetOnAxis(ap=slot_u[:, c:c + 1], axis=0)
                                    ).then_inc(y_gathered[c % NY], 16)

    @block.scalar
    def _(act):
        def split(n, u):
            act.wait_ge(gu_loaded[u], n * 8 + 16 - 8 * u)
            if not early(n):
                act.wait_ge(s["gate_ready"], n - 1)
            act.copy(gu16[:, u, HI], gu_raw[:, u]).then_inc(s["gu_hi"], 1)
            act.wait_ge(s["x_turned"], n * 2 + 1)
            act.copy(xgT[:, u, HI].rearrange("p t n -> p (t n)"), bank[:, 0, :].bitcast(F16)).then_inc(s["xT_hi"], 1)

        def gate(n, u):
            act.wait_ge(s["gate_ready"], n + 1)
            act.activation(silu_g[:, u, 0:BS], bank[:, 2 + 2 * u, 0:BS], ACT.Silu)
            act.activation(silu_g[64:P, u, BS:2 * BS], bank[0:64, 3 + 2 * u, 0:BS], ACT.Silu).then_inc(s["silu_done"], 1)
            act.wait_ge(s["h_ready"], n + 1)
            act.copy(h16[:, u, HI], h32[:, u]).then_inc(s["h_hi"], 1)

        def store(n, u):
            act.wait_ge(y_stored[u], n * 8 + 16 - 8 * u)
            act.wait_ge(s["y_ready"], n * 2 + 1)
            act.copy(y32[:, u, 0], bank[:, 6, :]).then_inc(s["y_act"], 1)
            act.wait_ge(s["y_act"], n + 1)
            act.wait_ge(s["y_dve"], n + 1)
            dst = pick(y_dram.rearrange("(n t p) c -> n p t c", n=NBLK, p=P), n)
            act.dma_start(dst, y32[:, u]).then_inc(y_stored[u], 16)

        pipeline(act, split, gate, store)

    @block.tensor
    def _(pe):
        pe.wait_ge(s["member_ready"], 1)
        pe.wait_ge(s["tri_ready"], 3)
        pe.matmul(bank[:, 0, :], before[:], member[:].rearrange("p t e -> p (t e)"), start=True, stop=True)
        for d in range(1, TILES):
            pe.matmul(bank[:, 0, d * EXPERTS:], ones16[:],
                      member[:, 0:TILES - d, :].rearrange("p t e -> p (t e)"), start=False, stop=True,
                      skip_group_check=True)
        for tile in range(TILES):
            last = pe.matmul(bank[0:EXPERTS, 1, 0:1], member[:, tile, :], ones16[:, 0:1], start=(tile == 0),
                             stop=(tile == TILES - 1))
        last.then_inc(s["counted"], 1)
        pe.wait_ge(s["blocks_ready"], 1)
        pe.matmul(bank[:, 2, 0:2 * EXPERTS], blocks_row[:], starts_ends[:], start=True,
                  stop=True).then_inc(s["based"], 1)

        def turn(n, u):
            pe.wait_ge(xg_loaded[u], n * 8 + 16 - 8 * u)
            if not (isinstance(n, int) and n < 1):
                pe.wait_ge(s["xT_hi"], n)
                pe.wait_ge(s["xT_lo"], n)
            for part in (HI, LO):
                for ft in range(FT):
                    for tt in range(TT):
                        last = pe.transpose(bank[:, part, :].bitcast(F16)[:, ft * BS + tt * P:ft * BS + (tt + 1) * P],
                                            xg[:, u, tt, part * DM + ft * P:part * DM + (ft + 1) * P], ident16[:])
                last.then_inc(s["x_turned"], 1)

        def gate_up(n, u):
            pe.wait_ge(s["gu_lo"], n + 1)
            pe.wait_ge(s["xT_hi"], n + 1)
            pe.wait_ge(s["xT_lo"], n + 1)
            if not early(n):
                pe.wait_ge(s["h_ready"], n - 1)
            for m, out in enumerate((bank[:, 2 + 2 * u, 0:BS], bank[:, 2 + 2 * u, BS:2 * BS], bank[:, 3 + 2 * u, 0:BS])):
                for ft in range(FT):
                    for j, (lp, rp) in enumerate(PASSES):
                        last = pe.matmul(out, gu16[:, u, lp, ft, m * P:(m + 1) * P], xgT[:, u, rp, ft, :],
                                         start=(ft == 0 and j == 0), stop=(ft == FT - 1 and j == 2))
            last.then_inc(s["gate_ready"], 1)

        def down(n, u):
            pe.wait_ge(s["dn_lo"], n + 1)
            pe.wait_ge(s["h_lo"], n + 1)
            if not (isinstance(n, int) and n < 1):
                pe.wait_ge(s["y_act"], n)
                pe.wait_ge(s["y_dve"], n)
            for tt in range(TT):
                for kt in range(2):
                    for j, (lp, rp) in enumerate(PASSES):
                        last = pe.matmul(bank[:, 6 + tt, :], h16[:, u, lp, kt * BS + tt * P:kt * BS + (tt + 1) * P],
                                         dn16[:, u, rp, kt, :], start=(kt == 0 and j == 0), stop=(kt == 1 and j == 2))
                last.then_inc(s["y_ready"], 1)

        pe.wait_ge(s["slots_ready"], 1)
        pipeline(pe, turn, gate_up, down)

    @block.vector
    def _(dve):
        count = [0]

        def step(ins):
            count[0] += 1
            ins.then_inc(s["route_step"], 1)
            dve.wait_ge(s["route_step"], count[0])

        dve.memset(dn_raw[0:64, :, 1], 0.0).then_inc(s["padded"], 1)
        for u in range(2):
            dve.memset(h32[0:64, u, BS:2 * BS], 0.0).then_inc(y_stored[u], 16)
        dve.wait_ge(s["iotas"], 3)
        dve.tensor_copy(block_f[:], block_i[:])
        step(dve.tensor_copy(expert_f[:], expert_i[:]))
        shape = [P, TILES * TOPK, EXPERTS]
        step(dve.tensor_tensor(chosen[:], route_e[:].rearrange("p t k -> p (t k)").unsqueeze(2).to_broadcast(shape),
                               expert_f[:].unsqueeze(1).to_broadcast(shape), ALU.is_equal))
        dve.tensor_reduce(member[:], chosen[:].rearrange("p (t k) e -> p t e k", k=TOPK), AX.X,
                          ALU.max).then_inc(s["member_ready"], 1)
        dve.wait_ge(s["counted"], 1)
        step(dve.tensor_scalar(count_i[:], bank[0:EXPERTS, 1, 0:1], float(BS - 1), None, ALU.add))
        step(dve.tensor_scalar(blocks_i[:], count_i[:], BS.bit_length() - 1, None, ALU.logical_shift_right))
        step(dve.tensor_copy(blocks_f[:], blocks_i[:]))
        dve.tensor_scalar(blocks_row[:], ones16[0:EXPERTS, :], blocks_f[:, 0:1], None,
                          ALU.mult).then_inc(s["blocks_ready"], 1)
        dve.wait_ge(s["based"], 1)
        dve.tensor_scalar(base[:, 0:EXPERTS], bank[:, 2, 0:EXPERTS], float(BS), None, ALU.mult)
        step(dve.tensor_scalar(ended[:], bank[:, 2, EXPERTS:2 * EXPERTS], block_f[:, 0:1], None, ALU.is_le))
        step(dve.tensor_reduce(eid_f[:], ended[:], AX.X, ALU.add))
        dve.tensor_scalar(eid_i[:], eid_f[:], float(EXPERTS - 1), None, ALU.min).then_inc(s["eid_ready"], 1)
        step(dve.tensor_tensor(slot_of[:], bank[:, 0, :].rearrange("p (t e) -> p t e", e=EXPERTS),
                               base[:, 0:EXPERTS].unsqueeze(1).to_broadcast([P, TILES, EXPERTS]), ALU.add))
        for k in range(TOPK):
            ins = dve.tensor_tensor(picked[:].rearrange("p (t k) e -> p t k e", k=TOPK)[:, :, k],
                                    chosen[:].rearrange("p (t k) e -> p t k e", k=TOPK)[:, :, k],
                                    slot_of[:], ALU.mult)
        step(ins)
        step(dve.tensor_reduce(slot_f[:], picked[:], AX.X, ALU.add))
        dve.tensor_copy(slot_u[:], slot_f[:]).then_inc(s["slots_ready"], 1)

        def split_down(u):
            dve.tensor_copy(dn16[:, u, HI], dn_raw[:, u]).then_inc(s["dn_hi"], 1)

        def split(n, u):
            dve.wait_ge(s["gu_hi"], n + 1)
            dve.tensor_tensor(gu16[:, u, LO], gu_raw[:, u], gu16[:, u, HI], ALU.subtract).then_inc(s["gu_lo"], 1)
            dve.wait_ge(s["x_turned"], n * 2 + 2)
            dve.tensor_copy(xgT[:, u, LO].rearrange("p t n -> p (t n)"), bank[:, 1, :].bitcast(F16)).then_inc(s["xT_lo"], 1)

        def gate(n, u):
            dve.wait_ge(s["silu_done"], n + 1)
            dve.tensor_tensor(h32[:, u, 0:BS], silu_g[:, u, 0:BS], bank[:, 2 + 2 * u, BS:2 * BS], ALU.mult)
            dve.tensor_tensor(h32[64:P, u, BS:2 * BS], silu_g[64:P, u, BS:2 * BS], bank[64:P, 3 + 2 * u, 0:BS],
                              ALU.mult).then_inc(s["h_ready"], 1)

        def leave(n, u):
            dve.wait_ge(y_stored[u], n * 8 + 16 - 8 * u)
            dve.wait_ge(s["y_ready"], n * 2 + 2)
            dve.tensor_copy(y32[:, u, 1], bank[:, 7, :]).then_inc(s["y_dve"], 1)
            if not (isinstance(n, int) and n >= NBLK - 2):
                dve.wait_ge(dn_loaded[u], n * 16 + 64 - 16 * u)
                split_down(u)

        for u in range(2):
            dve.wait_ge(dn_loaded[u], 32)
            split_down(u)
        pipeline(dve, split, gate, leave)
        for c in range(TILES * TOPK):
            tile, k = c // TOPK, c % TOPK
            if k == 0:
                dve.wait_ge(x3_loaded[tile % 2], 16 * (tile // 2 + 1))
            else:
                dve.wait_ge(s["added"], c)
            dve.wait_ge(y_gathered[c % NY], 16 * (c // NY + 1))
            dve.scalar_tensor_tensor(out=acc[:, tile % 2], in0=yg[:, c % NY], scalar=route_w[:, tile, k:k + 1],
                                     in1=acc[:, tile % 2], op0=ALU.mult, op1=ALU.add).then_inc(s["added"], 1)



def kernel(x, ctx_2048, mask_SxS2_bc0, mask_BxS2_bk0, L0_xattn_Wq, L0_xattn_bq, L0_xattn_Wk, L0_xattn_bk,
           L0_xattn_Wv, L0_xattn_bv, L0_xattn_Wo, L0_xattn_bo, L0_ffn_w1, L0_ffn_w3, L0_ffn_w2,
           L1_ffn_router_w, L1_ffn_gate_w, L1_ffn_up_w, L1_ffn_down_w):
    import concourse.bacc as bacc
    from concourse.bass_utils import run_bass_kernel_spmd

    def tiled(w):
        w = np.asarray(w).T
        return w.reshape(-1, P, w.shape[1]).transpose(1, 0, 2)

    def words(m):
        return np.ascontiguousarray(m).view(np.int32)

    mask = np.asarray(mask_SxS2_bc0)
    gate = np.asarray(L1_ffn_gate_w).transpose(0, 2, 1)
    up = np.asarray(L1_ffn_up_w).transpose(0, 2, 1)
    gu = np.concatenate([gate[:, :, :P], up[:, :, :P], gate[:, :, P:], up[:, :, P:]], axis=2)
    down = np.asarray(L1_ffn_down_w).transpose(0, 2, 1)
    arrays = {
        "x": np.asarray(x),
        "ctx": np.asarray(ctx_2048),
        "ctxT": np.asarray(ctx_2048).transpose(0, 2, 1),
        "mq": words(mask.reshape(TT, P, SEQ).transpose(1, 0, 2)),
        "mk": words(mask.T.reshape(TT, P, SEQ).transpose(1, 0, 2)),
        "pad": words(np.asarray(mask_BxS2_bk0)),
        "wq": tiled(L0_xattn_Wq),
        "bq": np.asarray(L0_xattn_bq).reshape(FT, P).T,
        "wk": tiled(L0_xattn_Wk),
        "bk": np.asarray(L0_xattn_bk).reshape(KVW, 1),
        "wv": tiled(L0_xattn_Wv),
        "bv": np.asarray(L0_xattn_bv).reshape(1, KVW),
        "wo": tiled(L0_xattn_Wo),
        "bo": np.asarray(L0_xattn_bo).reshape(1, DM),
        "w1": tiled(L0_ffn_w1),
        "w3": tiled(L0_ffn_w3),
        "w2": np.asarray(L0_ffn_w2).T,
        "rw": tiled(L1_ffn_router_w),
        "gu": gu.reshape(EXPERTS, FT, P, 2 * INTER).transpose(0, 2, 1, 3),
        "da": down[:, :P],
        "db": down[:, P:],
    }
    nc = bacc.Bacc("TRN2", target_bir_lowering=False, num_devices=1)
    given, args = {}, {}
    for name, a in arrays.items():
        given[name] = np.ascontiguousarray(a)
        args[name + "_d"] = nc.dram_tensor(name, given[name].shape, mybir.dt.from_np(given[name].dtype),
                                           kind="ExternalInput").ap()
    out = nc.dram_tensor("out", (TOKENS, DM), F32, kind="ExternalOutput").ap()
    build(nc, out_d=out, **args)
    r = run_bass_kernel_spmd(nc, [given], core_ids=[0])
    return np.asarray(r.results[0]["out"]).reshape(BATCH, SEQ, DM)
```

```python
from contextlib import ExitStack

import numpy as np

import concourse.bass as bass
from concourse import mybir

F32 = mybir.dt.float32
F16 = mybir.dt.float16
I32 = mybir.dt.int32
U32 = mybir.dt.uint32
U8 = mybir.dt.uint8
ALU = mybir.AluOpType
ACT = mybir.ActivationFunctionType
AX = mybir.AxisListType

P = 128
BATCH, SEQ, DM = 8, 256, 512
TOKENS = BATCH * SEQ
TT = SEQ // P
FT = DM // P
HEADS, GROUPS, HD = 32, 8, 16
HPG = HEADS // GROUPS
KVW = GROUPS * HD
HIDDEN = int(2 * DM * 4 / 3)
HT = -(-HIDDEN // P)
HPAD = HT * P
HPAIRS = -(-HT // 2)
EXPERTS, INTER, TOPK = 32, 192, 4
TILES = TOKENS // P
BS = 256
NBLK = TOKENS * TOPK // BS + EXPERTS - 1
SLOTS = NBLK * BS
EPS = 1e-5
MASKED = -60000.0
ZERO_RUN = 504
ZERO_RUNS = SLOTS * 2 * DM // (P * BATCH * ZERO_RUN)
ROW_PAD = 4 * HD
ROW_MAX = ROW_PAD + 1
ROWS_A = ROW_MAX
ROWS_B = ROW_MAX + 3
G_SCALE = 1.0 / 64.0
P_SCALE = 256.0
HI, LO = 0, 1
PASSES = ((HI, HI), (HI, LO), (LO, HI))


def pair_width(hp):
    return min(2, HT - 2 * hp) * SEQ


def pick(view, n):
    if isinstance(n, int):
        return view[n]
    names = " ".join("bcde"[:len(view.shape) - 2])
    return view[bass.ds(n, 1)].rearrange(f"o a {names} -> (o a) {names}")


def early(n):
    return isinstance(n, int) and n < 2


def pipeline(eng, first, second, third):
    first(0, 0)
    first(1, 1)
    second(0, 0)
    first(2, 0)
    second(1, 1)
    third(0, 0)
    with eng.Fori(1, NBLK // 2) as i:
        for u in range(2):
            n = 2 * i + u
            first(n + 1, 1 - u)
            second(n, u)
            third(n - 1, 1 - u)
    second(NBLK - 1, 0)
    third(NBLK - 2, 1)
    third(NBLK - 1, 0)


def build(nc, x_d, ctx_d, ctxT_d, mq_d, mk_d, pad_d, wq_d, bq_d, wk_d, bk_d, wv_d, bv_d, wo_d, bo_d,
          w1_d, w3_d, w2_d, rw_d, gu_d, da_d, db_d, out_d):
    def dram(name, shape, dt):
        return nc.dram_tensor(name, shape, dt, kind="Internal").ap()

    q_dram = dram("q_dram", (2, DM, SEQ), F16)
    k_dram = dram("k_dram", (2, KVW, SEQ), F16)
    m_dram = dram("m_dram", (3, TT * HEADS, P), F16)
    padbias_dram = dram("padbias_dram", (BATCH, SEQ), F16)
    x3_dram = dram("x3_dram", (TOKENS, DM), F32)
    xn_dram = dram("xn_dram", (TOKENS, 2 * DM), F16)
    slots_dram = dram("slots_dram", (SLOTS, 2 * DM), F16)
    y_dram = dram("y_dram", (SLOTS, DM), F32)
    eid_dram = dram("eid_dram", (P,), I32)

    ctx = ExitStack()
    with ctx:
        def sb(name, shape, dt, scope=ctx):
            return scope.enter_context(nc.sbuf_tensor(name, shape, dt))

        def sem(name):
            return ctx.enter_context(nc.semaphore(name))

        bank = ctx.enter_context(nc.psum_tensor("bank", [P, 8, 512], F32))

        ident = sb("ident", [P, P], F32)
        ident16 = sb("ident16", [P, P], F16)
        ones16 = sb("ones16", [P, P], F16)
        route_w = sb("route_w", [P, TILES, TOPK], F32)
        route_e = sb("route_e", [P, TILES, TOPK], F32)

        with ExitStack() as dense:
            dense_layers(nc, dense, sb, sem, bank, ident, ident16, ones16, route_w, route_e,
                         x_d, ctx_d, ctxT_d, mq_d, mk_d, pad_d, wq_d, bq_d, wk_d, bk_d, wv_d, bv_d,
                         wo_d, bo_d, w1_d, w3_d, w2_d, rw_d, q_dram, k_dram, m_dram, padbias_dram,
                         x3_dram, xn_dram, slots_dram)
        with ExitStack() as sparse:
            expert_layer(nc, sparse, sb, sem, bank, ident16, ones16, route_w, route_e,
                         gu_d, da_d, db_d, x3_dram, xn_dram, slots_dram, y_dram, eid_dram, out_d)


def dense_layers(nc, dense, sb, sem, bank, ident, ident16, ones16, route_w, route_e,
                 x_d, ctx_d, ctxT_d, mq_d, mk_d, pad_d, wq_d, bq_d, wk_d, bk_d, wv_d, bv_d,
                 wo_d, bo_d, w1_d, w3_d, w2_d, rw_d, q_dram, k_dram, m_dram, padbias_dram,
                 x3_dram, xn_dram, slots_dram):

    def t(name, shape, dt, scope=dense):
        return sb(name, shape, dt, scope)

    wq16 = t("wq16", [P, 2, FT, DM], F16)
    wk16 = t("wk16", [P, 2, FT, KVW], F16)
    wv16 = t("wv16", [P, 2, FT, KVW], F16)
    wo16 = t("wo16", [P, 2, FT, DM], F16)
    rw16 = t("rw16", [P, 2, FT, EXPERTS], F16)
    w1t = t("w1t", [P, FT, HPAD], F16)
    w3t = t("w3t", [P, FT, HPAD], F16)
    w2t = t("w2t", [P, HT, DM], F16)
    half_s1 = t("half_s1", [P, 1], F32)
    ffn_scale = t("ffn_scale", [P, 1], F32)
    bq_col = t("bq_col", [P, FT], F32)
    bk_col = t("bk_col", [KVW, 1], F32)
    bv_row = t("bv_row", [P, KVW], F32)
    bo_row = t("bo_row", [P, DM], F32)
    mask_q = t("mask_q", [P, TT, SEQ], F16)
    mask_k = t("mask_k", [P, TT, SEQ], F16)
    neg_half = t("neg_half", [P, TT], F32)
    zeros = t("zeros", [P, ZERO_RUN], F16)

    with ExitStack() as prologue:
        prepare(nc, prologue, sb, sem, bank, ident, ident16, ones16, wq16, wk16, wv16, wo16, rw16, w1t, w3t,
                w2t, half_s1, ffn_scale, bq_col, bk_col, bv_row, bo_row, mask_q, mask_k, neg_half, zeros,
                mq_d, mk_d, pad_d, wq_d, bq_d, wk_d, bk_d, wv_d, bv_d, wo_d, bo_d, w1_d, w3_d, w2_d,
                rw_d, padbias_dram)

    xin = t("xin", [P, TT, DM], F32)
    xres = t("xres", [P, TT, DM], F32)
    xnf = t("xnf", [P, TT, DM], F32)
    xTf16 = t("xTf16", [P, 2, FT, SEQ], F16)
    ctxT_raw = t("ctxT_raw", [P, FT, SEQ], F32)
    ctxT16 = t("ctxT16", [P, 2, FT, SEQ], F16)
    q16 = t("q16", [P, 2, FT, SEQ], F16)
    k16 = t("k16", [KVW, 2, SEQ], F16)
    neg_max = t("neg_max", [P, 2 * TT, HEADS], F32)
    m_rest = t("m_rest", [TT * HEADS, P], F32)
    m16 = t("m16", [TT * HEADS, 3, P], F16)
    statsf = t("statsf", [P, TT, 6], F32)
    momentsf = t("momentsf", [P, TT, 2], F32)
    var_epsf = t("var_epsf", [P, TT], F32)
    rstdf = t("rstdf", [P, TT], F32)
    q_stack = t("q_stack", [ROWS_B, HEADS, SEQ], F16)
    k_stack = t("k_stack", [ROWS_B, GROUPS, SEQ], F16)
    v_ones = t("v_ones", [P, TT, GROUPS, 32], F32)
    ctx_raw = t("ctx_raw", [P, TT, DM], F32)
    ctx16 = t("ctx16", [P, 2, TT, DM], F16)
    ctxT_kept = t("ctxT_kept", [P, 2, FT, SEQ], F16)
    res = t("res", [P, TT, DM], F32)
    xn = t("xn", [P, TT, DM], F32)
    xT16 = t("xT16", [P, 2, FT, SEQ], F16)
    xs16 = t("xs16", [P, TT, 2, DM], F16)
    stats = t("stats", [P, TT, 6], F32)
    moments = t("moments", [P, TT, 2], F32)
    var_eps = t("var_eps", [P, TT], F32)
    rstd = t("rstd", [P, TT], F32)
    nothing = t("nothing", [1, 3], F32)
    eps_col = t("eps_col", [P, TT], F32)
    probs = t("probs", [P, 8, 1024], F32)
    attn_raw = t("attn_raw", [P, 2, HPG, SEQ], F32)
    inv_sum = t("inv_sum", [P, 4, HPG, 4], F32)
    shared = t("shared", [P, 6, 1024], F32)
    tanh_a = shared[:, 0, :].rearrange("p (a n) -> p a n", a=2)
    gate_b = shared[:, 1, :].rearrange("p (a n) -> p a n", a=2)
    g32 = shared[:, 2, :].rearrange("p (a n) -> p a n", a=2)
    g16 = shared[:, 3:6, :].rearrange("p a n -> p (a n)").bitcast(F16).rearrange(
        "p (s h n) -> p s h n", s=2, h=2 * HPAIRS)
    e32 = shared[:, 0:2, :].rearrange("p a n -> p (a n)").rearrange("p (e n) -> p e n", e=FT)
    p32 = shared[:, 2:4, :].rearrange("p a n -> p (a n)").rearrange("p (e n) -> p e n", e=FT)
    p16 = shared[:, 4:6, :].rearrange("p a n -> p (a n)").bitcast(F16).rearrange(
        "p (s e n) -> p s e n", s=2, e=FT)
    ch_neg = t("ch_neg", [P, FT], F32)
    ch_bias = t("ch_bias", [P, FT], F32)
    ch_sum = t("ch_sum", [P, FT], F32)
    ch_inv = t("ch_inv", [P, FT], F32)
    lg_neg = t("lg_neg", [P, TT], F32)
    lg_exp = t("lg_exp", [P, TT, EXPERTS], F32)
    lg_sum = t("lg_sum", [P, TT], F32)
    lg_inv = t("lg_inv", [P, TT], F32)
    lg_prob = t("lg_prob", [P, TT, EXPERTS], F32)
    top8 = t("top8", [P, TT, 8], F32)
    idx8 = t("idx8", [P, TT, 8], U32)
    top_sum = t("top_sum", [P, TT], F32)
    top_inv = t("top_inv", [P, TT], F32)

    names = ("x_loaded ctx_loaded ctxT_loaded k_stored k_stacked q_stored q_stacked m_stored m_stacked "
             "x3_stored xn_stored zeroed ctxT_hi ctxT_lo ctx_hi ctx_lo f_stats f_rstd xf_ready f_transposed "
             "f_hi f_lo v_ready q_ready q_hi k_split v_placed q_split biased a_ready a_reduced "
             "m_turned m_split stats_ready rstd_ready xn_ready transposed hi_ready lo_ready "
             "b_ready exp_done pv_done raw_kept o_turned o_ready wo_ready x1_ready "
             "up1_ready up3_ready tanh_ready g_ready g_hi g_lo down_ready rows_hi rows_lo s_ready max_ready "
             "e_ready p_ready p_hi p_lo ch_ready x3_ready logits_ready lmax_ready lexp_ready "
             "front_step dve_step poolf_step pool_step ones_set").split()
    s = {n: sem(n) for n in names}
    S_SCALE = float(np.float32(1.0) / np.sqrt(np.float32(DM)))
    LN2, LN3, LN4 = range(3)
    T_ATTN_OUT, T_FFN, T_ROUTER = range(3)
    UNITS_B, UNITS_A = 16, 32
    A_IN_FFN = {2: (2, 2), 3: (2, 2), 4: (3, 3), 5: (3, 3)}
    A_BEFORE_DOWN, A_AFTER_DOWN, A_AFTER_S = range(20, 24), range(24, 28), range(28, 32)
    DVE_FRONT_STEPS, DVE_BACK_STEPS, POOL_BACK_STEPS = 5, 28, 3

    def a_in_ffn(hp, place):
        first = sum(sum(n) for h, n in A_IN_FFN.items() if h < hp)
        here = A_IN_FFN.get(hp, (0, 0))
        first += here[0] * place
        return range(first, first + here[place])

    class Chain:

        def __init__(self, eng, sem_, per, b):
            self.eng, self.sem, self.per, self.b, self.n = eng, sem_, per, b, 0

        def then(self, ins, alone=False):
            self.n += 1
            ins.then_inc(self.sem, 1)
            if alone:
                wait_apart(self.eng, self.sem, self.b * self.per + self.n)
            else:
                self.eng.wait_ge(self.sem, self.b * self.per + self.n)

        def end(self):
            assert self.n == self.per, self.n

    def wait_apart(dve, semaphore, value):
        dve.wait_ge(semaphore, value)
        dve.memset(nothing[:, 0:1], 0.0)

    def all_steps(eng, front, step):
        front(0)
        with eng.Fori(0, BATCH - 1) as b:
            step(b, True)
        step(BATCH - 1, False)

    block = dense.enter_context(nc.Block())

    @block.sync
    def _(sp):
        def sp_wait(semaphore, value):
            value = sp.snap(value)
            sp.wait_ge(s["ones_set"], 5)
            sp.wait_ge(semaphore, value)

        def rows(dram, b):
            return pick(dram.rearrange("(b t p) c -> b p t c", b=BATCH, p=P), b)

        def load_x(b):
            sp.dma_start(xin[:], pick(x_d, b).rearrange("(t p) d -> p t d", p=P)).then_inc(s["x_loaded"], 16)

        def load_ctx(b):
            sp.dma_start(ctx_raw[:], pick(ctx_d, b).rearrange("(t p) d -> p t d", p=P)).then_inc(s["ctx_loaded"], 16)

        def load_ctxT(b):
            sp.dma_start(ctxT_raw[:], pick(ctxT_d, b).rearrange("(t p) k -> p t k", p=P)
                         ).then_inc(s["ctxT_loaded"], 16)

        def stack_keys_queries(c):
            sp.wait_ge(s["k_split"], c + 1)
            for part in (HI, LO):
                sp.dma_start(k_dram[part], k16[:, part, :]).then_inc(s["k_stored"], 16)
            sp.wait_ge(s["k_stored"], c * 32 + 32)
            for i, part in enumerate((HI, LO, HI, LO)):
                sp.dma_start(k_stack[i * HD:(i + 1) * HD],
                             k_dram[part].rearrange("(g d) k -> d g k", d=HD)).then_inc(s["k_stacked"], 16)
            sp.dma_start(k_stack[ROW_PAD:ROW_PAD + 1],
                         padbias_dram[bass.ds(c, 1)].unsqueeze(1).to_broadcast([1, GROUPS, SEQ])
                         ).then_inc(s["k_stacked"], 16)
            sp.wait_ge(s["q_split"], c * FT + FT)
            for part in (HI, LO):
                sp.dma_start(q_dram[part].rearrange("(t p) q -> p t q", p=P),
                             q16[:, part]).then_inc(s["q_stored"], 16)
            sp.wait_ge(s["q_stored"], c * 32 + 32)
            for i, part in enumerate((HI, HI, LO, LO)):
                sp.dma_start(q_stack[i * HD:(i + 1) * HD],
                             q_dram[part].rearrange("(h d) q -> d h q", d=HD)).then_inc(s["q_stacked"], 16)

        def stack_maxima(c):
            sp.wait_ge(s["m_split"], c + 1)
            sp.dma_start(m_dram.rearrange("i h q -> h i q"), m16[:]).then_inc(s["m_stored"], 16)
            sp.wait_ge(s["m_stored"], c * 16 + 16)
            for tt in range(TT):
                sp.dma_start(q_stack[ROW_MAX:ROW_MAX + 3, :, tt * P:(tt + 1) * P],
                             m_dram[:, tt * HEADS:(tt + 1) * HEADS, :]).then_inc(s["m_stacked"], 16)

        def front(c):
            stack_keys_queries(c)
            sp.wait_ge(s["ctxT_lo"], c + 1)
            load_ctxT(c + 1)
            sp.wait_ge(s["biased"], c + 1)
            sp.wait_ge(s["xf_ready"], 2 * c + 2)
            load_x(c + 1)
            stack_maxima(c)

        def step(b, front_too, load_next=True):
            c = b + 1
            if front_too:
                sp_wait(s["ctx_lo"], b + 1)
                load_ctx(c)
                if load_next:
                    sp_wait(s["ctxT_lo"], c + 1)
                    load_ctxT(c + 1)
            sp.dma_start(slots_dram.rearrange("s c -> (s c)").rearrange("(p n c) -> p n c", p=P, c=ZERO_RUN)[
                :, bass.ds(b * ZERO_RUNS, ZERO_RUNS), :],
                zeros[:, :].unsqueeze(1).to_broadcast([P, ZERO_RUNS, ZERO_RUN])).then_inc(s["zeroed"], 16)
            if front_too:
                stack_keys_queries(c)
                if load_next:
                    sp_wait(s["biased"], c + 1)
                    load_x(c + 1)
                stack_maxima(c)
            sp_wait(s["x3_ready"], b * 2 + 2)
            sp.dma_start(rows(x3_dram, b), res[:]).then_inc(s["x3_stored"], 16)
            sp.wait_ge(s["rows_hi"], b * 4 + 4)
            sp.wait_ge(s["rows_lo"], b * 4 + 4)
            sp.dma_start(rows(xn_dram, b), xs16[:].rearrange("p t s d -> p t (s d)")).then_inc(s["xn_stored"], 16)

        load_ctxT(0)
        load_x(0)
        load_ctx(0)
        sp.wait_ge(s["ones_set"], 5)
        front(0)
        with sp.Fori(0, BATCH - 2) as b:
            step(b, True)
        step(BATCH - 2, True, load_next=False)
        step(BATCH - 1, False)
        sp.wait_ge(s["zeroed"], BATCH * 16)
        sp.wait_ge(s["x3_stored"], BATCH * 16 + 16)
        sp.wait_ge(s["xn_stored"], BATCH * 16 + 16)

    @block.gpsimd
    def _(pool):
        def context_low(c):
            pool.wait_ge(s["ctxT_hi"], c + 1)
            pool.tensor_tensor(ctxT16[:, LO], ctxT_raw[:], ctxT16[:, HI], ALU.subtract).then_inc(s["ctxT_lo"], 1)

        def front_deviation(c):
            pool.wait_ge(s["f_stats"], c + 1)
            pool.tensor_tensor(var_epsf[:], momentsf[:, :, 1], eps_col[:], ALU.add).then_inc(s["poolf_step"], 1)
            pool.wait_ge(s["poolf_step"], c + 1)
            pool.tensor_tensor(rstdf[:], var_epsf[:], neg_half[:], ALU.pow).then_inc(s["f_rstd"], 1)

        def add_bias(c):
            pool.tensor_tensor(xres[:], xin[:], bo_row[:].unsqueeze(1).to_broadcast([P, TT, DM]),
                               ALU.add).then_inc(s["biased"], 1)

        def front(c):
            context_low(c)
            front_deviation(c)
            add_bias(c)

        def step(b, front_too):
            steps = Chain(pool, s["pool_step"], POOL_BACK_STEPS, b)

            def inverse_deviation(ln):
                pool.wait_ge(s["stats_ready"], b * 3 + ln + 1)
                steps.then(pool.tensor_tensor(var_eps[:], moments[:, :, 1], eps_col[:], ALU.add))
                pool.tensor_tensor(rstd[:], var_eps[:], neg_half[:], ALU.pow).then_inc(s["rstd_ready"], 1)

            if front_too:
                context_low(b + 1)
                front_deviation(b + 1)
            pool.wait_ge(s["ctx_hi"], b + 1)
            pool.tensor_tensor(ctx16[:, LO], ctx_raw[:], ctx16[:, HI], ALU.subtract).then_inc(s["ctx_lo"], 1)
            inverse_deviation(LN2)
            if front_too:
                add_bias(b + 1)
            for hp in range(HPAIRS):
                w = pair_width(hp)
                pool.wait_ge(s["g_hi"], b * HPAIRS + hp + 1)
                pool.tensor_tensor(g16[:, LO, 2 * hp:2 * hp + w // SEQ, :].rearrange("p h n -> p (h n)"),
                                   g32[:, hp % 2, 0:w],
                                   g16[:, HI, 2 * hp:2 * hp + w // SEQ, :].rearrange("p h n -> p (h n)"),
                                   ALU.subtract).then_inc(s["g_lo"], 1)
            for ln in (LN3, LN4):
                inverse_deviation(ln)
                for tt in range(TT):
                    n = TT * (ln - LN3) + tt + 1
                    pool.wait_ge(s["rows_hi"], b * 4 + n)
                    pool.tensor_tensor(xs16[:, tt, LO], xn[:, tt], xs16[:, tt, HI],
                                       ALU.subtract).then_inc(s["rows_lo"], 1)
                if ln == LN3:
                    for et in range(FT):
                        pool.wait_ge(s["p_hi"], b * FT + et + 1)
                        pool.tensor_tensor(p16[:, LO, et], p32[:, et], p16[:, HI, et],
                                           ALU.subtract).then_inc(s["p_lo"], 1)
            steps.end()

        pool.wait_ge(s["ones_set"], 5)
        all_steps(pool, front, step)

    @block.scalar
    def _(act):
        def front_high(c):
            for i in range(2):
                act.wait_ge(s["f_transposed"], c * 2 + i + 1)
                act.copy(xTf16[:, HI, 2 * i:2 * i + 2, :].rearrange("p t n -> p (t n)"),
                         bank[:, 7 - i, :]).then_inc(s["f_hi"], 1)

        def queries_high(c, hts):
            for ht in hts:
                act.wait_ge(s["q_ready"], c * FT + ht // 2 * 2 + 2)
                act.activation(q16[:, HI, ht], bank[:, 7 - ht // 2, (ht % 2) * SEQ:(ht % 2 + 1) * SEQ],
                               ACT.Identity, bias=bq_col[:, ht:ht + 1]).then_inc(s["q_hi"], 1)

        def front(c):
            front_high(c)
            queries_high(c, range(FT))

        def step(b, front_too):
            def high_part(which, first_bank):
                for i in range(2):
                    act.wait_ge(s["transposed"], b * 6 + 2 * which + i + 1)
                    act.copy(xT16[:, HI, 2 * i:2 * i + 2, :].rearrange("p t n -> p (t n)"),
                             bank[:, first_bank + i, :]).then_inc(s["hi_ready"], 1)

            for u in range(UNITS_B):
                if u >= 8:
                    act.wait_ge(s["pv_done"], b * 4 + (u - 8) // 4 + 1)
                act.wait_ge(s["b_ready"], b * UNITS_B + u + 1)
                act.activation(probs[:, u % 8], bank[:, 2 * (u % 2):2 * (u % 2) + 2, :].rearrange("p a n -> p (a n)"),
                               ACT.Exp, scale=1.0 / 4.0).then_inc(s["exp_done"], 1)
                if u in (10, UNITS_B - 1):
                    gg = 0 if u == 10 else 1
                    act.wait_ge(s["pv_done"], b * 4 + 2 * gg + 2)
                    act.copy(attn_raw[:, gg].rearrange("p r n -> p (r n)"),
                             bank[:, 4:6, :].rearrange("p a n -> p (a n)")).then_inc(s["raw_kept"], 1)
            if front_too:
                front_high(b + 1)
            high_part(T_ATTN_OUT, 4)
            if front_too:
                queries_high(b + 1, range(FT))
            high_part(T_FFN, 2)
            for hp in range(HPAIRS + 1):
                if hp < HPAIRS:
                    w = pair_width(hp)
                    act.wait_ge(s["up1_ready"], b * HPAIRS + hp + 1)
                    if hp >= 2:
                        act.wait_ge(s["g_ready"], b * HPAIRS + hp - 1)
                    act.activation(tanh_a[:, hp % 2, 0:w], bank[:, 2 * (hp % 2), 0:w], ACT.Tanh,
                                   scale=half_s1[:, 0:1]).then_inc(s["tanh_ready"], 1)
                if hp >= 1:
                    j = hp - 1
                    w = pair_width(j)
                    act.wait_ge(s["g_ready"], b * HPAIRS + j + 1)
                    act.copy(g16[:, HI, 2 * j:2 * j + w // SEQ, :].rearrange("p h n -> p (h n)"),
                             g32[:, j % 2, 0:w]).then_inc(s["g_hi"], 1)

            def rows_high(ln):
                for tt in range(TT):
                    act.wait_ge(s["xn_ready"], b * 6 + 2 * ln + tt + 1)
                    act.copy(xs16[:, tt, HI], xn[:, tt]).then_inc(s["rows_hi"], 1)

            act.wait_ge(s["xn_stored"], b * 16 + 16)
            rows_high(LN3)
            for et in range(FT):
                act.wait_ge(s["max_ready"], b * FT + et + 1)
                act.activation(e32[:, et], bank[:, et, :], ACT.Exp, bias=ch_bias[:, et:et + 1], scale=S_SCALE,
                               accum_out=ch_sum[:, et:et + 1]).then_inc(s["e_ready"], 1)
            for et in range(FT):
                act.wait_ge(s["p_ready"], b * FT + et + 1)
                act.copy(p16[:, HI, et], p32[:, et]).then_inc(s["p_hi"], 1)
            rows_high(LN4)
            high_part(T_ROUTER, 0)
            act.wait_ge(s["lmax_ready"], b + 1)
            for tt in range(TT):
                act.activation(lg_exp[:, tt], bank[:, 4, tt * EXPERTS:(tt + 1) * EXPERTS], ACT.Exp,
                               bias=lg_neg[:, tt:tt + 1],
                               accum_out=lg_sum[:, tt:tt + 1]).then_inc(s["lexp_ready"], 1)

        all_steps(act, front, step)

    @block.tensor
    def _(pe):
        def three(out, left, right, n):
            for i in range(n):
                for j, (lp, rp) in enumerate(PASSES):
                    last = pe.matmul(out, left(lp, i), right(rp, i), start=(i == 0 and j == 0),
                                     stop=(i == n - 1 and j == 2))
            return last

        def turn(src, banks, signal, before=()):
            for ft in range(FT):
                if ft == 2:
                    for semaphore, value in before:
                        pe.wait_ge(semaphore, value)
                for tt in range(TT):
                    last = pe.transpose(
                        bank[:, banks[ft // 2], (ft % 2) * SEQ + tt * P:(ft % 2) * SEQ + (tt + 1) * P],
                        src[:, tt, ft * P:(ft + 1) * P], ident[:])
                if ft % 2 == 1:
                    last.then_inc(s[signal], 1)

        def keys_values(c):
            pe.wait_ge(s["ctxT_hi"], c + 1)
            pe.wait_ge(s["ctxT_lo"], c + 1)
            three(bank[0:KVW, 6, 0:SEQ], lambda p, i: wk16[:, p, i, :], lambda p, i: ctxT16[:, p, i, :],
                  FT)
            for kt in range(TT):
                last = three(bank[:, 6, SEQ + kt * KVW:SEQ + (kt + 1) * KVW],
                             lambda p, i: ctxT16[:, p, i, kt * P:(kt + 1) * P],
                             lambda p, i: wv16[:, p, i, :], FT)
            last.then_inc(s["v_ready"], 1)

        def turn_front(c):
            pe.wait_ge(s["xf_ready"], c * 2 + 2)
            turn(xnf, (7, 6), "f_transposed", before=((s["k_split"], c + 1), (s["v_placed"], c + 1)))

        def queries(c, hts):
            pe.wait_ge(s["f_lo"], c * 2 + 2)
            for ht in hts:
                three(bank[:, 7 - ht // 2, (ht % 2) * SEQ:(ht % 2 + 1) * SEQ],
                      lambda p, i: wq16[:, p, i, ht * P:(ht + 1) * P],
                      lambda p, i: xTf16[:, p, i, :], FT).then_inc(s["q_ready"], 1)

        def stacked(c):
            pe.wait_ge(s["k_stacked"], c * 80 + 80)
            pe.wait_ge(s["q_stacked"], c * 64 + 64)

        def scores_a(c, units):
            for u in units:
                g, half, qt = u // 4, u // 2 % 2, u % 2
                if u >= 2:
                    pe.wait_ge(s["a_reduced"], c * UNITS_A + u - 1)
                out = bank[:, 6 + u % 2, :]
                pe.matmul(out.rearrange("p (a n) -> p a n", a=2), ident16[:],
                          mask_q[:, qt, :].unsqueeze(1).to_broadcast([P, 2, SEQ]), start=True, stop=True)
                for r in range(2):
                    h = HPG * g + 2 * half + r
                    last = pe.matmul(out[:, r * SEQ:(r + 1) * SEQ],
                                     q_stack[0:ROWS_A, h, qt * P:(qt + 1) * P],
                                     k_stack[0:ROWS_A, g, :], start=False, stop=True,
                                     skip_group_check=True)
                last.then_inc(s["a_ready"], 1)

        def turn_maxima(c):
            pe.wait_ge(s["a_reduced"], c * UNITS_A + UNITS_A)
            pe.transpose(bank[:, 6, 0:P], neg_max[:].rearrange("p t h -> p (t h)"),
                         ident[:]).then_inc(s["m_turned"], 1)

        def front(c):
            keys_values(c)
            turn_front(c)
            queries(c, range(FT))
            stacked(c)
            scores_a(c, range(UNITS_A))
            turn_maxima(c)

        def step(b, front_too):
            c = b + 1

            def scores_b(u):
                gg, kt, j = u // 8, u // 4 % 2, u % 4
                g = 4 * gg + j
                if u >= 2:
                    pe.wait_ge(s["exp_done"], b * UNITS_B + u - 1)
                for half in range(2):
                    out = bank[:, 2 * (u % 2) + half, :]
                    pe.matmul(out.rearrange("p (a n) -> p a n", a=2), ident16[:],
                              mask_k[:, kt, :].unsqueeze(1).to_broadcast([P, 2, SEQ]), start=True, stop=True)
                    h = HPG * g + 2 * half
                    last = pe.matmul(out, k_stack[0:ROWS_B, g, kt * P:(kt + 1) * P],
                                     q_stack[0:ROWS_B, h:h + 2, :].rearrange("k h q -> k (h q)"),
                                     start=False, stop=True, skip_group_check=True)
                last.then_inc(s["b_ready"], 1)

            def pv(quartet):
                gg, kt = quartet // 2, quartet % 2
                pe.wait_ge(s["exp_done"], b * UNITS_B + 4 * quartet + 4)
                if quartet == 2:
                    pe.wait_ge(s["raw_kept"], b * 2 + 1)
                for half in range(2):
                    for j in range(4):
                        last = pe.matmul(bank[32 * j:32 * j + 32, 4 + half, :], v_ones[:, kt, 4 * gg + j, :],
                                         probs[:, 4 * (quartet % 2) + j, half * 512:(half + 1) * 512],
                                         start=(kt == 0), stop=(kt == TT - 1), tile_position=(0, 32 * j))
                last.then_inc(s["pv_done"], 1)

            pe.wait_ge(s["m_stacked"], b * 32 + 32)
            for u in range(UNITS_B):
                scores_b(u)
                if u in (5, 9, 13):
                    pv((u - 5) // 4)
            pv(3)
            if front_too:
                keys_values(c)
            pe.wait_ge(s["raw_kept"], b * 2 + 2)
            for qt in range(TT):
                for gg in range(2):
                    for r in range(HPG):
                        last = pe.transpose(bank[:, 2 * qt + gg, r * P:(r + 1) * P],
                                            attn_raw[:, gg, r, qt * P:(qt + 1) * P], ident[:])
                    last.then_inc(s["o_turned"], 1)
            if front_too:
                turn_front(c)
            pe.wait_ge(s["o_ready"], b * 4 + 4)
            turn(xn, (4, 5), "transposed")
            if front_too:
                queries(c, (0, 1))
            pe.wait_ge(s["lo_ready"], b * 6 + 2)
            for tt in range(TT):
                three(bank[:, tt, :], lambda p, i: xT16[:, p, i, tt * P:(tt + 1) * P],
                      lambda p, i: wo16[:, p, i, :], FT).then_inc(s["wo_ready"], 1)
            if front_too:
                queries(c, (2, 3))
            pe.wait_ge(s["xn_ready"], b * 6 + 2)
            turn(xn, (2, 3), "transposed")
            pe.wait_ge(s["lo_ready"], b * 6 + 4)
            for hp in range(HPAIRS):
                if hp >= 2:
                    pe.wait_ge(s["g_ready"], b * HPAIRS + hp - 1)
                if hp == 2 and front_too:
                    stacked(c)
                for which, (w, signal) in enumerate(((w1t, "up1_ready"), (w3t, "up3_ready"))):
                    for a in range(pair_width(hp) // SEQ):
                        h0 = (2 * hp + a) * P
                        for ft in range(FT):
                            for part in (HI, LO):
                                last = pe.matmul(bank[:, 2 * (hp % 2) + which, a * SEQ:(a + 1) * SEQ],
                                                 w[:, ft, h0:h0 + P], xT16[:, part, ft, :],
                                                 start=(ft == 0 and part == HI), stop=(ft == FT - 1 and part == LO))
                    last.then_inc(s[signal], 1)
                    if front_too:
                        scores_a(c, a_in_ffn(hp, which))
            if front_too:
                scores_a(c, A_BEFORE_DOWN)
            pe.wait_ge(s["g_lo"], b * HPAIRS + HPAIRS)
            for tt in range(TT):
                for ht in range(HT):
                    for part in (HI, LO):
                        last = pe.matmul(bank[:, 4 + tt, :], g16[:, part, ht, tt * P:(tt + 1) * P], w2t[:, ht, :],
                                         start=(ht == 0 and part == HI), stop=(ht == HT - 1 and part == LO))
                last.then_inc(s["down_ready"], 1)
            if front_too:
                scores_a(c, A_AFTER_DOWN)
            pe.wait_ge(s["rows_lo"], b * 4 + 2)
            pe.wait_ge(s["ctx_lo"], b + 1)
            for et in range(FT):
                three(bank[:, et, :], lambda p, i: ctx16[:, p, i, et * P:(et + 1) * P],
                      lambda p, i: xs16[:, i, p, :], TT).then_inc(s["s_ready"], 1)
            if front_too:
                scores_a(c, A_AFTER_S)
            for et in range(FT):
                pe.wait_ge(s["p_lo"], b * FT + et + 1)
                for tt in range(TT):
                    for j, (lp, rp) in enumerate(PASSES):
                        last = pe.matmul(bank[:, 4 + tt, :], ctxT_kept[:, lp, et, tt * P:(tt + 1) * P],
                                         p16[:, rp, et, :], start=(et == 0 and j == 0),
                                         stop=(et == FT - 1 and j == 2))
                    if et == FT - 1:
                        last.then_inc(s["ch_ready"], 1)
                if et == 1 and front_too:
                    turn_maxima(c)
            pe.wait_ge(s["xn_ready"], b * 6 + 6)
            turn(xn, (0, 1), "transposed")
            pe.wait_ge(s["lo_ready"], b * 6 + 6)
            for tt in range(TT):
                last = three(bank[:, 4, tt * EXPERTS:(tt + 1) * EXPERTS],
                             lambda p, i: xT16[:, p, i, tt * P:(tt + 1) * P], lambda p, i: rw16[:, p, i, :], FT)
            last.then_inc(s["logits_ready"], 1)

        all_steps(pe, front, step)

    @block.vector
    def _(dve):
        def context_high(c):
            dve.wait_ge(s["ctxT_loaded"], c * 16 + 16)
            dve.tensor_copy(ctxT16[:, HI], ctxT_raw[:]).then_inc(s["ctxT_hi"], 1)

        def front_norm(c, steps):
            dve.wait_ge(s["x_loaded"], c * 16 + 16)
            for tt in range(TT):
                ins = dve.bn_stats(statsf[:, tt], xin[:, tt])
            steps.then(ins, alone=True)
            for tt in range(TT):
                ins = dve.bn_aggr(momentsf[:, tt], statsf[:, tt])
            ins.then_inc(s["f_stats"], 1)
            dve.wait_ge(s["f_rstd"], c + 1)
            for tt in range(TT):
                dve.tensor_scalar(xnf[:, tt], xin[:, tt], momentsf[:, tt, 0:1], rstdf[:, tt:tt + 1],
                                  ALU.subtract, ALU.mult).then_inc(s["xf_ready"], 1)

        def place_keys_values(c, steps):
            dve.wait_ge(s["v_ready"], c + 1)
            steps.then(dve.tensor_scalar(k16[:, HI], bank[0:KVW, 6, 0:SEQ], bk_col[:, 0:1], None, ALU.add))
            dve.scalar_tensor_tensor(out=k16[:, LO], in0=bank[0:KVW, 6, 0:SEQ], scalar=bk_col[:, 0:1],
                                     in1=k16[:, HI], op0=ALU.add, op1=ALU.subtract).then_inc(s["k_split"], 1)
            for kt in range(TT):
                ins = dve.tensor_tensor(v_ones[:, kt, :, 0:HD],
                                        bank[:, 6, SEQ + kt * KVW:SEQ + (kt + 1) * KVW].rearrange(
                                            "p (g d) -> p g d", d=HD),
                                        bv_row[:].rearrange("p (g d) -> p g d", d=HD), ALU.add)
            ins.then_inc(s["v_placed"], 1)

        def front_low(c):
            for i in range(2):
                dve.wait_ge(s["f_hi"], c * 2 + i + 1)
                dve.tensor_tensor(xTf16[:, LO, 2 * i:2 * i + 2, :].rearrange("p t n -> p (t n)"),
                                  bank[:, 7 - i, :],
                                  xTf16[:, HI, 2 * i:2 * i + 2, :].rearrange("p t n -> p (t n)"),
                                  ALU.subtract).then_inc(s["f_lo"], 1)

        def queries_low(c, hts):
            for ht in hts:
                dve.wait_ge(s["q_hi"], c * FT + ht // 2 * 2 + 2)
                dve.scalar_tensor_tensor(out=q16[:, LO, ht],
                                         in0=bank[:, 7 - ht // 2, (ht % 2) * SEQ:(ht % 2 + 1) * SEQ],
                                         scalar=bq_col[:, ht:ht + 1], in1=q16[:, HI, ht], op0=ALU.add,
                                         op1=ALU.subtract).then_inc(s["q_split"], 1)

        def reduce_a(c, units):
            for u in units:
                g, half, qt = u // 4, u // 2 % 2, u % 2
                h = HPG * g + 2 * half
                dve.wait_ge(s["a_ready"], c * UNITS_A + u + 1)
                dve.tensor_reduce(neg_max[:, qt, h:h + 2], bank[:, 6 + u % 2, :].rearrange("p (r n) -> p r n", r=2),
                                  AX.X, ALU.max, negate=True).then_inc(s["a_reduced"], 1)

        def split_maxima(c, steps):
            dve.wait_ge(s["m_turned"], c + 1)
            turned = bank[0:TT * HEADS, 6, 0:P]
            steps.then(dve.tensor_copy(m16[:, 0], turned))
            steps.then(dve.tensor_tensor(m_rest[:], turned, m16[:, 0], ALU.subtract))
            steps.then(dve.tensor_copy(m16[:, 1], m_rest[:]))
            dve.tensor_tensor(m16[:, 2], m_rest[:], m16[:, 1], ALU.subtract).then_inc(s["m_split"], 1)

        def front(c):
            steps = Chain(dve, s["front_step"], DVE_FRONT_STEPS, c)
            context_high(c)
            front_norm(c, steps)
            place_keys_values(c, steps)
            front_low(c)
            queries_low(c, range(FT))
            reduce_a(c, range(UNITS_A))
            split_maxima(c, steps)
            steps.end()

        def step(b, front_too):
            c = b + 1
            front_steps = Chain(dve, s["front_step"], DVE_FRONT_STEPS, c)
            steps = Chain(dve, s["dve_step"], DVE_BACK_STEPS, b)

            def layer_norm(ln, fill=None):
                for tt in range(TT):
                    ins = dve.bn_stats(stats[:, tt], res[:, tt])
                steps.then(ins, alone=True)
                for tt in range(TT):
                    ins = dve.bn_aggr(moments[:, tt], stats[:, tt])
                ins.then_inc(s["stats_ready"], 1)
                if fill:
                    fill()
                dve.wait_ge(s["rstd_ready"], b * 3 + ln + 1)
                for tt in range(TT):
                    dve.tensor_scalar(xn[:, tt], res[:, tt], moments[:, tt, 0:1], rstd[:, tt:tt + 1],
                                      ALU.subtract, ALU.mult).then_inc(s["xn_ready"], 1)

            def low_part(which, first_bank):
                for i in range(2):
                    dve.wait_ge(s["hi_ready"], b * 6 + 2 * which + i + 1)
                    dve.tensor_tensor(xT16[:, LO, 2 * i:2 * i + 2, :].rearrange("p t n -> p (t n)"),
                                      bank[:, first_bank + i, :],
                                      xT16[:, HI, 2 * i:2 * i + 2, :].rearrange("p t n -> p (t n)"),
                                      ALU.subtract).then_inc(s["lo_ready"], 1)

            steps.then(dve.tensor_copy(ctxT_kept[:], ctxT16[:]))
            if front_too:
                context_high(c)
            dve.wait_ge(s["ctx_loaded"], b * 16 + 16)
            dve.tensor_copy(ctx16[:, HI], ctx_raw[:]).then_inc(s["ctx_hi"], 1)
            if front_too:
                front_norm(c, front_steps)
                place_keys_values(c, front_steps)
            for i in range(4):
                qt, gg = i // 2, i % 2
                dve.wait_ge(s["o_turned"], b * 4 + i + 1)
                ps = bank[:, i, :].rearrange("p (r j e) -> p r j e", r=HPG, j=4)
                steps.then(dve.reciprocal(inv_sum[:, i], ps[:, :, :, HD]))
                dve.tensor_tensor(xn[:, qt, gg * SEQ:(gg + 1) * SEQ].rearrange("p (j r d) -> p r j d", j=4, r=HPG),
                                  ps[:, :, :, 0:HD],
                                  inv_sum[:, i].unsqueeze(3).to_broadcast([P, HPG, 4, HD]),
                                  ALU.mult).then_inc(s["o_ready"], 1)
            if front_too:
                front_low(c)
            low_part(T_ATTN_OUT, 4)
            if front_too:
                queries_low(c, (0, 1))
            dve.wait_ge(s["biased"], b + 1)
            dve.wait_ge(s["x3_stored"], b * 16 + 16)
            for tt in range(TT):
                dve.wait_ge(s["wo_ready"], b * 2 + tt + 1)
                dve.tensor_tensor(res[:, tt], bank[:, tt, :], xres[:, tt], ALU.add).then_inc(s["x1_ready"], 1)
            dve.wait_ge(s["x1_ready"], b * 2 + 2)
            layer_norm(LN2)
            if front_too:
                queries_low(c, (2, 3))
            low_part(T_FFN, 2)
            for hp in range(HPAIRS):
                w = pair_width(hp)
                if front_too:
                    reduce_a(c, a_in_ffn(hp, 0))
                dve.wait_ge(s["tanh_ready"], b * HPAIRS + hp + 1)
                dve.wait_ge(s["up3_ready"], b * HPAIRS + hp + 1)
                steps.then(dve.scalar_tensor_tensor(out=gate_b[:, hp % 2, 0:w], in0=tanh_a[:, hp % 2, 0:w],
                                                    scalar=1.0, in1=bank[:, 2 * (hp % 2) + 1, 0:w], op0=ALU.add,
                                                    op1=ALU.mult))
                if hp >= 2:
                    dve.wait_ge(s["g_lo"], b * HPAIRS + hp - 1)
                dve.scalar_tensor_tensor(out=g32[:, hp % 2, 0:w], in0=gate_b[:, hp % 2, 0:w], scalar=G_SCALE,
                                         in1=bank[:, 2 * (hp % 2), 0:w], op0=ALU.mult,
                                         op1=ALU.mult).then_inc(s["g_ready"], 1)
                if front_too:
                    reduce_a(c, a_in_ffn(hp, 1))
            if front_too:
                reduce_a(c, A_BEFORE_DOWN)
            for tt in range(TT):
                dve.wait_ge(s["down_ready"], b * 2 + tt + 1)
                ins = dve.scalar_tensor_tensor(out=res[:, tt], in0=bank[:, 4 + tt, :], scalar=ffn_scale[:, 0:1],
                                               in1=res[:, tt], op0=ALU.mult, op1=ALU.add)
            steps.then(ins)
            layer_norm(LN3, fill=(lambda: reduce_a(c, A_AFTER_DOWN[:2])) if front_too else None)
            if front_too:
                reduce_a(c, A_AFTER_DOWN[2:])
            for et in range(FT):
                dve.wait_ge(s["s_ready"], b * FT + et + 1)
                steps.then(dve.tensor_reduce(ch_neg[:, et:et + 1], bank[:, et, :], AX.X, ALU.max, negate=True))
                dve.tensor_scalar(ch_bias[:, et:et + 1], ch_neg[:, et:et + 1], S_SCALE, None,
                                  ALU.mult).then_inc(s["max_ready"], 1)
            if front_too:
                reduce_a(c, A_AFTER_S[:2])
            for et in range(FT):
                dve.wait_ge(s["e_ready"], b * FT + et + 1)
                steps.then(dve.reciprocal(ch_inv[:, et:et + 1], ch_sum[:, et:et + 1]))
                dve.tensor_scalar(p32[:, et], e32[:, et], ch_inv[:, et:et + 1], P_SCALE, ALU.mult,
                                  ALU.mult).then_inc(s["p_ready"], 1)
            if front_too:
                reduce_a(c, A_AFTER_S[2:])
                split_maxima(c, front_steps)
                front_steps.end()
            for tt in range(TT):
                dve.wait_ge(s["ch_ready"], b * 2 + tt + 1)
                dve.scalar_tensor_tensor(out=res[:, tt], in0=bank[:, 4 + tt, :], scalar=1.0 / P_SCALE,
                                         in1=res[:, tt], op0=ALU.mult, op1=ALU.add).then_inc(s["x3_ready"], 1)
            dve.wait_ge(s["x3_ready"], b * 2 + 2)
            layer_norm(LN4)
            low_part(T_ROUTER, 0)
            dve.wait_ge(s["logits_ready"], b + 1)
            dve.tensor_reduce(lg_neg[:], bank[:, 4, 0:TT * EXPERTS].rearrange("p (t e) -> p t e", t=TT), AX.X,
                              ALU.max, negate=True).then_inc(s["lmax_ready"], 1)
            dve.wait_ge(s["lexp_ready"], b * 2 + 2)
            steps.then(dve.reciprocal(lg_inv[:], lg_sum[:]))
            for tt in range(TT):
                ins = dve.tensor_scalar(lg_prob[:, tt], lg_exp[:, tt], lg_inv[:, tt:tt + 1], None, ALU.mult)
            steps.then(ins, alone=True)
            for tt in range(TT):
                ins = dve.max(top8[:, tt], lg_prob[:, tt])
            steps.then(ins, alone=True)
            for tt in range(TT):
                dve.max_index(idx8[:, tt], top8[:, tt], lg_prob[:, tt])
            steps.then(dve.tensor_reduce(top_sum[:], top8[:, :, 0:TOPK], AX.X, ALU.add))
            steps.then(dve.reciprocal(top_inv[:], top_sum[:]))
            dve.wait_ge(s["rows_lo"], b * 4 + 4)
            dve.tensor_copy(route_e[:, bass.ds(b * TT, TT), :], idx8[:, :, 0:TOPK])
            dve.tensor_tensor(route_w[:, bass.ds(b * TT, TT), :], top8[:, :, 0:TOPK],
                              top_inv[:].unsqueeze(2).to_broadcast([P, TT, TOPK]), ALU.mult)
            steps.end()

        dve.memset(q_stack[ROW_PAD:ROWS_B], 1.0).then_inc(s["ones_set"], 1)
        dve.memset(k_stack[ROW_PAD:ROWS_B], 1.0).then_inc(s["ones_set"], 1)
        dve.memset(eps_col[:], EPS).then_inc(s["ones_set"], 1)
        dve.memset(neg_max[:], 0.0).then_inc(s["ones_set"], 1)
        dve.memset(v_ones[:], 1.0).then_inc(s["ones_set"], 1)
        dve.wait_ge(s["ones_set"], 5)
        dve.memset(nothing[:, 1:2], 0.0).then_inc(s["x3_stored"], 16)
        dve.memset(nothing[:, 2:3], 0.0).then_inc(s["xn_stored"], 16)
        all_steps(dve, front, step)


def prepare(nc, scope, sb, sem, bank, ident, ident16, ones16, wq16, wk16, wv16, wo16, rw16, w1t, w3t, w2t,
            half_s1, ffn_scale, bq_col, bk_col, bv_row, bo_row, mask_q, mask_k, neg_half, zeros,
            mq_d, mk_d, pad_d, wq_d, bq_d, wk_d, bk_d, wv_d, bv_d, wo_d, bo_d, w1_d, w3_d, w2_d, rw_d,
            padbias_dram):

    def t(name, shape, dt):
        return sb(name, shape, dt, scope)

    split = [(wk_d, wk16, KVW), (wv_d, wv16, KVW), (wq_d, wq16, DM), (wo_d, wo16, DM), (rw_d, rw16, EXPERTS)]
    raw = [t(f"raw{i}", [P, FT, n], F32) for i, (_, _, n) in enumerate(split)]
    w1_raw = t("w1_raw", [P, FT, HIDDEN], F32)
    w3_raw = t("w3_raw", [P, FT, HIDDEN], F32)
    w2_raw = t("w2_raw", [P, HT, DM], F32)
    below = t("below", [P, HT * DM], F16)
    mq_raw = t("mq_raw", [P, TT, SEQ // 4], I32)
    mk_raw = t("mk_raw", [P, TT, SEQ // 4], I32)
    pad_raw = t("pad_raw", [BATCH, SEQ // 4], I32)
    pad16 = t("pad16", [BATCH, SEQ], F16)
    ones32 = t("ones32", [P, P], F32)
    part_sums = t("part_sums", [P, 3, 140], F32)
    sums = t("sums", [P, 3], F32)
    scales = t("scales", [P, 3], F32)
    thresholds = t("thresholds", [P, 3, 2], F32)
    s12 = t("s12", [P, 1], F32)
    ws_loaded, small_loaded = sem("ws_loaded"), sem("small_loaded")
    ternary_loaded = [sem(f"ternary_loaded{i}") for i in range(3)]
    w_hi, pool_made, w2_zeroed = sem("w_hi"), sem("pool_made"), sem("w2_zeroed")
    sums_made, totals_made, pre_step, pad_stored = sem("sums_made"), sem("totals_made"), sem("pre_step"), sem("pad_stored")
    pad_made = sem("pad_made")
    TAIL = HIDDEN - (HT - 1) * P
    with nc.Block() as block:
        @block.sync
        def _(sp):
            sp.wait_ge(w2_zeroed, 1)
            sp.dma_start(w2_raw[:, 0:HT - 1, :],
                         w2_d[0:(HT - 1) * P].rearrange("(t p) d -> p t d", p=P)).then_inc(ternary_loaded[2], 16)
            sp.dma_start(w2_raw[0:TAIL, HT - 1, :], w2_d[(HT - 1) * P:HIDDEN]).then_inc(ternary_loaded[2], 16)
            sp.dma_start(w3_raw[:], w3_d).then_inc(ternary_loaded[1], 16)
            sp.wait_ge(pad_made, 1)
            sp.dma_start(padbias_dram, pad16[:]).then_inc(pad_stored, 16)
            sp.wait_ge(pad_stored, 16)

        @block.scalar
        def _(act):
            act.dma_start(w1_raw[:], w1_d).then_inc(ternary_loaded[0], 16)
            for i, (src, _, _) in enumerate(split):
                act.dma_start(raw[i][:], src).then_inc(ws_loaded, 16)
            act.wait_ge(ws_loaded, 16 * len(split))
            for i, (_, dst, _) in enumerate(split):
                act.copy(dst[:, HI], raw[i][:]).then_inc(w_hi, 1)

        @block.gpsimd
        def _(pool):
            pool.memset(ident[:], 0.0)
            pool.memset(ident16[:], 0.0)
            pool.memset(zeros[:], 0.0)
            pool.memset(neg_half[:], -0.5).then_inc(pool_made, 1)
            pool.dma_start(mq_raw[:], mq_d).then_inc(small_loaded, 16)
            pool.dma_start(mk_raw[:], mk_d).then_inc(small_loaded, 16)
            pool.dma_start(pad_raw[:], pad_d).then_inc(small_loaded, 16)
            pool.dma_start(bq_col[:], bq_d).then_inc(small_loaded, 16)
            pool.dma_start(bk_col[:], bk_d).then_inc(small_loaded, 16)
            pool.dma_start(bv_row[:], bv_d.to_broadcast([P, KVW])).then_inc(small_loaded, 16)
            pool.dma_start(bo_row[:], bo_d.to_broadcast([P, DM])).then_inc(small_loaded, 16)
            pool.wait_ge(pool_made, 1)
            for m in (ident, ident16):
                pool.affine_select(out=m[:], in_=m[:], compare_op=ALU.not_equal, fill=1.0, base=0,
                                   pattern=[[-1, P]], channel_multiplier=1).then_inc(pool_made, 1)
            for i, (_, dst, _) in enumerate(split):
                pool.wait_ge(w_hi, i + 1)
                pool.tensor_tensor(dst[:, LO], raw[i][:], dst[:, HI], ALU.subtract)

        @block.tensor
        def _(pe):
            pe.wait_ge(sums_made, 4)
            pe.matmul(bank[:, 0, 0:3], ones32[:], sums[:], start=True, stop=True).then_inc(totals_made, 1)

        @block.vector
        def _(dve):
            count = [0]

            def step(ins):
                count[0] += 1
                ins.then_inc(pre_step, 1)
                dve.wait_ge(pre_step, count[0])

            step(dve.memset(w2_raw[64:P, HT - 1, :], 0.0))
            dve.memset(w2_raw[0:64, HT - 1, :], 0.0).then_inc(w2_zeroed, 1)
            dve.memset(w1t[:, :, HIDDEN:HPAD], 0.0)
            dve.memset(w3t[:, :, HIDDEN:HPAD], 0.0)
            dve.memset(ones16[:], 1.0)
            dve.memset(ones32[:], 1.0).then_inc(sums_made, 1)
            dve.wait_ge(small_loaded, 7 * 16)
            dve.tensor_scalar(mask_q[:], mq_raw[:].bitcast(U8), MASKED, None, ALU.mult)
            dve.tensor_scalar(mask_k[:], mk_raw[:].bitcast(U8), MASKED, None, ALU.mult)
            dve.tensor_scalar(pad16[:], pad_raw[:].bitcast(U8), MASKED, None, ALU.mult).then_inc(pad_made, 1)
            flat = [w1_raw[:].rearrange("p t n -> p (t n)"), w3_raw[:].rearrange("p t n -> p (t n)"),
                    w2_raw[:].rearrange("p t n -> p (t n)")]
            chunks = [FT * HIDDEN // 140, FT * HIDDEN // 140, 44]
            for i in range(3):
                dve.wait_ge(ternary_loaded[i], 32 if i == 2 else 16)
                n = flat[i].shape[1] // chunks[i]
                step(dve.tensor_reduce(part_sums[:, i, 0:n], flat[i].rearrange("p (n c) -> p n c", c=chunks[i]),
                                       AX.X, ALU.add, apply_absolute_value=True))
                dve.tensor_reduce(sums[:, i:i + 1], part_sums[:, i, 0:n], AX.X, ALU.add).then_inc(sums_made, 1)
            dve.wait_ge(totals_made, 1)
            step(dve.tensor_scalar(scales[:], bank[:, 0, 0:3], 1.0 / (HIDDEN * DM), None, ALU.mult))
            dve.tensor_scalar(thresholds[:, :, 0], scales[:], 0.5, None, ALU.mult)
            dve.tensor_scalar(thresholds[:, :, 1], scales[:], -0.5, None, ALU.mult)
            dve.tensor_scalar(half_s1[:], scales[:, 0:1], 0.5, None, ALU.mult)
            step(dve.tensor_tensor(s12[:], scales[:, 0:1], scales[:, 1:2], ALU.mult))
            step(dve.scalar_tensor_tensor(out=ffn_scale[:], in0=s12[:], scalar=0.5 / G_SCALE, in1=scales[:, 2:3],
                                          op0=ALU.mult, op1=ALU.mult))
            for i, (w, dst) in enumerate(((flat[0], w1t[:, :, 0:HIDDEN]), (flat[1], w3t[:, :, 0:HIDDEN]),
                                          (flat[2], w2t[:]))):
                n = w.shape[1]
                step(dve.tensor_scalar(below[:, 0:n], w, thresholds[:, i, 1:2], None, ALU.is_lt))
                shaped = [a.rearrange("p (t n) -> p t n", n=dst.shape[2]) for a in (w, below[:, 0:n])]
                step(dve.scalar_tensor_tensor(out=dst, in0=shaped[0], scalar=thresholds[:, i, 0:1], in1=shaped[1],
                                              op0=ALU.is_gt, op1=ALU.subtract))


def expert_layer(nc, scope, sb, sem, bank, ident16, ones16, route_w, route_e, gu_d, da_d, db_d, x3_dram,
                 xn_dram, slots_dram, y_dram, eid_dram, out_d):

    def t(name, shape, dt):
        return sb(name, shape, dt, scope)

    GU = 2 * INTER
    expert_i = t("expert_i", [P, EXPERTS], I32)
    expert_f = t("expert_f", [P, EXPERTS], F32)
    block_i = t("block_i", [P, 1], I32)
    block_f = t("block_f", [P, 1], F32)
    before = t("before", [P, P], F16)
    starts_ends = t("starts_ends", [EXPERTS, 2 * EXPERTS], F16)
    chosen = t("chosen", [P, TILES * TOPK, EXPERTS], F32)
    member = t("member", [P, TILES, EXPERTS], F16)
    slot_of = t("slot_of", [P, TILES, EXPERTS], F32)
    picked = t("picked", [P, TILES * TOPK, EXPERTS], F32)
    slot_f = t("slot_f", [P, TILES * TOPK], F32)
    slot_u = t("slot_u", [P, TILES * TOPK], U32)
    count_i = t("count_i", [EXPERTS, 1], I32)
    blocks_i = t("blocks_i", [EXPERTS, 1], I32)
    blocks_f = t("blocks_f", [EXPERTS, 1], F32)
    blocks_row = t("blocks_row", [EXPERTS, P], F16)
    base = t("base", [P, 2 * EXPERTS], F32)
    ended = t("ended", [P, EXPERTS], F32)
    eid_f = t("eid_f", [P, 1], F32)
    eid_i = t("eid_i", [P, 1], I32)
    eids = t("eids", [1, P], I32)
    rows16 = t("rows16", [P, TILES, 2 * DM], F16)
    xg = t("xg", [P, 2, TT, 2 * DM], F16)
    xgT = t("xgT", [P, 2, 2, FT, BS], F16)
    gu_raw = t("gu_raw", [P, 2, FT, GU], F32)
    dn_raw = t("dn_raw", [P, 2, 2, DM], F32)
    gu16 = t("gu16", [P, 2, 2, FT, GU], F16)
    dn16 = t("dn16", [P, 2, 2, 2, DM], F16)
    silu_g = t("silu_g", [P, 2, 2 * BS], F32)
    h32 = t("h32", [P, 2, 2 * BS], F32)
    h16 = t("h16", [P, 2, 2, 2 * BS], F16)
    y32 = t("y32", [P, 2, TT, DM], F32)
    NY = 8
    yg = t("yg", [P, NY, DM], F32)
    acc = t("acc", [P, 2, DM], F32)

    names = ("rows_loaded iotas member_ready counted blocks_ready based slots_ready eid_ready eid_out eid_in "
             "scattered route_step gu_hi dn_hi gu_lo dn_lo x_turned xT_hi xT_lo gate_ready "
             "silu_done h_ready h_hi h_lo y_ready y_act y_dve added out_stored "
             "padded tri_ready ").split()
    s = {n: sem("e_" + n) for n in names}
    gu_loaded, dn_loaded, xg_loaded, y_stored, x3_loaded = (
        [sem(f"e_{n}{u}") for u in range(2)] for n in ("gu_loaded", "dn_loaded", "xg_loaded", "y_stored", "x3_loaded"))
    y_gathered = [sem(f"e_y_gathered{i}") for i in range(NY)]
    block = scope.enter_context(nc.Block())

    @block.sync
    def _(sp):
        sp.dma_start(rows16[:], xn_dram.rearrange("(t p) c -> p t c", p=P)).then_inc(s["rows_loaded"], 16)
        sp.wait_ge(s["eid_ready"], 1)
        sp.dma_start(eid_dram.rearrange("(p o) -> p o", o=1), eid_i[:]).then_inc(s["eid_out"], 16)
        sp.wait_ge(s["eid_out"], 16)
        sp.dma_start(eids[:], eid_dram.rearrange("(o p) -> o p", o=1)).then_inc(s["eid_in"], 16)
        sp.wait_ge(s["eid_in"], 16)
        sp.wait_ge(s["padded"], 1)

        def gate_up_weights(n, u):
            e = sp.value_load(eids[0:1, bass.ds(n, 1)], min_val=0, max_val=EXPERTS - 1)
            if not early(n):
                sp.wait_ge(s["gu_lo"], n - 1)
            sp.dma_start(gu_raw[:, u], gu_d[bass.ds(e, 1)].rearrange("o p t n -> (o p) t n")).then_inc(gu_loaded[u], 16)

        def down_weights(n, u):
            e = sp.value_load(eids[0:1, bass.ds(n, 1)], min_val=0, max_val=EXPERTS - 1)
            if not early(n):
                sp.wait_ge(s["dn_lo"], n - 1)
            sp.dma_start(dn_raw[:, u, 0], da_d[bass.ds(e, 1)].rearrange("o p n -> (o p) n")).then_inc(dn_loaded[u], 16)
            sp.dma_start(dn_raw[64:P, u, 1], db_d[bass.ds(e, 1)].rearrange("o p n -> (o p) n")).then_inc(dn_loaded[u], 16)

        def tokens(n, u):
            if not early(n):
                sp.wait_ge(s["x_turned"], 2 * n - 2)
            src = pick(slots_dram.rearrange("(n t p) c -> n p t c", n=NBLK, p=P), n)
            sp.dma_start(xg[:, u], src).then_inc(xg_loaded[u], 16)

        for u in range(2):
            gate_up_weights(u, u)
            down_weights(u, u)
        sp.wait_ge(s["scattered"], 16 * TILES * TOPK)
        tokens(0, 0)
        tokens(1, 1)
        with sp.Fori(1, NBLK // 2) as i:
            for u in range(2):
                gate_up_weights(2 * i + u, u)
                tokens(2 * i + u, u)
                down_weights(2 * i + u, u)
        gate_up_weights(NBLK - 1, 0)
        tokens(NBLK - 1, 0)
        down_weights(NBLK - 1, 0)
        for tile in range(2):
            sp.dma_start(acc[:, tile], x3_dram[tile * P:(tile + 1) * P]).then_inc(x3_loaded[tile % 2], 16)
        for tile in range(TILES):
            sp.wait_ge(s["added"], TOPK * (tile + 1))
            sp.dma_start(out_d[tile * P:(tile + 1) * P], acc[:, tile % 2]).then_inc(s["out_stored"], 16)
            if tile + 2 < TILES:
                sp.wait_ge(s["out_stored"], 16 * (tile + 1))
                sp.dma_start(acc[:, tile % 2], x3_dram[(tile + 2) * P:(tile + 3) * P]).then_inc(x3_loaded[tile % 2], 16)
        sp.wait_ge(s["out_stored"], 16 * TILES)

    @block.gpsimd
    def _(pool):
        pool.memset(before[:], 1.0)
        pool.memset(starts_ends[:], 1.0).then_inc(s["iotas"], 1)
        pool.iota(expert_i[:], pattern=[[1, EXPERTS]], base=0, channel_multiplier=0).then_inc(s["iotas"], 1)
        pool.iota(block_i[:], pattern=[[0, 1]], base=0, channel_multiplier=1).then_inc(s["iotas"], 1)
        pool.wait_ge(s["iotas"], 1)
        pool.affine_select(out=before[:], in_=before[:], compare_op=ALU.is_gt, fill=0.0, base=0,
                           pattern=[[1, P]], channel_multiplier=-1).then_inc(s["tri_ready"], 1)
        pool.affine_select(out=starts_ends[:, 0:EXPERTS], in_=starts_ends[:, 0:EXPERTS], compare_op=ALU.is_gt,
                           fill=0.0, base=0, pattern=[[1, EXPERTS]], channel_multiplier=-1).then_inc(s["tri_ready"], 1)
        pool.affine_select(out=starts_ends[:, EXPERTS:], in_=starts_ends[:, EXPERTS:], compare_op=ALU.is_ge,
                           fill=0.0, base=0, pattern=[[1, EXPERTS]], channel_multiplier=-1).then_inc(s["tri_ready"], 1)
        pool.wait_ge(s["rows_loaded"], 16)
        pool.wait_ge(s["slots_ready"], 1)
        for tile in range(TILES):
            for k in range(TOPK):
                c = tile * TOPK + k
                pool.indirect_dma_start(out=slots_dram,
                                        out_offset=bass.IndirectOffsetOnAxis(ap=slot_u[:, c:c + 1], axis=0),
                                        in_=rows16[:, tile, :], in_offset=None).then_inc(s["scattered"], 16)

        def split_down(n, u):
            if not (isinstance(n, int) and n >= NBLK - 2):
                pool.wait_ge(s["dn_hi"], n + 3)
                pool.tensor_tensor(dn16[:, u, LO], dn_raw[:, u], dn16[:, u, HI], ALU.subtract).then_inc(s["dn_lo"], 1)

        def split_h(n, u):
            pool.wait_ge(s["h_hi"], n + 1)
            pool.tensor_tensor(h16[:, u, LO], h32[:, u], h16[:, u, HI], ALU.subtract).then_inc(s["h_lo"], 1)

        split_down(-2, 0)
        split_down(-1, 1)
        pipeline(pool, lambda n, u: None, split_h, split_down)
        pool.wait_ge(y_stored[0], 16 * (NBLK // 2 + 2))
        pool.wait_ge(y_stored[1], 16 * (NBLK // 2 + 1))
        for c in range(TILES * TOPK):
            if c >= NY:
                pool.wait_ge(s["added"], c - NY + 1)
            pool.indirect_dma_start(out=yg[:, c % NY], out_offset=None, in_=y_dram,
                                    in_offset=bass.IndirectOffsetOnAxis(ap=slot_u[:, c:c + 1], axis=0)
                                    ).then_inc(y_gathered[c % NY], 16)

    @block.scalar
    def _(act):
        def split(n, u):
            act.wait_ge(gu_loaded[u], n * 8 + 16 - 8 * u)
            if not early(n):
                act.wait_ge(s["gate_ready"], n - 1)
            act.copy(gu16[:, u, HI], gu_raw[:, u]).then_inc(s["gu_hi"], 1)
            act.wait_ge(s["x_turned"], n * 2 + 1)
            act.copy(xgT[:, u, HI].rearrange("p t n -> p (t n)"), bank[:, 0, :].bitcast(F16)).then_inc(s["xT_hi"], 1)

        def gate(n, u):
            act.wait_ge(s["gate_ready"], n + 1)
            act.activation(silu_g[:, u, 0:BS], bank[:, 2 + 2 * u, 0:BS], ACT.Silu)
            act.activation(silu_g[64:P, u, BS:2 * BS], bank[0:64, 3 + 2 * u, 0:BS], ACT.Silu).then_inc(s["silu_done"], 1)
            act.wait_ge(s["h_ready"], n + 1)
            act.copy(h16[:, u, HI], h32[:, u]).then_inc(s["h_hi"], 1)

        def store(n, u):
            act.wait_ge(y_stored[u], n * 8 + 16 - 8 * u)
            act.wait_ge(s["y_ready"], n * 2 + 1)
            act.copy(y32[:, u, 0], bank[:, 6, :]).then_inc(s["y_act"], 1)
            act.wait_ge(s["y_act"], n + 1)
            act.wait_ge(s["y_dve"], n + 1)
            dst = pick(y_dram.rearrange("(n t p) c -> n p t c", n=NBLK, p=P), n)
            act.dma_start(dst, y32[:, u]).then_inc(y_stored[u], 16)

        pipeline(act, split, gate, store)

    @block.tensor
    def _(pe):
        pe.wait_ge(s["member_ready"], 1)
        pe.wait_ge(s["tri_ready"], 3)
        pe.matmul(bank[:, 0, :], before[:], member[:].rearrange("p t e -> p (t e)"), start=True, stop=True)
        for d in range(1, TILES):
            pe.matmul(bank[:, 0, d * EXPERTS:], ones16[:],
                      member[:, 0:TILES - d, :].rearrange("p t e -> p (t e)"), start=False, stop=True,
                      skip_group_check=True)
        for tile in range(TILES):
            last = pe.matmul(bank[0:EXPERTS, 1, 0:1], member[:, tile, :], ones16[:, 0:1], start=(tile == 0),
                             stop=(tile == TILES - 1))
        last.then_inc(s["counted"], 1)
        pe.wait_ge(s["blocks_ready"], 1)
        pe.matmul(bank[:, 2, 0:2 * EXPERTS], blocks_row[:], starts_ends[:], start=True,
                  stop=True).then_inc(s["based"], 1)

        def turn(n, u):
            pe.wait_ge(xg_loaded[u], n * 8 + 16 - 8 * u)
            if not (isinstance(n, int) and n < 1):
                pe.wait_ge(s["xT_hi"], n)
                pe.wait_ge(s["xT_lo"], n)
            for part in (HI, LO):
                for ft in range(FT):
                    for tt in range(TT):
                        last = pe.transpose(bank[:, part, :].bitcast(F16)[:, ft * BS + tt * P:ft * BS + (tt + 1) * P],
                                            xg[:, u, tt, part * DM + ft * P:part * DM + (ft + 1) * P], ident16[:])
                last.then_inc(s["x_turned"], 1)

        def gate_up(n, u):
            pe.wait_ge(s["gu_lo"], n + 1)
            pe.wait_ge(s["xT_hi"], n + 1)
            pe.wait_ge(s["xT_lo"], n + 1)
            if not early(n):
                pe.wait_ge(s["h_ready"], n - 1)
            for m, out in enumerate((bank[:, 2 + 2 * u, 0:BS], bank[:, 2 + 2 * u, BS:2 * BS], bank[:, 3 + 2 * u, 0:BS])):
                for ft in range(FT):
                    for j, (lp, rp) in enumerate(PASSES):
                        last = pe.matmul(out, gu16[:, u, lp, ft, m * P:(m + 1) * P], xgT[:, u, rp, ft, :],
                                         start=(ft == 0 and j == 0), stop=(ft == FT - 1 and j == 2))
            last.then_inc(s["gate_ready"], 1)

        def down(n, u):
            pe.wait_ge(s["dn_lo"], n + 1)
            pe.wait_ge(s["h_lo"], n + 1)
            if not (isinstance(n, int) and n < 1):
                pe.wait_ge(s["y_act"], n)
                pe.wait_ge(s["y_dve"], n)
            for tt in range(TT):
                for kt in range(2):
                    for j, (lp, rp) in enumerate(PASSES):
                        last = pe.matmul(bank[:, 6 + tt, :], h16[:, u, lp, kt * BS + tt * P:kt * BS + (tt + 1) * P],
                                         dn16[:, u, rp, kt, :], start=(kt == 0 and j == 0), stop=(kt == 1 and j == 2))
                last.then_inc(s["y_ready"], 1)

        pe.wait_ge(s["slots_ready"], 1)
        pipeline(pe, turn, gate_up, down)

    @block.vector
    def _(dve):
        count = [0]

        def step(ins):
            count[0] += 1
            ins.then_inc(s["route_step"], 1)
            dve.wait_ge(s["route_step"], count[0])

        dve.memset(dn_raw[0:64, :, 1], 0.0).then_inc(s["padded"], 1)
        for u in range(2):
            dve.memset(h32[0:64, u, BS:2 * BS], 0.0).then_inc(y_stored[u], 16)
        dve.wait_ge(s["iotas"], 3)
        dve.tensor_copy(block_f[:], block_i[:])
        step(dve.tensor_copy(expert_f[:], expert_i[:]))
        shape = [P, TILES * TOPK, EXPERTS]
        step(dve.tensor_tensor(chosen[:], route_e[:].rearrange("p t k -> p (t k)").unsqueeze(2).to_broadcast(shape),
                               expert_f[:].unsqueeze(1).to_broadcast(shape), ALU.is_equal))
        dve.tensor_reduce(member[:], chosen[:].rearrange("p (t k) e -> p t e k", k=TOPK), AX.X,
                          ALU.max).then_inc(s["member_ready"], 1)
        dve.wait_ge(s["counted"], 1)
        step(dve.tensor_scalar(count_i[:], bank[0:EXPERTS, 1, 0:1], float(BS - 1), None, ALU.add))
        step(dve.tensor_scalar(blocks_i[:], count_i[:], BS.bit_length() - 1, None, ALU.logical_shift_right))
        step(dve.tensor_copy(blocks_f[:], blocks_i[:]))
        dve.tensor_scalar(blocks_row[:], ones16[0:EXPERTS, :], blocks_f[:, 0:1], None,
                          ALU.mult).then_inc(s["blocks_ready"], 1)
        dve.wait_ge(s["based"], 1)
        dve.tensor_scalar(base[:, 0:EXPERTS], bank[:, 2, 0:EXPERTS], float(BS), None, ALU.mult)
        step(dve.tensor_scalar(ended[:], bank[:, 2, EXPERTS:2 * EXPERTS], block_f[:, 0:1], None, ALU.is_le))
        step(dve.tensor_reduce(eid_f[:], ended[:], AX.X, ALU.add))
        dve.tensor_scalar(eid_i[:], eid_f[:], float(EXPERTS - 1), None, ALU.min).then_inc(s["eid_ready"], 1)
        step(dve.tensor_tensor(slot_of[:], bank[:, 0, :].rearrange("p (t e) -> p t e", e=EXPERTS),
                               base[:, 0:EXPERTS].unsqueeze(1).to_broadcast([P, TILES, EXPERTS]), ALU.add))
        for k in range(TOPK):
            ins = dve.tensor_tensor(picked[:].rearrange("p (t k) e -> p t k e", k=TOPK)[:, :, k],
                                    chosen[:].rearrange("p (t k) e -> p t k e", k=TOPK)[:, :, k],
                                    slot_of[:], ALU.mult)
        step(ins)
        step(dve.tensor_reduce(slot_f[:], picked[:], AX.X, ALU.add))
        dve.tensor_copy(slot_u[:], slot_f[:]).then_inc(s["slots_ready"], 1)

        def split_down(u):
            dve.tensor_copy(dn16[:, u, HI], dn_raw[:, u]).then_inc(s["dn_hi"], 1)

        def split(n, u):
            dve.wait_ge(s["gu_hi"], n + 1)
            dve.tensor_tensor(gu16[:, u, LO], gu_raw[:, u], gu16[:, u, HI], ALU.subtract).then_inc(s["gu_lo"], 1)
            dve.wait_ge(s["x_turned"], n * 2 + 2)
            dve.tensor_copy(xgT[:, u, LO].rearrange("p t n -> p (t n)"), bank[:, 1, :].bitcast(F16)).then_inc(s["xT_lo"], 1)

        def gate(n, u):
            dve.wait_ge(s["silu_done"], n + 1)
            dve.tensor_tensor(h32[:, u, 0:BS], silu_g[:, u, 0:BS], bank[:, 2 + 2 * u, BS:2 * BS], ALU.mult)
            dve.tensor_tensor(h32[64:P, u, BS:2 * BS], silu_g[64:P, u, BS:2 * BS], bank[64:P, 3 + 2 * u, 0:BS],
                              ALU.mult).then_inc(s["h_ready"], 1)

        def leave(n, u):
            dve.wait_ge(y_stored[u], n * 8 + 16 - 8 * u)
            dve.wait_ge(s["y_ready"], n * 2 + 2)
            dve.tensor_copy(y32[:, u, 1], bank[:, 7, :]).then_inc(s["y_dve"], 1)
            if not (isinstance(n, int) and n >= NBLK - 2):
                dve.wait_ge(dn_loaded[u], n * 16 + 64 - 16 * u)
                split_down(u)

        for u in range(2):
            dve.wait_ge(dn_loaded[u], 32)
            split_down(u)
        pipeline(dve, split, gate, leave)
        for c in range(TILES * TOPK):
            tile, k = c // TOPK, c % TOPK
            if k == 0:
                dve.wait_ge(x3_loaded[tile % 2], 16 * (tile // 2 + 1))
            else:
                dve.wait_ge(s["added"], c)
            dve.wait_ge(y_gathered[c % NY], 16 * (c // NY + 1))
            dve.scalar_tensor_tensor(out=acc[:, tile % 2], in0=yg[:, c % NY], scalar=route_w[:, tile, k:k + 1],
                                     in1=acc[:, tile % 2], op0=ALU.mult, op1=ALU.add).then_inc(s["added"], 1)



def kernel(x, ctx_2048, mask_SxS2_bc0, mask_BxS2_bk0, L0_xattn_Wq, L0_xattn_bq, L0_xattn_Wk, L0_xattn_bk,
           L0_xattn_Wv, L0_xattn_bv, L0_xattn_Wo, L0_xattn_bo, L0_ffn_w1, L0_ffn_w3, L0_ffn_w2,
           L1_ffn_router_w, L1_ffn_gate_w, L1_ffn_up_w, L1_ffn_down_w):
    import concourse.bacc as bacc
    from concourse.bass_utils import run_bass_kernel_spmd

    def tiled(w):
        w = np.asarray(w).T
        return w.reshape(-1, P, w.shape[1]).transpose(1, 0, 2)

    def words(m):
        return np.ascontiguousarray(m).view(np.int32)

    mask = np.asarray(mask_SxS2_bc0)
    gate = np.asarray(L1_ffn_gate_w).transpose(0, 2, 1)
    up = np.asarray(L1_ffn_up_w).transpose(0, 2, 1)
    gu = np.concatenate([gate[:, :, :P], up[:, :, :P], gate[:, :, P:], up[:, :, P:]], axis=2)
    down = np.asarray(L1_ffn_down_w).transpose(0, 2, 1)
    arrays = {
        "x": np.asarray(x),
        "ctx": np.asarray(ctx_2048),
        "ctxT": np.asarray(ctx_2048).transpose(0, 2, 1),
        "mq": words(mask.reshape(TT, P, SEQ).transpose(1, 0, 2)),
        "mk": words(mask.T.reshape(TT, P, SEQ).transpose(1, 0, 2)),
        "pad": words(np.asarray(mask_BxS2_bk0)),
        "wq": tiled(L0_xattn_Wq),
        "bq": np.asarray(L0_xattn_bq).reshape(FT, P).T,
        "wk": tiled(L0_xattn_Wk),
        "bk": np.asarray(L0_xattn_bk).reshape(KVW, 1),
        "wv": tiled(L0_xattn_Wv),
        "bv": np.asarray(L0_xattn_bv).reshape(1, KVW),
        "wo": tiled(L0_xattn_Wo),
        "bo": np.asarray(L0_xattn_bo).reshape(1, DM),
        "w1": tiled(L0_ffn_w1),
        "w3": tiled(L0_ffn_w3),
        "w2": np.asarray(L0_ffn_w2).T,
        "rw": tiled(L1_ffn_router_w),
        "gu": gu.reshape(EXPERTS, FT, P, 2 * INTER).transpose(0, 2, 1, 3),
        "da": down[:, :P],
        "db": down[:, P:],
    }
    nc = bacc.Bacc("TRN2", target_bir_lowering=False, num_devices=1)
    given, args = {}, {}
    for name, a in arrays.items():
        given[name] = np.ascontiguousarray(a)
        args[name + "_d"] = nc.dram_tensor(name, given[name].shape, mybir.dt.from_np(given[name].dtype),
                                           kind="ExternalInput").ap()
    out = nc.dram_tensor("out", (TOKENS, DM), F32, kind="ExternalOutput").ap()
    build(nc, out_d=out, **args)
    r = run_bass_kernel_spmd(nc, [given], core_ids=[0])
    return np.asarray(r.results[0]["out"]).reshape(BATCH, SEQ, DM)
```

```python
from contextlib import ExitStack

import numpy as np

import concourse.bass as bass
from concourse import mybir

F32 = mybir.dt.float32
F16 = mybir.dt.float16
I32 = mybir.dt.int32
U32 = mybir.dt.uint32
U8 = mybir.dt.uint8
ALU = mybir.AluOpType
ACT = mybir.ActivationFunctionType
AX = mybir.AxisListType

P = 128
BATCH, SEQ, DM = 8, 256, 512
TOKENS = BATCH * SEQ
TT = SEQ // P
FT = DM // P
HEADS, GROUPS, HD = 32, 8, 16
HPG = HEADS // GROUPS
KVW = GROUPS * HD
HIDDEN = int(2 * DM * 4 / 3)
HT = -(-HIDDEN // P)
HPAD = HT * P
HPAIRS = -(-HT // 2)
EXPERTS, INTER, TOPK = 32, 192, 4
TILES = TOKENS // P
BS = 256
NBLK = TOKENS * TOPK // BS + EXPERTS - 1
SLOTS = NBLK * BS
EPS = 1e-5
MASKED = -60000.0
LEAST = -3.0e38
ROW_PAD = 4 * HD
ROW_MAX = ROW_PAD + 1
ROWS_A = ROW_MAX
ROWS_B = ROW_MAX + 3
G_SCALE = 1.0 / 64.0
P_SCALE = 256.0
HI, LO = 0, 1
PASSES = ((HI, HI), (LO, HI), (HI, LO))
LEFT_LOW_LAST = ((HI, HI), (HI, LO), (LO, HI))


def pair_width(hp):
    return min(2, HT - 2 * hp) * SEQ


def pick(view, n):
    if isinstance(n, int):
        return view[n]
    names = " ".join("bcde"[:len(view.shape) - 2])
    return view[bass.ds(n, 1)].rearrange(f"o a {names} -> (o a) {names}")


def early(n):
    return isinstance(n, int) and n < 2


def pipeline(eng, first, second, third):
    first(0, 0)
    first(1, 1)
    second(0, 0)
    first(2, 0)
    second(1, 1)
    third(0, 0)
    with eng.Fori(1, NBLK // 2) as i:
        for u in range(2):
            n = 2 * i + u
            first(n + 1, 1 - u)
            second(n, u)
            third(n - 1, 1 - u)
    second(NBLK - 1, 0)
    third(NBLK - 2, 1)
    third(NBLK - 1, 0)


def build(nc, x_d, ctx_d, ctxT_d, mq_d, mk_d, pad_d, wq_d, bq_d, wk_d, bk_d, wv_d, bv_d, wo_d, bo_d,
          w1_d, w3_d, w2_d, rw_d, gu_d, da_d, db_d, out_d):
    def dram(name, shape, dt):
        return nc.dram_tensor(name, shape, dt, kind="Internal").ap()

    q_dram = dram("q_dram", (2, DM, SEQ), F16)
    k_dram = dram("k_dram", (2, KVW, SEQ), F16)
    m_dram = dram("m_dram", (3, TT * HEADS, P), F16)
    padbias_dram = dram("padbias_dram", (BATCH, SEQ), F16)
    x3_dram = dram("x3_dram", (TOKENS, DM), F32)
    xn_dram = dram("xn_dram", (TOKENS, 2 * DM), F16)
    y_dram = dram("y_dram", (SLOTS, DM), F32)
    eid_dram = dram("eid_dram", (P,), I32)

    ctx = ExitStack()
    with ctx:
        def sb(name, shape, dt, scope=ctx):
            return scope.enter_context(nc.sbuf_tensor(name, shape, dt))

        def sem(name):
            return ctx.enter_context(nc.semaphore(name))

        bank = ctx.enter_context(nc.psum_tensor("bank", [P, 8, 512], F32))

        ident = sb("ident", [P, P], F32)
        ident16 = sb("ident16", [P, P], F16)
        ones16 = sb("ones16", [P, P], F16)
        route_w = sb("route_w", [P, TILES, TOPK], F32)
        route_e = sb("route_e", [P, TILES, TOPK], F32)

        with ExitStack() as dense:
            dense_layers(nc, dense, sb, sem, bank, ident, ident16, ones16, route_w, route_e,
                         x_d, ctx_d, ctxT_d, mq_d, mk_d, pad_d, wq_d, bq_d, wk_d, bk_d, wv_d, bv_d,
                         wo_d, bo_d, w1_d, w3_d, w2_d, rw_d, q_dram, k_dram, m_dram, padbias_dram,
                         x3_dram, xn_dram)
        with ExitStack() as sparse:
            expert_layer(nc, sparse, sb, sem, bank, ident16, ones16, route_w, route_e,
                         gu_d, da_d, db_d, x3_dram, xn_dram, y_dram, eid_dram, out_d)


def dense_layers(nc, dense, sb, sem, bank, ident, ident16, ones16, route_w, route_e,
                 x_d, ctx_d, ctxT_d, mq_d, mk_d, pad_d, wq_d, bq_d, wk_d, bk_d, wv_d, bv_d,
                 wo_d, bo_d, w1_d, w3_d, w2_d, rw_d, q_dram, k_dram, m_dram, padbias_dram,
                 x3_dram, xn_dram):

    def t(name, shape, dt, scope=dense):
        return sb(name, shape, dt, scope)

    wq16 = t("wq16", [P, 2, FT, DM], F16)
    wk16 = t("wk16", [P, 2, FT, KVW], F16)
    wv16 = t("wv16", [P, 2, FT, KVW], F16)
    wo16 = t("wo16", [P, 2, FT, DM], F16)
    rw16 = t("rw16", [P, 2, FT, EXPERTS], F16)
    w1t = t("w1t", [P, FT, HPAD], F16)
    w3t = t("w3t", [P, FT, HPAD], F16)
    w2t = t("w2t", [P, HT, DM], F16)
    half_s1 = t("half_s1", [P, 1], F32)
    ffn_scale = t("ffn_scale", [P, 1], F32)
    bq_col = t("bq_col", [P, FT], F32)
    bk_col = t("bk_col", [KVW, 1], F32)
    bv_row = t("bv_row", [P, KVW], F32)
    bo_row = t("bo_row", [P, DM], F32)
    mask_q = t("mask_q", [P, TT, SEQ], F16)
    mask_k = t("mask_k", [P, TT, SEQ], F16)
    neg_half = t("neg_half", [P, TT], F32)
    q_stack = t("q_stack", [ROWS_B, HEADS, SEQ], F16)
    k_stack = t("k_stack", [ROWS_B, GROUPS, SEQ], F16)
    v_ones = t("v_ones", [P, TT, GROUPS, 32], F32)
    xin = t("xin", [P, TT, DM], F32)
    ctxT_raw = t("ctxT_raw", [P, FT, SEQ], F32)
    row_max = t("row_max", [P, 2 * TT, HEADS], F32)

    names = ("x_loaded ctx_loaded ctxT_loaded k_stored k_stacked q_stored q_stacked m_stored m_stacked "
             "x3_stored xn_stored ctxT_hi ctxT_lo ctx_hi ctx_lo f_stats f_rstd xf_ready f_transposed "
             "f_hi f_lo v_ready q_ready q_hi k_split v_placed q_split biased a_ready a_reduced "
             "m_turned m_split stats_ready rstd_ready xn_ready transposed hi_ready lo_ready "
             "b_ready exp_done pv_done raw_kept o_turned o_ready wo_ready "
             "up1_ready up3_ready tanh_ready g_ready g_hi g_lo down_ready rows_hi rows_lo s_ready max_ready "
             "e_ready p_ready p_hi p_lo ch_ready logits_ready lmax_ready lexp_ready "
             "front_step dve_step started").split()
    s = {n: sem(n) for n in names}

    with ExitStack() as prologue:
        prepare(nc, prologue, sb, sem, bank, ident, ident16, ones16, wq16, wk16, wv16, wo16, rw16, w1t, w3t,
                w2t, half_s1, ffn_scale, bq_col, bk_col, bv_row, bo_row, mask_q, mask_k, neg_half,
                q_stack, k_stack, v_ones, row_max,
                mq_d, mk_d, pad_d, wq_d, bq_d, wk_d, bk_d, wv_d, bv_d, wo_d, bo_d, w1_d, w3_d, w2_d,
                rw_d, padbias_dram, x_d, xin, s["x_loaded"], ctxT_d, ctxT_raw, s["ctxT_loaded"])

    xres = t("xres", [P, TT, DM], F32)
    xnf = t("xnf", [P, TT, DM], F32)
    xTf16 = t("xTf16", [P, 2, FT, SEQ], F16)
    ctxT16 = t("ctxT16", [P, 2, FT, SEQ], F16)
    q16 = t("q16", [P, 2, FT, SEQ], F16)
    k16 = t("k16", [KVW, 2, SEQ], F16)
    m_rest = t("m_rest", [TT * HEADS, P], F32)
    m16 = t("m16", [TT * HEADS, 3, P], F16)
    statsf = t("statsf", [P, TT, 6], F32)
    momentsf = t("momentsf", [P, TT, 2], F32)
    var_epsf = t("var_epsf", [P, TT], F32)
    rstdf = t("rstdf", [P, TT], F32)
    ctx_raw = t("ctx_raw", [P, TT, DM], F32)
    ctx16 = t("ctx16", [P, 2, TT, DM], F16)
    ctxT_kept = t("ctxT_kept", [P, 2, FT, SEQ], F16)
    res = t("res", [P, TT, DM], F32)
    xn = t("xn", [P, TT, DM], F32)
    xT16 = t("xT16", [P, 2, FT, SEQ], F16)
    xs16 = t("xs16", [P, TT, 2, DM], F16)
    stats = t("stats", [P, TT, 6], F32)
    moments = t("moments", [P, TT, 2], F32)
    var_eps = t("var_eps", [P, TT], F32)
    rstd = t("rstd", [P, TT], F32)
    nothing = t("nothing", [1, 4], F32)
    reduce_started = t("reduce_started", [1, 2], F32)
    probs = t("probs", [P, 8, 1024], F32)
    biased_scores = probs[:, 0, 0:512].bitcast(F16).rearrange("p (u n) -> p u n", u=4)
    attn_raw = t("attn_raw", [P, 2, HPG, SEQ], F32)
    inv_sum = t("inv_sum", [P, 4, HPG, 4], F32)
    shared = t("shared", [P, 6, 1024], F32)
    tanh_a = shared[:, 0, :].rearrange("p (a n) -> p a n", a=2)
    gate_b = shared[:, 1, :].rearrange("p (a n) -> p a n", a=2)
    g32 = shared[:, 2, :].rearrange("p (a n) -> p a n", a=2)
    g16 = shared[:, 3:6, :].rearrange("p a n -> p (a n)").bitcast(F16).rearrange(
        "p (s h n) -> p s h n", s=2, h=2 * HPAIRS)
    e32 = shared[:, 0:2, :].rearrange("p a n -> p (a n)").rearrange("p (e n) -> p e n", e=FT)
    p32 = shared[:, 2:4, :].rearrange("p a n -> p (a n)").rearrange("p (e n) -> p e n", e=FT)
    p16 = shared[:, 4:6, :].rearrange("p a n -> p (a n)").bitcast(F16).rearrange(
        "p (s e n) -> p s e n", s=2, e=FT)
    ch_neg = t("ch_neg", [P, FT], F32)
    ch_bias = t("ch_bias", [P, FT], F32)
    ch_sum = t("ch_sum", [P, FT], F32)
    ch_inv = t("ch_inv", [P, FT], F32)
    lg_neg = t("lg_neg", [P, TT], F32)
    lg_exp = t("lg_exp", [P, TT, EXPERTS], F32)
    lg_sum = t("lg_sum", [P, TT], F32)
    lg_inv = t("lg_inv", [P, TT], F32)
    lg_prob = t("lg_prob", [P, TT, EXPERTS], F32)
    top8 = t("top8", [P, TT, 8], F32)
    idx8 = t("idx8", [P, TT, 8], U32)
    top_sum = t("top_sum", [P, TT], F32)
    top_inv = t("top_inv", [P, TT], F32)

    S_SCALE = float(np.float32(1.0) / np.sqrt(np.float32(DM)))
    LN2, LN3, LN4 = range(3)
    T_ATTN_OUT, T_FFN, T_ROUTER = range(3)
    UNITS_B, UNITS_A = 16, 32
    A_IN_UP = {2: (0, 1, 1, 1), 3: (1, 1, 1, 1), 4: (1, 1, 1, 1), 5: (1, 1)}
    A_IN_DOWN = ((1, 2, 3, 5, 7, 9), (1, 3, 5, 6, 7, 9), (1, 3, 5, 7, 9), (1, 3))
    A_UP = sum(sum(n) for n in A_IN_UP.values())
    assert A_UP + sum(len(run) for run in A_IN_DOWN) == UNITS_A
    EARLY_B = 3
    DVE_FRONT_STEPS, DVE_BACK_STEPS = 8, 42

    def a_in_up(hp, product):
        here = A_IN_UP.get(hp, (0, 0, 0, 0))
        first = sum(sum(n) for h, n in A_IN_UP.items() if h < hp) + sum(here[:product])
        return range(first, first + here[product])

    class Chain:

        def __init__(self, eng, sem_, per, b):
            self.eng, self.sem, self.per, self.b, self.n = eng, sem_, per, b, 0

        def then(self, ins, alone=False):
            self.n += 1
            ins.then_inc(self.sem, 1)
            if alone:
                wait_apart(self.eng, self.sem, self.b * self.per + self.n)
            else:
                self.eng.wait_ge(self.sem, self.b * self.per + self.n)

        def end(self):
            assert self.n == self.per, self.n

    def wait_apart(dve, semaphore, value):
        dve.wait_ge(semaphore, value)
        dve.memset(nothing[:, 0:1], 0.0)

    def all_steps(eng, front, step):
        front(0)
        with eng.Fori(0, BATCH - 1) as b:
            step(b, True)
        step(BATCH - 1, False)

    block = dense.enter_context(nc.Block())

    @block.sync
    def _(sp):
        def sp_wait(semaphore, value):
            value = sp.snap(value)
            sp.wait_ge(s["started"], 1)
            sp.wait_ge(semaphore, value)

        def rows(dram, b):
            return pick(dram.rearrange("(b t p) c -> b p t c", b=BATCH, p=P), b)

        def load_x(b):
            sp.dma_start(xin[:], pick(x_d, b).rearrange("(t p) d -> p t d", p=P)).then_inc(s["x_loaded"], 16)

        def load_ctx(b):
            sp.dma_start(ctx_raw[:], pick(ctx_d, b).rearrange("(t p) d -> p t d", p=P)).then_inc(s["ctx_loaded"], 16)

        def load_ctxT(b):
            sp.dma_start(ctxT_raw[:], pick(ctxT_d, b).rearrange("(t p) k -> p t k", p=P)
                         ).then_inc(s["ctxT_loaded"], 16)

        def stack_keys_queries(c):
            sp.wait_ge(s["k_split"], c + 1)
            for part in (HI, LO):
                sp.dma_start(k_dram[part], k16[:, part, :]).then_inc(s["k_stored"], 16)
            sp.wait_ge(s["k_stored"], c * 32 + 32)
            for i, part in enumerate((HI, LO, HI, LO)):
                sp.dma_start(k_stack[i * HD:(i + 1) * HD],
                             k_dram[part].rearrange("(g d) k -> d g k", d=HD)).then_inc(s["k_stacked"], 16)
            sp.dma_start(k_stack[ROW_PAD:ROW_PAD + 1],
                         padbias_dram[bass.ds(c, 1)].unsqueeze(1).to_broadcast([1, GROUPS, SEQ])
                         ).then_inc(s["k_stacked"], 16)
            sp.wait_ge(s["q_split"], c * FT + FT)
            for part in (HI, LO):
                sp.dma_start(q_dram[part].rearrange("(t p) q -> p t q", p=P),
                             q16[:, part]).then_inc(s["q_stored"], 16)
            sp.wait_ge(s["q_stored"], c * 32 + 32)
            for i, part in enumerate((HI, HI, LO, LO)):
                sp.dma_start(q_stack[i * HD:(i + 1) * HD],
                             q_dram[part].rearrange("(h d) q -> d h q", d=HD)).then_inc(s["q_stacked"], 16)

        def stack_maxima(c):
            sp.wait_ge(s["m_split"], c + 1)
            sp.dma_start(m_dram.rearrange("i h q -> h i q"), m16[:]).then_inc(s["m_stored"], 16)
            sp.wait_ge(s["m_stored"], c * 16 + 16)
            for tt in range(TT):
                sp.dma_start(q_stack[ROW_MAX:ROW_MAX + 3, :, tt * P:(tt + 1) * P],
                             m_dram[:, tt * HEADS:(tt + 1) * HEADS, :]).then_inc(s["m_stacked"], 16)

        def front(c):
            stack_keys_queries(c)
            sp.wait_ge(s["ctxT_lo"], c + 1)
            load_ctxT(c + 1)
            sp.wait_ge(s["biased"], c + 1)
            sp.wait_ge(s["xf_ready"], 2 * c + 2)
            load_x(c + 1)
            stack_maxima(c)

        def step(b, front_too, load_next=True):
            c = b + 1
            if front_too:
                sp_wait(s["ctx_lo"], b + 1)
                load_ctx(c)
                if load_next:
                    sp_wait(s["ctxT_lo"], c + 1)
                    load_ctxT(c + 1)
            if front_too:
                stack_keys_queries(c)
                if load_next:
                    sp_wait(s["biased"], c + 1)
                    load_x(c + 1)
                stack_maxima(c)
            sp_wait(s["xn_ready"], b * 6 + 6)
            sp.dma_start(rows(x3_dram, b), res[:]).then_inc(s["x3_stored"], 16)
            sp.wait_ge(s["rows_hi"], b * 4 + 4)
            sp.wait_ge(s["rows_lo"], b * 4 + 4)
            sp.dma_start(rows(xn_dram, b), xs16[:].rearrange("p t s d -> p t (s d)")).then_inc(s["xn_stored"], 16)

        load_ctx(0)
        sp.wait_ge(s["started"], 1)
        front(0)
        with sp.Fori(0, BATCH - 2) as b:
            step(b, True)
        step(BATCH - 2, True, load_next=False)
        step(BATCH - 1, False)
        sp.wait_ge(s["x3_stored"], BATCH * 16 + 16)
        sp.wait_ge(s["xn_stored"], BATCH * 16 + 16)

    @block.gpsimd
    def _(pool):
        def context_low(c):
            pool.wait_ge(s["ctxT_hi"], c + 1)
            pool.tensor_tensor(ctxT16[:, LO], ctxT_raw[:], ctxT16[:, HI], ALU.subtract).then_inc(s["ctxT_lo"], 1)

        def deviations(asked, given, var_eps, rstd, first):
            for tt in range(TT):
                pool.wait_ge(s[asked], first + tt + 1)
                pool.tensor_tensor(rstd[:, tt:tt + 1], var_eps[:, tt:tt + 1], neg_half[:, 0:1],
                                   ALU.pow).then_inc(s[given], 1)

        def add_bias(c):
            pool.tensor_tensor(xres[:], xin[:], bo_row[:].unsqueeze(1).to_broadcast([P, TT, DM]),
                               ALU.add).then_inc(s["biased"], 1)

        def front(c):
            context_low(c)
            deviations("f_stats", "f_rstd", var_epsf, rstdf, c * TT)
            add_bias(c)

        def step(b, front_too):
            def inverse_deviation(ln):
                deviations("stats_ready", "rstd_ready", var_eps, rstd, b * 3 * TT + ln * TT)

            if front_too:
                context_low(b + 1)
                deviations("f_stats", "f_rstd", var_epsf, rstdf, (b + 1) * TT)
            pool.wait_ge(s["ctx_hi"], b + 1)
            pool.tensor_tensor(ctx16[:, LO], ctx_raw[:], ctx16[:, HI], ALU.subtract).then_inc(s["ctx_lo"], 1)
            inverse_deviation(LN2)
            if front_too:
                add_bias(b + 1)
            for hp in range(HPAIRS):
                w = pair_width(hp)
                pool.wait_ge(s["g_hi"], b * HPAIRS + hp + 1)
                pool.tensor_tensor(g16[:, LO, 2 * hp:2 * hp + w // SEQ, :].rearrange("p h n -> p (h n)"),
                                   g32[:, hp % 2, 0:w],
                                   g16[:, HI, 2 * hp:2 * hp + w // SEQ, :].rearrange("p h n -> p (h n)"),
                                   ALU.subtract).then_inc(s["g_lo"], 1)
            for ln in (LN3, LN4):
                inverse_deviation(ln)
                for tt in range(TT):
                    n = TT * (ln - LN3) + tt + 1
                    pool.wait_ge(s["rows_hi"], b * 4 + n)
                    pool.tensor_tensor(xs16[:, tt, LO], xn[:, tt], xs16[:, tt, HI],
                                       ALU.subtract).then_inc(s["rows_lo"], 1)
                if ln == LN3:
                    for et in range(FT):
                        pool.wait_ge(s["p_hi"], b * FT + et + 1)
                        pool.tensor_tensor(p16[:, LO, et], p32[:, et], p16[:, HI, et],
                                           ALU.subtract).then_inc(s["p_lo"], 1)

        pool.wait_ge(s["started"], 1)
        all_steps(pool, front, step)

    @block.scalar
    def _(act):
        def front_high(c):
            for i in range(2):
                act.wait_ge(s["f_transposed"], c * 2 + i + 1)
                act.copy(xTf16[:, HI, 2 * i:2 * i + 2, :].rearrange("p t n -> p (t n)"),
                         bank[:, 5 - i, :]).then_inc(s["f_hi"], 1)

        def queries_high(c, hts):
            for ht in hts:
                act.wait_ge(s["q_ready"], c * FT + ht // 2 * 2 + 2)
                act.activation(q16[:, HI, ht], bank[:, 5 - ht // 2, (ht % 2) * SEQ:(ht % 2 + 1) * SEQ],
                               ACT.Identity, bias=bq_col[:, ht:ht + 1]).then_inc(s["q_hi"], 1)

        def exponentials(b, u):
            if u >= 8:
                act.wait_ge(s["pv_done"], b * 4 + (u - 8) // 4 + 1)
            act.wait_ge(s["b_ready"], b * UNITS_B + u + 1)
            act.activation(probs[:, u % 8], bank[:, 2 * (u % 3):2 * (u % 3) + 2, :].rearrange("p a n -> p (a n)"),
                           ACT.Exp, scale=1.0 / 4.0).then_inc(s["exp_done"], 1)

        def front(c):
            front_high(c)
            queries_high(c, range(FT))
            for u in range(EARLY_B):
                exponentials(c, u)

        def step(b, front_too):
            def high_part(which, first_bank):
                for i in range(2):
                    act.wait_ge(s["transposed"], b * 6 + 2 * which + i + 1)
                    act.copy(xT16[:, HI, 2 * i:2 * i + 2, :].rearrange("p t n -> p (t n)"),
                             bank[:, first_bank + i, :]).then_inc(s["hi_ready"], 1)

            for u in range(EARLY_B, UNITS_B):
                exponentials(b, u)
                if u in (10, UNITS_B - 1):
                    gg = 0 if u == 10 else 1
                    act.wait_ge(s["pv_done"], b * 4 + 2 * gg + 2)
                    act.copy(attn_raw[:, gg].rearrange("p r n -> p (r n)"),
                             bank[:, 6:8, :].rearrange("p a n -> p (a n)")).then_inc(s["raw_kept"], 1)
            if front_too:
                front_high(b + 1)
            high_part(T_ATTN_OUT, 6)
            if front_too:
                queries_high(b + 1, range(FT))
            high_part(T_FFN, 2)
            for hp in range(HPAIRS + 1):
                if hp < HPAIRS:
                    w = pair_width(hp)
                    act.wait_ge(s["up1_ready"], b * HPAIRS + hp + 1)
                    if hp >= 2:
                        act.wait_ge(s["g_ready"], b * HPAIRS + hp - 1)
                    act.activation(tanh_a[:, hp % 2, 0:w], bank[:, 2 * (hp % 2), 0:w], ACT.Tanh,
                                   scale=half_s1[:, 0:1]).then_inc(s["tanh_ready"], 1)
                if hp >= 1:
                    j = hp - 1
                    w = pair_width(j)
                    act.wait_ge(s["g_ready"], b * HPAIRS + j + 1)
                    act.copy(g16[:, HI, 2 * j:2 * j + w // SEQ, :].rearrange("p h n -> p (h n)"),
                             g32[:, j % 2, 0:w]).then_inc(s["g_hi"], 1)

            def rows_high(ln):
                for tt in range(TT):
                    act.wait_ge(s["xn_ready"], b * 6 + 2 * ln + tt + 1)
                    act.copy(xs16[:, tt, HI], xn[:, tt]).then_inc(s["rows_hi"], 1)

            act.wait_ge(s["xn_stored"], b * 16 + 16)
            rows_high(LN3)
            for et in range(FT + 1):
                if et < FT:
                    act.wait_ge(s["max_ready"], b * FT + et + 1)
                    act.activation(e32[:, et], bank[:, et, :], ACT.Exp, bias=ch_bias[:, et:et + 1], scale=S_SCALE,
                                   accum_out=ch_sum[:, et:et + 1]).then_inc(s["e_ready"], 1)
                if et >= 1:
                    act.wait_ge(s["p_ready"], b * FT + et)
                    act.copy(p16[:, HI, et - 1], p32[:, et - 1]).then_inc(s["p_hi"], 1)
            if front_too:
                for u in range(EARLY_B - 1):
                    exponentials(b + 1, u)
            rows_high(LN4)
            high_part(T_ROUTER, 6)
            if front_too:
                exponentials(b + 1, EARLY_B - 1)
            act.wait_ge(s["lmax_ready"], b + 1)
            for tt in range(TT):
                act.activation(lg_exp[:, tt], bank[:, 7, tt * EXPERTS:(tt + 1) * EXPERTS], ACT.Exp,
                               bias=lg_neg[:, tt:tt + 1],
                               accum_out=lg_sum[:, tt:tt + 1]).then_inc(s["lexp_ready"], 1)

        all_steps(act, front, step)

    @block.tensor
    def _(pe):
        def three(out, left, right, n, passes=(0, 1, 2), order=PASSES):
            for j in passes:
                lp, rp = order[j]
                for i in range(n):
                    last = pe.matmul(out, left(lp, i), right(rp, i), start=(i == 0 and j == 0),
                                     stop=(i == n - 1 and j == 2))
            return last

        def turn(src, banks, signal, ready, first, steps=1):
            for tt in range(TT):
                pe.wait_ge(s[ready], first + steps * (tt + 1))
                for ft in range(FT):
                    last = pe.transpose(
                        bank[:, banks[ft // 2], (ft % 2) * SEQ + tt * P:(ft % 2) * SEQ + (tt + 1) * P],
                        src[:, tt, ft * P:(ft + 1) * P], ident[:])
                    if ft % 2 == 1 and tt == TT - 1:
                        last.then_inc(s[signal], 1)

        def keys_values(c):
            pe.wait_ge(s["ctxT_hi"], c + 1)
            pe.wait_ge(s["ctxT_lo"], c + 1)
            three(bank[0:KVW, 4, 0:SEQ], lambda p, i: wk16[:, p, i, :], lambda p, i: ctxT16[:, p, i, :],
                  FT)
            for kt in range(TT):
                last = three(bank[:, 4, SEQ + kt * KVW:SEQ + (kt + 1) * KVW],
                             lambda p, i: ctxT16[:, p, i, kt * P:(kt + 1) * P],
                             lambda p, i: wv16[:, p, i, :], FT)
            last.then_inc(s["v_ready"], 1)

        def turn_front(c):
            pe.wait_ge(s["k_split"], c + 1)
            pe.wait_ge(s["v_placed"], c + 1)
            turn(xnf, (5, 4), "f_transposed", "xf_ready", c * 2)

        def queries(c, hts):
            pe.wait_ge(s["f_lo"], c * 2 + 2)
            for ht in hts:
                three(bank[:, 5 - ht // 2, (ht % 2) * SEQ:(ht % 2 + 1) * SEQ],
                      lambda p, i: wq16[:, p, i, ht * P:(ht + 1) * P],
                      lambda p, i: xTf16[:, p, i, :], FT).then_inc(s["q_ready"], 1)

        def stacked(c):
            pe.wait_ge(s["k_stacked"], c * 80 + 80)
            pe.wait_ge(s["q_stacked"], c * 64 + 64)

        def scores_a(c, units):
            for u in units:
                g, half, qt = u // 4, u // 2 % 2, u % 2
                if u >= 2:
                    pe.wait_ge(s["a_reduced"], c * UNITS_A + u - 1)
                for r in range(2):
                    h = HPG * g + 2 * half + r
                    last = pe.matmul(bank[:, 6 + u % 2, r * SEQ:(r + 1) * SEQ],
                                     q_stack[0:ROWS_A, h, qt * P:(qt + 1) * P],
                                     k_stack[0:ROWS_A, g, :], start=True, stop=True)
                last.then_inc(s["a_ready"], 1)

        def turn_maxima(c):
            pe.wait_ge(s["a_reduced"], c * UNITS_A + UNITS_A)
            pe.transpose(bank[:, 6, 0:P], row_max[:].rearrange("p t h -> p (t h)"),
                         ident[:]).then_inc(s["m_turned"], 1)

        def scores_b(b, u):
            gg, kt, j = u // 8, u // 4 % 2, u % 4
            g = 4 * gg + j
            if u >= 3:
                pe.wait_ge(s["exp_done"], b * UNITS_B + u - 2)
            for half in range(2):
                out = bank[:, 2 * (u % 3) + half, :]
                pe.matmul(out.rearrange("p (a n) -> p a n", a=2), ident16[:],
                          mask_k[:, kt, :].unsqueeze(1).to_broadcast([P, 2, SEQ]), start=True, stop=True)
                h = HPG * g + 2 * half
                last = pe.matmul(out, k_stack[0:ROWS_B, g, kt * P:(kt + 1) * P],
                                 q_stack[0:ROWS_B, h:h + 2, :].rearrange("k h q -> k (h q)"),
                                 start=False, stop=True, skip_group_check=True)
            last.then_inc(s["b_ready"], 1)

        def early_b(b, units):
            if units[0] == 0:
                pe.wait_ge(s["m_stacked"], b * 32 + 32)
            for u in units:
                scores_b(b, u)

        def front(c):
            keys_values(c)
            turn_front(c)
            queries(c, range(FT))
            stacked(c)
            scores_a(c, range(UNITS_A))
            turn_maxima(c)
            early_b(c, range(EARLY_B))

        def step(b, front_too):
            c = b + 1

            def pv(quartet):
                gg, kt = quartet // 2, quartet % 2
                pe.wait_ge(s["exp_done"], b * UNITS_B + 4 * quartet + 4)
                if quartet == 2:
                    pe.wait_ge(s["raw_kept"], b * 2 + 1)
                for half in range(2):
                    for j in range(4):
                        last = pe.matmul(bank[32 * j:32 * j + 32, 6 + half, :], v_ones[:, kt, 4 * gg + j, :],
                                         probs[:, 4 * (quartet % 2) + j, half * 512:(half + 1) * 512],
                                         start=(kt == 0), stop=(kt == TT - 1), tile_position=(0, 32 * j))
                last.then_inc(s["pv_done"], 1)

            for u in range(EARLY_B, UNITS_B):
                scores_b(b, u)
                if u in (6, 10, 14):
                    pv((u - 6) // 4)
            pv(3)
            if front_too:
                keys_values(c)
            pe.wait_ge(s["raw_kept"], b * 2 + 2)
            for qt in range(TT):
                for gg in range(2):
                    for r in range(HPG):
                        last = pe.transpose(bank[:, 2 * qt + gg, r * P:(r + 1) * P],
                                            attn_raw[:, gg, r, qt * P:(qt + 1) * P], ident[:])
                    last.then_inc(s["o_turned"], 1)
            if front_too:
                turn_front(c)
            turn(xn, (6, 7), "transposed", "o_ready", b * 4, 2)
            if front_too:
                queries(c, (0, 1))
            pe.wait_ge(s["hi_ready"], b * 6 + 2)
            for passes in ((0, 1), (2,)):
                if passes == (2,):
                    pe.wait_ge(s["lo_ready"], b * 6 + 2)
                for tt in range(TT):
                    last = three(bank[:, tt, :], lambda p, i: xT16[:, p, i, tt * P:(tt + 1) * P],
                                 lambda p, i: wo16[:, p, i, :], FT, passes, LEFT_LOW_LAST)
                    if passes == (2,):
                        last.then_inc(s["wo_ready"], 1)
            if front_too:
                queries(c, (2, 3))
            turn(xn, (2, 3), "transposed", "xn_ready", b * 6)
            pe.wait_ge(s["hi_ready"], b * 6 + 4)
            for hp in range(HPAIRS):
                if hp >= 2:
                    pe.wait_ge(s["g_ready"], b * HPAIRS + hp - 1)
                if hp == 2 and front_too:
                    stacked(c)
                for which, (w, signal) in enumerate(((w1t, "up1_ready"), (w3t, "up3_ready"))):
                    alike = pair_width(hp) // SEQ
                    for a in range(alike):
                        h0 = (2 * hp + a) * P
                        for part in (HI, LO):
                            if hp == 0 and part == LO:
                                pe.wait_ge(s["lo_ready"], b * 6 + 4)
                            for ft in range(FT):
                                last = pe.matmul(bank[:, 2 * (hp % 2) + which, a * SEQ:(a + 1) * SEQ],
                                                 w[:, ft, h0:h0 + P], xT16[:, part, ft, :],
                                                 start=(ft == 0 and part == HI), stop=(ft == FT - 1 and part == LO))
                        if a == alike - 1:
                            last.then_inc(s[signal], 1)
                        if front_too:
                            scores_a(c, a_in_up(hp, which * alike + a))
            unit = A_UP
            for part, ready in ((HI, "g_hi"), (LO, "g_lo")):
                for tt in range(TT):
                    for ht in range(HT):
                        if tt == 0:
                            pe.wait_ge(s[ready], b * HPAIRS + ht // 2 + 1)
                        last = pe.matmul(bank[:, 4 + tt, :], g16[:, part, ht, tt * P:(tt + 1) * P], w2t[:, ht, :],
                                         start=(ht == 0 and part == HI), stop=(ht == HT - 1 and part == LO))
                        if part == LO and ht == HT - 1:
                            last.then_inc(s["down_ready"], 1)
                        if front_too and ht in A_IN_DOWN[TT * part + tt]:
                            scores_a(c, range(unit, unit + 1))
                            unit += 1
            if front_too:
                turn_maxima(c)
            pe.wait_ge(s["ctx_lo"], b + 1)
            for tt in range(TT):
                pe.wait_ge(s["rows_hi"], b * 4 + tt + 1)
                for et in range(FT):
                    for part in (HI, LO):
                        pe.matmul(bank[:, et, :], ctx16[:, part, tt, et * P:(et + 1) * P], xs16[:, tt, HI, :],
                                  start=(tt == 0 and part == HI), stop=False)
            pe.wait_ge(s["rows_lo"], b * 4 + 2)
            for et in range(FT):
                for tt in range(TT):
                    last = pe.matmul(bank[:, et, :], ctx16[:, HI, tt, et * P:(et + 1) * P], xs16[:, tt, LO, :],
                                     start=False, stop=(tt == TT - 1))
                last.then_inc(s["s_ready"], 1)
            for et in range(FT):
                pe.wait_ge(s["p_hi"], b * FT + et + 1)
                for tt in range(TT):
                    for part in (HI, LO):
                        pe.matmul(bank[:, 4 + tt, :], ctxT_kept[:, part, et, tt * P:(tt + 1) * P],
                                  p16[:, HI, et, :], start=(et == 0 and part == HI), stop=False)
            pe.wait_ge(s["p_lo"], b * FT + FT)
            for tt in range(TT):
                for et in range(FT):
                    last = pe.matmul(bank[:, 4 + tt, :], ctxT_kept[:, HI, et, tt * P:(tt + 1) * P],
                                     p16[:, LO, et, :], start=False, stop=(et == FT - 1))
                last.then_inc(s["ch_ready"], 1)
            if front_too:
                early_b(c, range(EARLY_B - 1))
            turn(xn, (6, 7), "transposed", "xn_ready", b * 6 + 4)
            if front_too:
                early_b(c, range(EARLY_B - 1, EARLY_B))
            pe.wait_ge(s["lo_ready"], b * 6 + 6)
            for tt in range(TT):
                last = three(bank[:, 7, tt * EXPERTS:(tt + 1) * EXPERTS],
                             lambda p, i: xT16[:, p, i, tt * P:(tt + 1) * P], lambda p, i: rw16[:, p, i, :], FT)
            last.then_inc(s["logits_ready"], 1)

        all_steps(pe, front, step)

    @block.vector
    def _(dve):
        def context_high(c):
            dve.wait_ge(s["ctxT_loaded"], c * 16 + 16)
            dve.tensor_copy(ctxT16[:, HI], ctxT_raw[:]).then_inc(s["ctxT_hi"], 1)

        def normalise(dst, src, tt, stats, moments, var_eps, rstd, asked, given, n, steps):
            steps.then(dve.bn_stats(stats[:, tt], src[:, tt]), alone=True)
            steps.then(dve.bn_aggr(moments[:, tt], stats[:, tt]))
            dve.tensor_scalar(var_eps[:, tt:tt + 1], moments[:, tt, 1:2], EPS, None, ALU.add).then_inc(s[asked], 1)
            dve.wait_ge(s[given], n + 1)
            return dve.tensor_scalar(dst[:, tt], src[:, tt], moments[:, tt, 0:1], rstd[:, tt:tt + 1],
                                     ALU.subtract, ALU.mult)

        def front_norm(c, steps):
            dve.wait_ge(s["x_loaded"], c * 16 + 16)
            for tt in range(TT):
                normalise(xnf, xin, tt, statsf, momentsf, var_epsf, rstdf, "f_stats", "f_rstd", c * TT + tt,
                          steps).then_inc(s["xf_ready"], 1)

        def place_keys_values(c, steps):
            dve.wait_ge(s["v_ready"], c + 1)
            steps.then(dve.tensor_scalar(k16[:, HI], bank[0:KVW, 4, 0:SEQ], bk_col[:, 0:1], None, ALU.add))
            dve.scalar_tensor_tensor(out=k16[:, LO], in0=bank[0:KVW, 4, 0:SEQ], scalar=bk_col[:, 0:1],
                                     in1=k16[:, HI], op0=ALU.add, op1=ALU.subtract).then_inc(s["k_split"], 1)
            for kt in range(TT):
                ins = dve.tensor_tensor(v_ones[:, kt, :, 0:HD],
                                        bank[:, 4, SEQ + kt * KVW:SEQ + (kt + 1) * KVW].rearrange(
                                            "p (g d) -> p g d", d=HD),
                                        bv_row[:].rearrange("p (g d) -> p g d", d=HD), ALU.add)
            ins.then_inc(s["v_placed"], 1)

        def front_low(c):
            for i in range(2):
                dve.wait_ge(s["f_hi"], c * 2 + i + 1)
                dve.tensor_tensor(xTf16[:, LO, 2 * i:2 * i + 2, :].rearrange("p t n -> p (t n)"),
                                  bank[:, 5 - i, :],
                                  xTf16[:, HI, 2 * i:2 * i + 2, :].rearrange("p t n -> p (t n)"),
                                  ALU.subtract).then_inc(s["f_lo"], 1)

        def queries_low(c, hts):
            for ht in hts:
                dve.wait_ge(s["q_hi"], c * FT + ht // 2 * 2 + 2)
                dve.scalar_tensor_tensor(out=q16[:, LO, ht],
                                         in0=bank[:, 5 - ht // 2, (ht % 2) * SEQ:(ht % 2 + 1) * SEQ],
                                         scalar=bq_col[:, ht:ht + 1], in1=q16[:, HI, ht], op0=ALU.add,
                                         op1=ALU.subtract).then_inc(s["q_split"], 1)

        def reduce_a(c, units):
            for u in units:
                g, half, qt = u // 4, u // 2 % 2, u % 2
                h = HPG * g + 2 * half
                dve.wait_ge(s["a_ready"], c * UNITS_A + u + 1)
                dve.memset(reduce_started[:, u % 2:u % 2 + 1], 0.0)
                for r in range(2):
                    last = dve.tensor_tensor_reduce(
                        out=biased_scores[:, 2 * (u % 2) + r], in0=bank[:, 6 + u % 2, r * SEQ:(r + 1) * SEQ],
                        in1=mask_q[:, qt, :], scale=1.0, scalar=LEAST, op0=ALU.add, op1=ALU.max,
                        accum_out=row_max[:, qt, h + r:h + r + 1])
                last.then_inc(s["a_reduced"], 1)

        def split_maxima(c, steps):
            dve.wait_ge(s["m_turned"], c + 1)
            turned = bank[0:TT * HEADS, 6, 0:P]
            steps.then(dve.tensor_scalar(m16[:, 0], turned, -1.0, None, ALU.mult))
            steps.then(dve.scalar_tensor_tensor(out=m_rest[:], in0=turned, scalar=-1.0, in1=m16[:, 0],
                                                op0=ALU.mult, op1=ALU.subtract))
            steps.then(dve.tensor_copy(m16[:, 1], m_rest[:]))
            dve.tensor_tensor(m16[:, 2], m_rest[:], m16[:, 1], ALU.subtract).then_inc(s["m_split"], 1)

        def front(c):
            steps = Chain(dve, s["front_step"], DVE_FRONT_STEPS, c)
            context_high(c)
            front_norm(c, steps)
            place_keys_values(c, steps)
            front_low(c)
            queries_low(c, range(FT))
            reduce_a(c, range(UNITS_A))
            split_maxima(c, steps)
            steps.end()

        def step(b, front_too):
            c = b + 1
            front_steps = Chain(dve, s["front_step"], DVE_FRONT_STEPS, c)
            steps = Chain(dve, s["dve_step"], DVE_BACK_STEPS, b)

            def add_and_norm(ln, add):
                for tt in range(TT):
                    steps.then(add(tt))
                    normalise(xn, res, tt, stats, moments, var_eps, rstd, "stats_ready", "rstd_ready",
                              b * 3 * TT + ln * TT + tt, steps).then_inc(s["xn_ready"], 1)

            def low_part(which, first_bank):
                for i in range(2):
                    dve.wait_ge(s["hi_ready"], b * 6 + 2 * which + i + 1)
                    dve.tensor_tensor(xT16[:, LO, 2 * i:2 * i + 2, :].rearrange("p t n -> p (t n)"),
                                      bank[:, first_bank + i, :],
                                      xT16[:, HI, 2 * i:2 * i + 2, :].rearrange("p t n -> p (t n)"),
                                      ALU.subtract).then_inc(s["lo_ready"], 1)

            steps.then(dve.tensor_copy(ctxT_kept[:], ctxT16[:]))
            if front_too:
                context_high(c)
            dve.wait_ge(s["ctx_loaded"], b * 16 + 16)
            dve.tensor_copy(ctx16[:, HI], ctx_raw[:]).then_inc(s["ctx_hi"], 1)
            if front_too:
                front_norm(c, front_steps)
                place_keys_values(c, front_steps)
            for i in range(4):
                qt, gg = i // 2, i % 2
                dve.wait_ge(s["o_turned"], b * 4 + i + 1)
                ps = bank[:, i, :].rearrange("p (r j e) -> p r j e", r=HPG, j=4)
                steps.then(dve.reciprocal(inv_sum[:, i], ps[:, :, :, HD]))
                dve.tensor_tensor(xn[:, qt, gg * SEQ:(gg + 1) * SEQ].rearrange("p (j r d) -> p r j d", j=4, r=HPG),
                                  ps[:, :, :, 0:HD],
                                  inv_sum[:, i].unsqueeze(3).to_broadcast([P, HPG, 4, HD]),
                                  ALU.mult).then_inc(s["o_ready"], 1)
            if front_too:
                front_low(c)
            low_part(T_ATTN_OUT, 6)
            if front_too:
                queries_low(c, (0, 1))
            dve.wait_ge(s["biased"], b + 1)
            dve.wait_ge(s["x3_stored"], b * 16 + 16)

            def add_attention(tt):
                dve.wait_ge(s["wo_ready"], b * 2 + tt + 1)
                return dve.tensor_tensor(res[:, tt], bank[:, tt, :], xres[:, tt], ALU.add)

            add_and_norm(LN2, add_attention)
            if front_too:
                queries_low(c, (2, 3))
            low_part(T_FFN, 2)
            for hp in range(HPAIRS):
                w = pair_width(hp)
                products = 2 * w // SEQ
                if front_too:
                    for product in range(products - 1):
                        reduce_a(c, a_in_up(hp, product))
                dve.wait_ge(s["tanh_ready"], b * HPAIRS + hp + 1)
                dve.wait_ge(s["up3_ready"], b * HPAIRS + hp + 1)
                steps.then(dve.scalar_tensor_tensor(out=gate_b[:, hp % 2, 0:w], in0=tanh_a[:, hp % 2, 0:w],
                                                    scalar=1.0, in1=bank[:, 2 * (hp % 2) + 1, 0:w], op0=ALU.add,
                                                    op1=ALU.mult))
                if hp >= 2:
                    dve.wait_ge(s["g_lo"], b * HPAIRS + hp - 1)
                dve.scalar_tensor_tensor(out=g32[:, hp % 2, 0:w], in0=gate_b[:, hp % 2, 0:w], scalar=G_SCALE,
                                         in1=bank[:, 2 * (hp % 2), 0:w], op0=ALU.mult,
                                         op1=ALU.mult).then_inc(s["g_ready"], 1)
                if front_too:
                    reduce_a(c, a_in_up(hp, products - 1))
            if front_too:
                reduce_a(c, range(A_UP, UNITS_A))

            def add_ffn(tt):
                dve.wait_ge(s["down_ready"], b * 2 + tt + 1)
                return dve.scalar_tensor_tensor(out=res[:, tt], in0=bank[:, 4 + tt, :], scalar=ffn_scale[:, 0:1],
                                                in1=res[:, tt], op0=ALU.mult, op1=ALU.add)

            add_and_norm(LN3, add_ffn)
            if front_too:
                split_maxima(c, front_steps)
                front_steps.end()
            for et in range(FT + 1):
                if et < FT:
                    dve.wait_ge(s["s_ready"], b * FT + et + 1)
                    steps.then(dve.tensor_reduce(ch_neg[:, et:et + 1], bank[:, et, :], AX.X, ALU.max, negate=True))
                    dve.tensor_scalar(ch_bias[:, et:et + 1], ch_neg[:, et:et + 1], S_SCALE, None,
                                      ALU.mult).then_inc(s["max_ready"], 1)
                if et >= 1:
                    e = et - 1
                    dve.wait_ge(s["e_ready"], b * FT + e + 1)
                    steps.then(dve.reciprocal(ch_inv[:, e:e + 1], ch_sum[:, e:e + 1]))
                    dve.tensor_scalar(p32[:, e], e32[:, e], ch_inv[:, e:e + 1], P_SCALE, ALU.mult,
                                      ALU.mult).then_inc(s["p_ready"], 1)

            def add_channels(tt):
                dve.wait_ge(s["ch_ready"], b * 2 + tt + 1)
                return dve.scalar_tensor_tensor(out=res[:, tt], in0=bank[:, 4 + tt, :], scalar=1.0 / P_SCALE,
                                                in1=res[:, tt], op0=ALU.mult, op1=ALU.add)

            add_and_norm(LN4, add_channels)
            low_part(T_ROUTER, 6)
            dve.wait_ge(s["logits_ready"], b + 1)
            dve.tensor_reduce(lg_neg[:], bank[:, 7, 0:TT * EXPERTS].rearrange("p (t e) -> p t e", t=TT), AX.X,
                              ALU.max, negate=True).then_inc(s["lmax_ready"], 1)
            dve.wait_ge(s["lexp_ready"], b * 2 + 2)
            steps.then(dve.reciprocal(lg_inv[:], lg_sum[:]))
            for tt in range(TT):
                ins = dve.tensor_scalar(lg_prob[:, tt], lg_exp[:, tt], lg_inv[:, tt:tt + 1], None, ALU.mult)
            steps.then(ins, alone=True)
            for tt in range(TT):
                ins = dve.max(top8[:, tt], lg_prob[:, tt])
            steps.then(ins, alone=True)
            for tt in range(TT):
                dve.max_index(idx8[:, tt], top8[:, tt], lg_prob[:, tt])
            steps.then(dve.tensor_reduce(top_sum[:], top8[:, :, 0:TOPK], AX.X, ALU.add))
            steps.then(dve.reciprocal(top_inv[:], top_sum[:]))
            dve.wait_ge(s["rows_lo"], b * 4 + 4)
            dve.tensor_copy(route_e[:, bass.ds(b * TT, TT), :], idx8[:, :, 0:TOPK])
            dve.tensor_tensor(route_w[:, bass.ds(b * TT, TT), :], top8[:, :, 0:TOPK],
                              top_inv[:].unsqueeze(2).to_broadcast([P, TT, TOPK]), ALU.mult)
            steps.end()

        dve.memset(nothing[:, 3:4], 0.0).then_inc(s["started"], 1)
        dve.memset(nothing[:, 1:2], 0.0).then_inc(s["x3_stored"], 16)
        dve.memset(nothing[:, 2:3], 0.0).then_inc(s["xn_stored"], 16)
        all_steps(dve, front, step)


def prepare(nc, scope, sb, sem, bank, ident, ident16, ones16, wq16, wk16, wv16, wo16, rw16, w1t, w3t, w2t,
            half_s1, ffn_scale, bq_col, bk_col, bv_row, bo_row, mask_q, mask_k, neg_half,
                q_stack, k_stack, v_ones, row_max,
            mq_d, mk_d, pad_d, wq_d, bq_d, wk_d, bk_d, wv_d, bv_d, wo_d, bo_d, w1_d, w3_d, w2_d, rw_d,
            padbias_dram, x_d, xin, x_loaded, ctxT_d, ctxT_raw, ctxT_loaded):

    def t(name, shape, dt):
        return sb(name, shape, dt, scope)

    split = [(wk_d, wk16, KVW), (wv_d, wv16, KVW), (wq_d, wq16, DM), (wo_d, wo16, DM), (rw_d, rw16, EXPERTS)]
    raw = [t(f"raw{i}", [P, FT, n], F32) for i, (_, _, n) in enumerate(split)]
    w1_raw = t("w1_raw", [P, FT, HIDDEN], F32)
    w3_raw = t("w3_raw", [P, FT, HIDDEN], F32)
    w2_raw = t("w2_raw", [P, HT, DM], F32)
    below = t("below", [P, HT * DM], F16)
    magnitudes = t("magnitudes", [P, HT * DM // FT], F16)
    mq_raw = t("mq_raw", [P, TT, SEQ // 4], I32)
    mk_raw = t("mk_raw", [P, TT, SEQ // 4], I32)
    pad_raw = t("pad_raw", [BATCH, SEQ // 4], I32)
    pad16 = t("pad16", [BATCH, SEQ], F16)
    ones32 = t("ones32", [P, P], F32)
    part_sums = t("part_sums", [P, 3, FT], F32)
    sums = t("sums", [P, 3], F32)
    scales = t("scales", [P, 3], F32)
    thresholds = t("thresholds", [P, 3, 2], F32)
    s12 = t("s12", [P, 1], F32)
    ws_loaded, small_loaded = sem("ws_loaded"), sem("small_loaded")
    ternary_loaded = [sem(f"ternary_loaded{i}") for i in range(3)]
    w_hi, pool_made, w2_zeroed = sem("w_hi"), sem("pool_made"), sem("w2_zeroed")
    magnitudes_made, ones_made = sem("magnitudes_made"), sem("ones_made")
    totals_made, pre_step, pad_stored = sem("totals_made"), sem("pre_step"), sem("pad_stored")
    pad_made = sem("pad_made")
    TAIL = HIDDEN - (HT - 1) * P
    with nc.Block() as block:
        @block.sync
        def _(sp):
            sp.dma_start(w1_raw[:], w1_d).then_inc(ternary_loaded[0], 16)
            sp.dma_start(w3_raw[:], w3_d).then_inc(ternary_loaded[1], 16)
            sp.wait_ge(w2_zeroed, 1)
            sp.dma_start(w2_raw[:, 0:HT - 1, :],
                         w2_d[0:(HT - 1) * P].rearrange("(t p) d -> p t d", p=P)).then_inc(ternary_loaded[2], 16)
            sp.dma_start(w2_raw[0:TAIL, HT - 1, :], w2_d[(HT - 1) * P:HIDDEN]).then_inc(ternary_loaded[2], 16)
            for i, (src, _, _) in enumerate(split):
                sp.dma_start(raw[i][:], src).then_inc(ws_loaded, 16)
            sp.dma_start(ctxT_raw[:], ctxT_d[0].rearrange("(t p) k -> p t k", p=P)).then_inc(ctxT_loaded, 16)
            sp.dma_start(xin[:], x_d[0].rearrange("(t p) d -> p t d", p=P)).then_inc(x_loaded, 16)
            sp.wait_ge(pad_made, 1)
            sp.dma_start(padbias_dram, pad16[:]).then_inc(pad_stored, 16)
            sp.wait_ge(pad_stored, 16)

        @block.scalar
        def _(act):
            for i, w in enumerate((w1_raw, w3_raw, w2_raw)):
                act.wait_ge(ternary_loaded[i], 32 if i == 2 else 16)
                flat = w[:].rearrange("p t n -> p (t n)")
                n = flat.shape[1] // FT
                for part in range(FT):
                    if i or part:
                        act.wait_ge(magnitudes_made, i * FT + part)
                    act.activation(magnitudes[:, 0:n], flat[:, part * n:(part + 1) * n], ACT.Abs,
                                   accum_out=part_sums[:, i, part:part + 1]).then_inc(magnitudes_made, 1)
            act.wait_ge(ws_loaded, 16 * len(split))
            for i, (_, dst, _) in enumerate(split):
                act.copy(dst[:, HI], raw[i][:]).then_inc(w_hi, 1)

        @block.gpsimd
        def _(pool):
            pool.memset(ident[:], 0.0)
            pool.memset(ident16[:], 0.0)
            pool.memset(neg_half[:], -0.5).then_inc(pool_made, 1)
            pool.dma_start(mq_raw[:], mq_d).then_inc(small_loaded, 16)
            pool.dma_start(mk_raw[:], mk_d).then_inc(small_loaded, 16)
            pool.dma_start(pad_raw[:], pad_d).then_inc(small_loaded, 16)
            pool.dma_start(bq_col[:], bq_d).then_inc(small_loaded, 16)
            pool.dma_start(bk_col[:], bk_d).then_inc(small_loaded, 16)
            pool.dma_start(bv_row[:], bv_d.to_broadcast([P, KVW])).then_inc(small_loaded, 16)
            pool.dma_start(bo_row[:], bo_d.to_broadcast([P, DM])).then_inc(small_loaded, 16)
            pool.wait_ge(pool_made, 1)
            for m in (ident, ident16):
                pool.affine_select(out=m[:], in_=m[:], compare_op=ALU.not_equal, fill=1.0, base=0,
                                   pattern=[[-1, P]], channel_multiplier=1).then_inc(pool_made, 1)
            for i, (_, dst, _) in enumerate(split):
                pool.wait_ge(w_hi, i + 1)
                pool.tensor_tensor(dst[:, LO], raw[i][:], dst[:, HI], ALU.subtract)

        @block.tensor
        def _(pe):
            pe.wait_ge(ones_made, 1)
            for i in range(3):
                pe.wait_ge(magnitudes_made, (i + 1) * FT)
                pe.matmul(bank[:, i, 0:FT], ones32[:], part_sums[:, i, :], start=True,
                          stop=True).then_inc(totals_made, 1)

        @block.vector
        def _(dve):
            count = [0]

            def step(ins):
                count[0] += 1
                ins.then_inc(pre_step, 1)
                dve.wait_ge(pre_step, count[0])

            step(dve.memset(w2_raw[64:P, HT - 1, :], 0.0))
            dve.memset(w2_raw[0:64, HT - 1, :], 0.0).then_inc(w2_zeroed, 1)
            dve.memset(w1t[:, :, HIDDEN:HPAD], 0.0)
            dve.memset(w3t[:, :, HIDDEN:HPAD], 0.0)
            dve.memset(ones16[:], 1.0)
            dve.memset(ones32[:], 1.0).then_inc(ones_made, 1)
            dve.memset(q_stack[ROW_PAD:ROWS_B], 1.0)
            dve.memset(k_stack[ROW_PAD:ROWS_B], 1.0)
            dve.memset(v_ones[:], 1.0)
            dve.memset(row_max[:], 0.0)
            flat = [w1_raw[:].rearrange("p t n -> p (t n)"), w3_raw[:].rearrange("p t n -> p (t n)"),
                    w2_raw[:].rearrange("p t n -> p (t n)")]
            for i, (w, dst) in enumerate(((flat[0], w1t[:, :, 0:HIDDEN]), (flat[1], w3t[:, :, 0:HIDDEN]),
                                          (flat[2], w2t[:]))):
                dve.wait_ge(totals_made, i + 1)
                step(dve.tensor_reduce(sums[:, i:i + 1], bank[:, i, 0:FT], AX.X, ALU.add))
                step(dve.tensor_scalar(scales[:, i:i + 1], sums[:, i:i + 1], 1.0 / (HIDDEN * DM), None, ALU.mult))
                dve.tensor_scalar(thresholds[:, i, 0:1], scales[:, i:i + 1], 0.5, None, ALU.mult)
                step(dve.tensor_scalar(thresholds[:, i, 1:2], scales[:, i:i + 1], -0.5, None, ALU.mult))
                n = w.shape[1]
                step(dve.tensor_scalar(below[:, 0:n], w, thresholds[:, i, 1:2], None, ALU.is_lt))
                shaped = [a.rearrange("p (t n) -> p t n", n=dst.shape[2]) for a in (w, below[:, 0:n])]
                step(dve.scalar_tensor_tensor(out=dst, in0=shaped[0], scalar=thresholds[:, i, 0:1], in1=shaped[1],
                                              op0=ALU.is_gt, op1=ALU.subtract))
            dve.tensor_scalar(half_s1[:], scales[:, 0:1], 0.5, None, ALU.mult)
            step(dve.tensor_tensor(s12[:], scales[:, 0:1], scales[:, 1:2], ALU.mult))
            step(dve.scalar_tensor_tensor(out=ffn_scale[:], in0=s12[:], scalar=0.5 / G_SCALE, in1=scales[:, 2:3],
                                          op0=ALU.mult, op1=ALU.mult))
            dve.wait_ge(small_loaded, 7 * 16)
            dve.tensor_scalar(mask_q[:], mq_raw[:].bitcast(U8), MASKED, None, ALU.mult)
            dve.tensor_scalar(mask_k[:], mk_raw[:].bitcast(U8), MASKED, None, ALU.mult)
            dve.tensor_scalar(pad16[:], pad_raw[:].bitcast(U8), MASKED, None, ALU.mult).then_inc(pad_made, 1)


def expert_layer(nc, scope, sb, sem, bank, ident16, ones16, route_w, route_e, gu_d, da_d, db_d, x3_dram,
                 xn_dram, y_dram, eid_dram, out_d):

    def t(name, shape, dt):
        return sb(name, shape, dt, scope)

    GU = 2 * INTER
    expert_i = t("expert_i", [P, EXPERTS], I32)
    expert_f = t("expert_f", [P, EXPERTS], F32)
    block_i = t("block_i", [P, 1], I32)
    block_f = t("block_f", [P, 1], F32)
    before = t("before", [P, P], F16)
    starts_ends = t("starts_ends", [EXPERTS, 2 * EXPERTS], F16)
    chosen = t("chosen", [P, TILES * TOPK, EXPERTS], F32)
    member = t("member", [P, TILES, EXPERTS], F16)
    slot_of = t("slot_of", [P, TILES, EXPERTS], F32)
    picked = t("picked", [P, TILES * TOPK, EXPERTS], F32)
    slot_f = t("slot_f", [P, TILES * TOPK], F32)
    slot_u = t("slot_u", [P, TILES * TOPK], U32)
    count_i = t("count_i", [EXPERTS, 1], I32)
    blocks_i = t("blocks_i", [EXPERTS, 1], I32)
    blocks_f = t("blocks_f", [EXPERTS, 1], F32)
    blocks_row = t("blocks_row", [EXPERTS, P], F16)
    base = t("base", [P, 2 * EXPERTS], F32)
    ended = t("ended", [P, EXPERTS], F32)
    eid_f = t("eid_f", [P, 1], F32)
    eid_i = t("eid_i", [P, 1], I32)
    eids = t("eids", [1, P], I32)
    token_i = t("token_i", [P, TILES], I32)
    token_f = t("token_f", [P, TILES], F32)
    place_i = t("place_i", [P, P], I32)
    place16 = t("place16", [P, P], F16)
    slot_i = t("slot_i", [P, TILES * TOPK], I32)
    col_i = t("col_i", [P, TILES * TOPK], I32)
    col_f = t("col_f", [P, TILES * TOPK], F32)
    row_f = t("row_f", [P, TILES * TOPK], F32)
    POOL_ROWS = 2
    row_hot = t("row_hot", [P, TILES * TOPK, P], F16)
    token_hot = t("token_hot", [P, TILES * TOPK, P], F16)
    table = t("table", [P, P], U32)
    pool_nothing = t("pool_nothing", [1, 1], F32)
    index = t("index", [P, 2, TT], U32)
    xg = t("xg", [P, 2, TT, 2 * DM], F16)
    xgT = t("xgT", [P, 2, 2, FT, BS], F16)
    gu_raw = t("gu_raw", [P, 2, FT, GU], F32)
    dn_raw = t("dn_raw", [P, 2, 2, DM], F32)
    gu16 = t("gu16", [P, 2, 2, FT, GU], F16)
    dn16 = t("dn16", [P, 2, 2, 2, DM], F16)
    silu_g = t("silu_g", [P, 2, 2 * BS], F32)
    h32 = t("h32", [P, 2, 2 * BS], F32)
    h16 = t("h16", [P, 2, 2, 2 * BS], F16)
    y32 = t("y32", [P, 2, TT, DM], F32)
    NY = 16
    yg = t("yg", [P, NY, DM], F32)
    acc = t("acc", [P, TILES, DM], F32)

    names = ("iotas member_ready counted blocks_ready based slots_ready eid_ready eid_out eid_in "
             "table_ready index_set rows_ready pool_hot_made hot_made hot_used x3_loaded route_step gu_hi dn_hi gu_lo dn_lo x_turned xT_hi xT_lo gate_ready "
             "silu_done h_ready h_hi h_lo y_ready y_act y_dve added out_stored "
             "padded tri_ready ").split()
    s = {n: sem("e_" + n) for n in names}
    gu_loaded, dn_loaded, xg_loaded, y_stored = (
        [sem(f"e_{n}{u}") for u in range(2)] for n in ("gu_loaded", "dn_loaded", "xg_loaded", "y_stored"))
    y_gathered = [sem(f"e_y_gathered{i}") for i in range(NY)]
    block = scope.enter_context(nc.Block())

    @block.sync
    def _(sp):
        sp.wait_ge(s["eid_ready"], 1)
        sp.dma_start(eid_dram.rearrange("(p o) -> p o", o=1), eid_i[:]).then_inc(s["eid_out"], 16)
        sp.wait_ge(s["eid_out"], 16)
        sp.dma_start(eids[:], eid_dram.rearrange("(o p) -> o p", o=1)).then_inc(s["eid_in"], 16)
        sp.wait_ge(s["eid_in"], 16)
        sp.wait_ge(s["padded"], 1)

        def gate_up_weights(n, u):
            e = sp.value_load(eids[0:1, bass.ds(n, 1)], min_val=0, max_val=EXPERTS - 1)
            if not early(n):
                sp.wait_ge(s["gu_lo"], n - 1)
            sp.dma_start(gu_raw[:, u], gu_d[bass.ds(e, 1)].rearrange("o p t n -> (o p) t n")).then_inc(gu_loaded[u], 16)

        def down_weights(n, u):
            e = sp.value_load(eids[0:1, bass.ds(n, 1)], min_val=0, max_val=EXPERTS - 1)
            if not early(n):
                sp.wait_ge(s["dn_lo"], n - 1)
            sp.dma_start(dn_raw[:, u, 0], da_d[bass.ds(e, 1)].rearrange("o p n -> (o p) n")).then_inc(dn_loaded[u], 16)
            sp.dma_start(dn_raw[64:P, u, 1], db_d[bass.ds(e, 1)].rearrange("o p n -> (o p) n")).then_inc(dn_loaded[u], 16)

        for u in range(2):
            gate_up_weights(u, u)
            down_weights(u, u)
        sp.dma_start(acc[:], x3_dram.rearrange("(t p) c -> p t c", p=P)).then_inc(s["x3_loaded"], 16)
        with sp.Fori(1, NBLK // 2) as i:
            for u in range(2):
                gate_up_weights(2 * i + u, u)
                down_weights(2 * i + u, u)
        gate_up_weights(NBLK - 1, 0)
        down_weights(NBLK - 1, 0)
        for tile in range(TILES):
            sp.wait_ge(s["added"], TOPK * (tile + 1))
            sp.dma_start(out_d[tile * P:(tile + 1) * P], acc[:, tile]).then_inc(s["out_stored"], 16)
        sp.wait_ge(s["out_stored"], 16 * TILES)

    @block.gpsimd
    def _(pool):
        pool.memset(before[:], 1.0)
        pool.memset(starts_ends[:], 1.0).then_inc(s["iotas"], 1)
        pool.iota(expert_i[:], pattern=[[1, EXPERTS]], base=0, channel_multiplier=0).then_inc(s["iotas"], 1)
        pool.iota(block_i[:], pattern=[[0, 1]], base=0, channel_multiplier=1).then_inc(s["iotas"], 1)
        pool.iota(place_i[:], pattern=[[1, P]], base=0, channel_multiplier=0).then_inc(s["iotas"], 1)
        pool.iota(token_i[:], pattern=[[P, TILES]], base=0, channel_multiplier=1).then_inc(s["iotas"], 1)
        pool.wait_ge(s["iotas"], 1)
        pool.affine_select(out=before[:], in_=before[:], compare_op=ALU.is_gt, fill=0.0, base=0,
                           pattern=[[1, P]], channel_multiplier=-1).then_inc(s["tri_ready"], 1)
        pool.affine_select(out=starts_ends[:, 0:EXPERTS], in_=starts_ends[:, 0:EXPERTS], compare_op=ALU.is_gt,
                           fill=0.0, base=0, pattern=[[1, EXPERTS]], channel_multiplier=-1).then_inc(s["tri_ready"], 1)
        pool.affine_select(out=starts_ends[:, EXPERTS:], in_=starts_ends[:, EXPERTS:], compare_op=ALU.is_ge,
                           fill=0.0, base=0, pattern=[[1, EXPERTS]], channel_multiplier=-1).then_inc(s["tri_ready"], 1)
        def gather(n, u):
            pool.tensor_copy(index[:, u], table[:, bass.ds(TT * n, TT)]).then_inc(s["index_set"], 1)
            pool.wait_ge(s["index_set"], n + 1)
            pool.tensor_tensor(pool_nothing[:], ones16[0:1, 0:1], ones16[0:1, 0:1], ALU.add)
            for tt in range(TT):
                pool.indirect_dma_start(out=xg[:, u, tt, :], out_offset=None, in_=xn_dram,
                                        in_offset=bass.IndirectOffsetOnAxis(ap=index[:, u, tt:tt + 1], axis=0)
                                        ).then_inc(xg_loaded[u], 16)

        def split_down(n, u):
            pool.wait_ge(s["dn_hi"], n + 1)
            pool.tensor_tensor(dn16[:, u, LO], dn_raw[:, u], dn16[:, u, HI], ALU.subtract).then_inc(s["dn_lo"], 1)

        def gather_split(n, u):
            if not (isinstance(n, int) and n == NBLK - 1):
                pool.wait_ge(s["x_turned"], 2 * n + 2)
                gather(n + 2, u)
            split_down(n, u)
            pool.wait_ge(s["h_hi"], n + 1)
            pool.tensor_tensor(h16[:, u, LO], h32[:, u], h16[:, u, HI], ALU.subtract).then_inc(s["h_lo"], 1)

        pool.wait_ge(s["rows_ready"], 1)
        for c in range(0, TILES * TOPK, POOL_ROWS):
            pool.tensor_scalar(row_hot[:, c], place16[:], row_f[:, c:c + 1], None,
                               ALU.is_equal).then_inc(s["pool_hot_made"], 1)
        pool.wait_ge(s["table_ready"], 1)
        gather(0, 0)
        gather(1, 1)
        pipeline(pool, lambda n, u: None, gather_split, lambda n, u: None)
        pool.wait_ge(xg_loaded[1], 32 * (NBLK // 2 + 1))
        pool.wait_ge(s["slots_ready"], 1)
        pool.wait_ge(y_stored[0], 16 * (NBLK // 2 + 2))
        pool.wait_ge(y_stored[1], 16 * (NBLK // 2 + 1))
        for c in range(TILES * TOPK):
            if c >= NY:
                pool.wait_ge(s["added"], c - NY + 1)
            pool.indirect_dma_start(out=yg[:, c % NY], out_offset=None, in_=y_dram,
                                    in_offset=bass.IndirectOffsetOnAxis(ap=slot_u[:, c:c + 1], axis=0)
                                    ).then_inc(y_gathered[c % NY], 16)

    @block.scalar
    def _(act):
        def split(n, u):
            act.wait_ge(gu_loaded[u], n * 8 + 16 - 8 * u)
            if not early(n):
                act.wait_ge(s["gate_ready"], n - 1)
            act.copy(gu16[:, u, HI], gu_raw[:, u]).then_inc(s["gu_hi"], 1)
            act.wait_ge(s["x_turned"], n * 2 + 1)
            act.copy(xgT[:, u, HI].rearrange("p t n -> p (t n)"), bank[:, 0, :].bitcast(F16)).then_inc(s["xT_hi"], 1)

        def gate(n, u):
            act.wait_ge(s["gate_ready"], n + 1)
            act.activation(silu_g[:, u, 0:BS], bank[:, 2 + 2 * u, 0:BS], ACT.Silu)
            act.activation(silu_g[64:P, u, BS:2 * BS], bank[0:64, 3 + 2 * u, 0:BS], ACT.Silu).then_inc(s["silu_done"], 1)
            act.wait_ge(s["h_ready"], n + 1)
            act.copy(h16[:, u, HI], h32[:, u]).then_inc(s["h_hi"], 1)

        def store(n, u):
            act.wait_ge(y_stored[u], n * 8 + 16 - 8 * u)
            act.wait_ge(s["y_ready"], n * 2 + 1)
            act.copy(y32[:, u, 0], bank[:, 6, :]).then_inc(s["y_act"], 1)
            act.wait_ge(s["y_act"], n + 1)
            act.wait_ge(s["y_dve"], n + 1)
            dst = pick(y_dram.rearrange("(n t p) c -> n p t c", n=NBLK, p=P), n)
            act.dma_start(dst, y32[:, u]).then_inc(y_stored[u], 16)

        pipeline(act, split, gate, store)

    @block.tensor
    def _(pe):
        pe.wait_ge(s["member_ready"], 1)
        for tile in range(TILES):
            last = pe.matmul(bank[0:EXPERTS, 1, 0:1], member[:, tile, :], ones16[:, 0:1], start=(tile == 0),
                             stop=(tile == TILES - 1))
        last.then_inc(s["counted"], 1)
        pe.wait_ge(s["tri_ready"], 3)
        pe.matmul(bank[:, 0, :], before[:], member[:].rearrange("p t e -> p (t e)"), start=True, stop=True)
        for d in range(1, TILES):
            pe.matmul(bank[:, 0, d * EXPERTS:], ones16[:],
                      member[:, 0:TILES - d, :].rearrange("p t e -> p (t e)"), start=False, stop=True,
                      skip_group_check=True)
        pe.wait_ge(s["blocks_ready"], 1)
        pe.matmul(bank[:, 2, 0:2 * EXPERTS], blocks_row[:], starts_ends[:], start=True,
                  stop=True).then_inc(s["based"], 1)

        def turn(n, u):
            pe.wait_ge(xg_loaded[u], n * 16 + 32 - 16 * u)
            if not (isinstance(n, int) and n < 1):
                pe.wait_ge(s["xT_hi"], n)
                pe.wait_ge(s["xT_lo"], n)
            for part in (HI, LO):
                for ft in range(FT):
                    for tt in range(TT):
                        last = pe.transpose(bank[:, part, :].bitcast(F16)[:, ft * BS + tt * P:ft * BS + (tt + 1) * P],
                                            xg[:, u, tt, part * DM + ft * P:part * DM + (ft + 1) * P], ident16[:])
                last.then_inc(s["x_turned"], 1)

        def gate_up(n, u):
            pe.wait_ge(s["gu_lo"], n + 1)
            pe.wait_ge(s["xT_hi"], n + 1)
            pe.wait_ge(s["xT_lo"], n + 1)
            if not early(n):
                pe.wait_ge(s["h_ready"], n - 1)
            for m, out in enumerate((bank[:, 2 + 2 * u, 0:BS], bank[:, 2 + 2 * u, BS:2 * BS], bank[:, 3 + 2 * u, 0:BS])):
                for ft in range(FT):
                    for j, (lp, rp) in enumerate(PASSES):
                        last = pe.matmul(out, gu16[:, u, lp, ft, m * P:(m + 1) * P], xgT[:, u, rp, ft, :],
                                         start=(ft == 0 and j == 0), stop=(ft == FT - 1 and j == 2))
            last.then_inc(s["gate_ready"], 1)

        def down(n, u):
            pe.wait_ge(s["dn_lo"], n + 1)
            pe.wait_ge(s["h_lo"], n + 1)
            if not (isinstance(n, int) and n < 1):
                pe.wait_ge(s["y_act"], n)
                pe.wait_ge(s["y_dve"], n)
            for tt in range(TT):
                for kt in range(2):
                    for j, (lp, rp) in enumerate(PASSES):
                        last = pe.matmul(bank[:, 6 + tt, :], h16[:, u, lp, kt * BS + tt * P:kt * BS + (tt + 1) * P],
                                         dn16[:, u, rp, kt, :], start=(kt == 0 and j == 0), stop=(kt == 1 and j == 2))
                last.then_inc(s["y_ready"], 1)

        for c in range(TILES * TOPK):
            pe.wait_ge(s["hot_made"], c + 1)
            pe.wait_ge(s["pool_hot_made"], c // POOL_ROWS + 1)
            pe.matmul(bank[:, 3, 0:P], row_hot[:, c, :], token_hot[:, c, :], start=(c == 0),
                      stop=(c == TILES * TOPK - 1)).then_inc(s["hot_used"], 1)
        pipeline(pe, turn, gate_up, down)

    @block.vector
    def _(dve):
        count = [0]

        def step(ins):
            count[0] += 1
            ins.then_inc(s["route_step"], 1)
            dve.wait_ge(s["route_step"], count[0])

        dve.memset(dn_raw[0:64, :, 1], 0.0).then_inc(s["padded"], 1)
        for u in range(2):
            dve.memset(h32[0:64, u, BS:2 * BS], 0.0).then_inc(y_stored[u], 16)
        dve.wait_ge(s["iotas"], 5)
        dve.tensor_copy(block_f[:], block_i[:])
        dve.tensor_copy(place16[:], place_i[:])
        dve.tensor_copy(token_f[:], token_i[:])
        step(dve.tensor_copy(expert_f[:], expert_i[:]))
        shape = [P, TILES * TOPK, EXPERTS]
        step(dve.tensor_tensor(chosen[:], route_e[:].rearrange("p t k -> p (t k)").unsqueeze(2).to_broadcast(shape),
                               expert_f[:].unsqueeze(1).to_broadcast(shape), ALU.is_equal))
        dve.tensor_reduce(member[:], chosen[:].rearrange("p (t k) e -> p t e k", k=TOPK), AX.X,
                          ALU.max).then_inc(s["member_ready"], 1)
        dve.wait_ge(s["counted"], 1)
        step(dve.tensor_scalar(count_i[:], bank[0:EXPERTS, 1, 0:1], float(BS - 1), None, ALU.add))
        step(dve.tensor_scalar(blocks_i[:], count_i[:], BS.bit_length() - 1, None, ALU.logical_shift_right))
        step(dve.tensor_copy(blocks_f[:], blocks_i[:]))
        dve.tensor_scalar(blocks_row[:], ones16[0:EXPERTS, :], blocks_f[:, 0:1], None,
                          ALU.mult).then_inc(s["blocks_ready"], 1)
        dve.wait_ge(s["based"], 1)
        dve.tensor_scalar(base[:, 0:EXPERTS], bank[:, 2, 0:EXPERTS], float(BS), None, ALU.mult)
        step(dve.tensor_scalar(ended[:], bank[:, 2, EXPERTS:2 * EXPERTS], block_f[:, 0:1], None, ALU.is_le))
        step(dve.tensor_reduce(eid_f[:], ended[:], AX.X, ALU.add))
        dve.tensor_scalar(eid_i[:], eid_f[:], float(EXPERTS - 1), None, ALU.min).then_inc(s["eid_ready"], 1)
        step(dve.tensor_tensor(slot_of[:], bank[:, 0, :].rearrange("p (t e) -> p t e", e=EXPERTS),
                               base[:, 0:EXPERTS].unsqueeze(1).to_broadcast([P, TILES, EXPERTS]), ALU.add))
        for k in range(TOPK):
            ins = dve.tensor_tensor(picked[:].rearrange("p (t k) e -> p t k e", k=TOPK)[:, :, k],
                                    chosen[:].rearrange("p (t k) e -> p t k e", k=TOPK)[:, :, k],
                                    slot_of[:], ALU.mult)
        step(ins)
        step(dve.tensor_reduce(slot_f[:], picked[:], AX.X, ALU.add))
        dve.tensor_copy(slot_u[:], slot_f[:]).then_inc(s["slots_ready"], 1)
        step(dve.tensor_copy(slot_i[:], slot_f[:]))
        step(dve.tensor_scalar(col_i[:], slot_i[:], P.bit_length() - 1, None, ALU.logical_shift_right))
        step(dve.tensor_copy(col_f[:], col_i[:]))
        dve.scalar_tensor_tensor(out=row_f[:], in0=col_f[:], scalar=-float(P), in1=slot_f[:], op0=ALU.mult,
                                 op1=ALU.add).then_inc(s["rows_ready"], 1)
        dve.wait_ge(s["rows_ready"], 1)
        for c in range(TILES * TOPK):
            if c % POOL_ROWS:
                dve.tensor_scalar(row_hot[:, c], place16[:], row_f[:, c:c + 1], None, ALU.is_equal)
            tile = c // TOPK
            dve.tensor_scalar(token_hot[:, c], place16[:], col_f[:, c:c + 1], token_f[:, tile:tile + 1],
                              ALU.is_equal, ALU.mult).then_inc(s["hot_made"], 1)
        dve.wait_ge(s["hot_used"], TILES * TOPK)
        dve.tensor_copy(table[:], bank[:, 3, 0:P]).then_inc(s["table_ready"], 1)

        def split_down(u):
            dve.tensor_copy(dn16[:, u, HI], dn_raw[:, u]).then_inc(s["dn_hi"], 1)

        def split(n, u):
            dve.wait_ge(s["gu_hi"], n + 1)
            dve.tensor_tensor(gu16[:, u, LO], gu_raw[:, u], gu16[:, u, HI], ALU.subtract).then_inc(s["gu_lo"], 1)
            dve.wait_ge(s["x_turned"], n * 2 + 2)
            dve.tensor_copy(xgT[:, u, LO].rearrange("p t n -> p (t n)"), bank[:, 1, :].bitcast(F16)).then_inc(s["xT_lo"], 1)

        def gate(n, u):
            dve.wait_ge(s["silu_done"], n + 1)
            dve.tensor_tensor(h32[:, u, 0:BS], silu_g[:, u, 0:BS], bank[:, 2 + 2 * u, BS:2 * BS], ALU.mult)
            dve.tensor_tensor(h32[64:P, u, BS:2 * BS], silu_g[64:P, u, BS:2 * BS], bank[64:P, 3 + 2 * u, 0:BS],
                              ALU.mult).then_inc(s["h_ready"], 1)

        def leave(n, u):
            dve.wait_ge(y_stored[u], n * 8 + 16 - 8 * u)
            dve.wait_ge(s["y_ready"], n * 2 + 2)
            dve.tensor_copy(y32[:, u, 1], bank[:, 7, :]).then_inc(s["y_dve"], 1)
            if not (isinstance(n, int) and n >= NBLK - 2):
                dve.wait_ge(dn_loaded[u], n * 16 + 64 - 16 * u)
                split_down(u)

        for u in range(2):
            dve.wait_ge(dn_loaded[u], 32)
            split_down(u)
        pipeline(dve, split, gate, leave)
        for c in range(TILES * TOPK):
            tile, k = c // TOPK, c % TOPK
            if c == 0:
                dve.wait_ge(s["x3_loaded"], 16)
            else:
                dve.wait_ge(s["added"], c)
            dve.wait_ge(y_gathered[c % NY], 16 * (c // NY + 1))
            dve.scalar_tensor_tensor(out=acc[:, tile], in0=yg[:, c % NY], scalar=route_w[:, tile, k:k + 1],
                                     in1=acc[:, tile], op0=ALU.mult, op1=ALU.add).then_inc(s["added"], 1)



def kernel(x, ctx_2048, mask_SxS2_bc0, mask_BxS2_bk0, L0_xattn_Wq, L0_xattn_bq, L0_xattn_Wk, L0_xattn_bk,
           L0_xattn_Wv, L0_xattn_bv, L0_xattn_Wo, L0_xattn_bo, L0_ffn_w1, L0_ffn_w3, L0_ffn_w2,
           L1_ffn_router_w, L1_ffn_gate_w, L1_ffn_up_w, L1_ffn_down_w):
    import concourse.bacc as bacc
    from concourse.bass_utils import run_bass_kernel_spmd

    def tiled(w):
        w = np.asarray(w).T
        return w.reshape(-1, P, w.shape[1]).transpose(1, 0, 2)

    def words(m):
        return np.ascontiguousarray(m).view(np.int32)

    mask = np.asarray(mask_SxS2_bc0)
    gate = np.asarray(L1_ffn_gate_w).transpose(0, 2, 1)
    up = np.asarray(L1_ffn_up_w).transpose(0, 2, 1)
    gu = np.concatenate([gate[:, :, :P], up[:, :, :P], gate[:, :, P:], up[:, :, P:]], axis=2)
    down = np.asarray(L1_ffn_down_w).transpose(0, 2, 1)
    arrays = {
        "x": np.asarray(x),
        "ctx": np.asarray(ctx_2048),
        "ctxT": np.asarray(ctx_2048).transpose(0, 2, 1),
        "mq": words(mask.reshape(TT, P, SEQ).transpose(1, 0, 2)),
        "mk": words(mask.T.reshape(TT, P, SEQ).transpose(1, 0, 2)),
        "pad": words(np.asarray(mask_BxS2_bk0)),
        "wq": tiled(L0_xattn_Wq),
        "bq": np.asarray(L0_xattn_bq).reshape(FT, P).T,
        "wk": tiled(L0_xattn_Wk),
        "bk": np.asarray(L0_xattn_bk).reshape(KVW, 1),
        "wv": tiled(L0_xattn_Wv),
        "bv": np.asarray(L0_xattn_bv).reshape(1, KVW),
        "wo": tiled(L0_xattn_Wo),
        "bo": np.asarray(L0_xattn_bo).reshape(1, DM),
        "w1": tiled(L0_ffn_w1),
        "w3": tiled(L0_ffn_w3),
        "w2": np.asarray(L0_ffn_w2).T,
        "rw": tiled(L1_ffn_router_w),
        "gu": gu.reshape(EXPERTS, FT, P, 2 * INTER).transpose(0, 2, 1, 3),
        "da": down[:, :P],
        "db": down[:, P:],
    }
    nc = bacc.Bacc("TRN2", target_bir_lowering=False, num_devices=1)
    given, args = {}, {}
    for name, a in arrays.items():
        given[name] = np.ascontiguousarray(a)
        args[name + "_d"] = nc.dram_tensor(name, given[name].shape, mybir.dt.from_np(given[name].dtype),
                                           kind="ExternalInput").ap()
    out = nc.dram_tensor("out", (TOKENS, DM), F32, kind="ExternalOutput").ap()
    build(nc, out_d=out, **args)
    r = run_bass_kernel_spmd(nc, [given], core_ids=[0])
    return np.asarray(r.results[0]["out"]).reshape(BATCH, SEQ, DM)
```
